# Optimizing a Trainium2 kernel written in Bass

```python
import numpy as np
import jax
import jax.numpy as jnp

def _softmax(x, axis=-1):
    return jax.nn.softmax(x, axis=axis)

def _gelu(x):
    return jax.nn.gelu(x, approximate=True)

def _silu(x):
    return jax.nn.silu(x)

def _sigmoid(x):
    return jax.nn.sigmoid(x)

def _layernorm(x, axis=-1, eps=1e-05):
    m = jnp.mean(x, axis=axis, keepdims=True)
    v = jnp.var(x, axis=axis, keepdims=True)
    return (x - m) / jnp.sqrt(v + eps)

def _scatter_add(tgt, idx, src, axis=0):
    return tgt.at[idx].add(src)

def _segment_sum(src, seg, n):
    return jax.ops.segment_sum(src, seg, n)
kernel_name = 'mk_conv_preact_d4_conv_nhwc128_r2_9e0c8b'

def setup_inputs(seed: int=0):
    np.random.seed(seed)
    _w = jnp.asarray

    def _rec_inputs():
        import jax
        import jax.numpy as jnp
        _gk = jax.random.key(seed)
        x = 7.22e-05 + 1 * jax.random.normal(jax.random.fold_in(_gk, 1), (1, 128, 128, 64), jnp.float32)
        return x
    x = _rec_inputs()

    def _L0_conv_setup():
        import jax, jax.numpy as jnp
        import numpy as np
        D_PAIR = 64
        N_HEAD = 4
        D_HID = 32
        SCALING = 1.0 / np.sqrt(D_HID)

        def _layernorm(x, gamma, beta, eps=1e-05):
            mu = jnp.mean(x, axis=-1, keepdims=True)
            var = jnp.var(x, axis=-1, keepdims=True)
            return (x - mu) * jax.lax.rsqrt(var + eps) * gamma + beta
        key = jax.random.key(seed)
        ks = jax.random.split(key, 12)
        B, L = (1, 128)
        s = 0.02
        return {'pair': jax.random.normal(ks[0], (B, L, L, D_PAIR), dtype=jnp.float32), 'gamma': jnp.ones((D_PAIR,), jnp.float32), 'beta': jnp.zeros((D_PAIR,), jnp.float32), 'Wq': jax.random.normal(ks[1], (D_PAIR, N_HEAD * D_HID), jnp.float32) * s, 'Wk': jax.random.normal(ks[2], (D_PAIR, N_HEAD * D_HID), jnp.float32) * s, 'Wv': jax.random.normal(ks[3], (D_PAIR, N_HEAD * D_HID), jnp.float32) * s, 'Wb': jax.random.normal(ks[4], (D_PAIR, N_HEAD), jnp.float32) * s, 'Wg': jax.random.normal(ks[5], (D_PAIR, N_HEAD * D_HID), jnp.float32) * s, 'bg': jnp.ones((N_HEAD * D_HID,), jnp.float32), 'Wo': jax.random.normal(ks[6], (N_HEAD * D_HID, D_PAIR), jnp.float32) * s, 'bo': jnp.zeros((D_PAIR,), jnp.float32)}
    _L0_conv_all = _L0_conv_setup()
    _L0_conv_in = {k: v for k, v in _L0_conv_all.items() if k in ('gamma', 'beta', 'Wq', 'Wk', 'Wv', 'Wb', 'Wg', 'bg', 'Wo', 'bo')}
    del _L0_conv_all

    def _L1_conv_setup():
        import jax, jax.numpy as jnp
        import numpy as np
        DIM = 64
        QK = 64
        HEADS = 8
        NWIN = 8
        KVWIN = 4
        TOPK = 4
        SCALE = QK ** (-0.5)
        key = jax.random.key(seed)
        ks = jax.random.split(key, 7)
        N, H, W = (4, 128, 128)
        x = jax.random.normal(ks[0], (N, H, W, DIM), jnp.float32)
        qkv_w = jax.random.normal(ks[1], (2 * QK + DIM, DIM), jnp.float32) * 0.02
        qkv_b = jnp.zeros((2 * QK + DIM,), jnp.float32)
        wo_w = jax.random.normal(ks[2], (DIM, DIM), jnp.float32) * 0.02
        wo_b = jnp.zeros((DIM,), jnp.float32)
        dw_w = jax.random.normal(ks[3], (3, 3, 1, DIM), jnp.float32) * 0.1
        dw_b = jnp.zeros((DIM,), jnp.float32)
        return {'x': x, 'qkv_w': qkv_w, 'qkv_b': qkv_b, 'wo_w': wo_w, 'wo_b': wo_b, 'dw_w': dw_w, 'dw_b': dw_b}
    _L1_conv_all = _L1_conv_setup()
    _L1_conv_in = {k: v for k, v in _L1_conv_all.items() if k in ('qkv_w', 'qkv_b', 'wo_w', 'wo_b', 'dw_w', 'dw_b')}
    del _L1_conv_all

    def _L2_conv_setup():
        import jax, jax.numpy as jnp
        import numpy as np
        T0, T1 = (0.0, 0.2)
        NUM_STEPS = 8

        def _build_A(pt, k):
            B, N, P, D = pt.shape
            x = pt - pt.mean(axis=-1, keepdims=True)
            x = x / (pt.std(axis=-1, ddof=1, keepdims=True) + 1e-06)
            corr = jnp.einsum('bnpd,bnqd->bnpq', x, x) / (D - 1 + 1e-06)
            kk = min(k + 1, P)
            _, idx = jax.lax.top_k(corr, kk)
            bi = jnp.arange(B)[:, None, None, None]
            ni = jnp.arange(N)[None, :, None, None]
            pi = jnp.arange(P)[None, None, :, None]
            mask = jnp.zeros_like(corr).at[bi, ni, pi, idx].set(1.0)
            A = corr * mask
            A = 0.5 * (A + jnp.swapaxes(A, -1, -2))
            A = A + jnp.eye(P, dtype=A.dtype)
            deg = jnp.clip(A.sum(-1), 1e-06, None)
            dinv = deg ** (-0.5)
            return dinv[..., :, None] * A * dinv[..., None, :]

        def _rhs(A, L, theta_w, alpha_raw, x):
            alpha = jnp.minimum(jax.nn.softplus(alpha_raw), 2.0)
            diff = alpha * jnp.einsum('bnpr,bnrd->bnpd', L, x)
            react = jnp.einsum('bnpr,bnrd->bnpd', A, x) @ theta_w.T
            return diff + react

        def _odeint(A, theta_w, alpha_raw, y0):
            P = A.shape[-1]
            L = jnp.eye(P, dtype=A.dtype) - A
            h = jnp.asarray((T1 - T0) / NUM_STEPS, y0.dtype)
            f = lambda y: _rhs(A, L, theta_w, alpha_raw, y)

            def step(y, _):
                k1 = f(y)
                k2 = f(y + 0.5 * h * k1)
                k3 = f(y + 0.5 * h * k2)
                k4 = f(y + h * k3)
                return (y + h / 6.0 * (k1 + 2 * k2 + 2 * k3 + k4), None)
            y, _ = jax.lax.scan(step, y0, None, length=NUM_STEPS)
            return y
        key = jax.random.key(seed)
        k1, k2 = jax.random.split(key, 2)
        B, N, P, D = (16, 128, 32, 64)
        patch_tokens = jax.random.normal(k1, (B, N, P, D), dtype=jnp.float32)
        theta_w = jax.random.normal(k2, (D, D), dtype=jnp.float32) * 0.05
        alpha_raw = jnp.full((1,), 0.1, dtype=jnp.float32)
        return {'patch_tokens': patch_tokens, 'theta_w': theta_w, 'alpha_raw': alpha_raw, 'k': 8}
    _L2_conv_all = _L2_conv_setup()
    _L2_conv_in = {k: v for k, v in _L2_conv_all.items() if k in ('theta_w', 'alpha_raw')}
    del _L2_conv_all

    def _L3_conv_setup():
        import jax, jax.numpy as jnp
        import numpy as np
        B, N, DIN, DOUT = (16, 64, 64, 64)
        key = jax.random.key(seed)
        k = jax.random.split(key, 4)
        scale_w = 1.0 / np.sqrt(DIN)
        return {'X': jax.random.normal(k[0], (B, N, N, DIN), dtype=jnp.float32), 'Ws': jax.random.normal(k[1], (15, DIN, DOUT), dtype=jnp.float32) * scale_w, 'Wm': jax.random.normal(k[2], (DOUT, DOUT), dtype=jnp.float32) * (1.0 / np.sqrt(DOUT)), 'bm': jax.random.normal(k[3], (DOUT,), dtype=jnp.float32) * 0.01}
    _L3_conv_all = _L3_conv_setup()
    _L3_conv_in = {k: v for k, v in _L3_conv_all.items() if k in ('Ws', 'Wm', 'bm')}
    del _L3_conv_all
    return {'x': x, 'L0_conv_gamma': _L0_conv_in['gamma'], 'L0_conv_beta': _L0_conv_in['beta'], 'L0_conv_Wq': _L0_conv_in['Wq'], 'L0_conv_Wk': _L0_conv_in['Wk'], 'L0_conv_Wv': _L0_conv_in['Wv'], 'L0_conv_Wb': _L0_conv_in['Wb'], 'L0_conv_Wg': _L0_conv_in['Wg'], 'L0_conv_bg': _L0_conv_in['bg'], 'L0_conv_Wo': _L0_conv_in['Wo'], 'L0_conv_bo': _L0_conv_in['bo'], 'L1_conv_qkv_w': _L1_conv_in['qkv_w'], 'L1_conv_qkv_b': _L1_conv_in['qkv_b'], 'L1_conv_wo_w': _L1_conv_in['wo_w'], 'L1_conv_wo_b': _L1_conv_in['wo_b'], 'L1_conv_dw_w': _L1_conv_in['dw_w'], 'L1_conv_dw_b': _L1_conv_in['dw_b'], 'L2_conv_theta_w': _L2_conv_in['theta_w'], 'L2_conv_alpha_raw': _L2_conv_in['alpha_raw'], 'L3_conv_Ws': _L3_conv_in['Ws'], 'L3_conv_Wm': _L3_conv_in['Wm'], 'L3_conv_bm': _L3_conv_in['bm']}

def reference(x, L0_conv_gamma, L0_conv_beta, L0_conv_Wq, L0_conv_Wk, L0_conv_Wv, L0_conv_Wb, L0_conv_Wg, L0_conv_bg, L0_conv_Wo, L0_conv_bo, L1_conv_qkv_w, L1_conv_qkv_b, L1_conv_wo_w, L1_conv_wo_b, L1_conv_dw_w, L1_conv_dw_b, L2_conv_theta_w, L2_conv_alpha_raw, L3_conv_Ws, L3_conv_Wm, L3_conv_bm):
    import jax
    import jax.numpy as jnp

    def _L0_conv_ref(pair, gamma, beta, Wq, Wk, Wv, Wb, Wg, bg, Wo, bo):
        import jax, jax.numpy as jnp
        import numpy as np
        D_PAIR = 64
        N_HEAD = 4
        D_HID = 32
        SCALING = 1.0 / np.sqrt(D_HID)

        def _layernorm(x, gamma, beta, eps=1e-05):
            mu = jnp.mean(x, axis=-1, keepdims=True)
            var = jnp.var(x, axis=-1, keepdims=True)
            return (x - mu) * jax.lax.rsqrt(var + eps) * gamma + beta
        B, L = pair.shape[:2]
        x = _layernorm(pair, gamma, beta)
        q = (x @ Wq).reshape(B, L, L, N_HEAD, D_HID) * SCALING
        k = (x @ Wk).reshape(B, L, L, N_HEAD, D_HID)
        v = (x @ Wv).reshape(B, L, L, N_HEAD, D_HID)
        bias = x @ Wb
        gate = jax.nn.sigmoid(x @ Wg + bg)
        attn = jnp.einsum('bijhd,bikhd->bijkh', q, k)
        attn = attn + bias[:, None]
        attn = jax.nn.softmax(attn, axis=-2)
        out = jnp.einsum('bijkh,bikhd->bijhd', attn, v).reshape(B, L, L, N_HEAD * D_HID)
        out = gate * out
        return out @ Wo + bo

    def _L1_conv_ref(x, qkv_w, qkv_b, wo_w, wo_b, dw_w, dw_b):
        import jax, jax.numpy as jnp
        import numpy as np
        DIM = 64
        QK = 64
        HEADS = 8
        NWIN = 8
        KVWIN = 4
        TOPK = 4
        SCALE = QK ** (-0.5)
        N, H, W, C = x.shape
        J = NWIN
        h = H // J
        ckv = QK + DIM
        xr = x.reshape(N, J, h, W, C)
        qkv = jnp.einsum('njhwc,oc->njhwo', xr, qkv_w) + qkv_b
        q = qkv[..., :QK]
        kv = qkv[..., QK:]
        q_win = jax.lax.stop_gradient(q.mean((2, 3)))
        logits = jnp.einsum('nic,njc->nij', q_win * SCALE, q_win)
        _, topk_idx = jax.lax.top_k(logits, TOPK)
        kvp = kv.reshape(N, J, KVWIN, h // KVWIN, KVWIN, W // KVWIN, ckv).mean((3, 5))
        kvp = kvp.reshape(N, J, KVWIN * KVWIN, ckv)
        fkv = kvp[jnp.arange(N)[:, None, None], topk_idx]
        kf = fkv[..., :QK]
        vf = fkv[..., QK:]
        dh = QK // HEADS
        dv = DIM // HEADS
        kw2 = TOPK * KVWIN * KVWIN
        kf = kf.reshape(N, J, kw2, HEADS, dh)
        vf = vf.reshape(N, J, kw2, HEADS, dv)
        qp = q.reshape(N, J, h * W, HEADS, dh)
        attn = jnp.einsum('npqmd,npkmd->npmqk', qp * SCALE, kf)
        out = jnp.einsum('npmqk,npkmd->npqmd', attn, vf)
        out = out.reshape(N, H, W, DIM)
        v_glob = kv[..., QK:].reshape(N, H, W, DIM)
        g = jax.lax.conv_general_dilated(v_glob, dw_w, window_strides=(1, 1), padding='SAME', feature_group_count=DIM, dimension_numbers=('NHWC', 'HWIO', 'NHWC')) + dw_b
        out = out + g
        out = jnp.einsum('nhwc,oc->nhwo', out, wo_w) + wo_b
        return out

    def _L2_conv_ref(patch_tokens, theta_w, alpha_raw, k):
        import jax, jax.numpy as jnp
        import numpy as np
        T0, T1 = (0.0, 0.2)
        NUM_STEPS = 8

        def _build_A(pt, k):
            B, N, P, D = pt.shape
            x = pt - pt.mean(axis=-1, keepdims=True)
            x = x / (pt.std(axis=-1, ddof=1, keepdims=True) + 1e-06)
            corr = jnp.einsum('bnpd,bnqd->bnpq', x, x) / (D - 1 + 1e-06)
            kk = min(k + 1, P)
            _, idx = jax.lax.top_k(corr, kk)
            bi = jnp.arange(B)[:, None, None, None]
            ni = jnp.arange(N)[None, :, None, None]
            pi = jnp.arange(P)[None, None, :, None]
            mask = jnp.zeros_like(corr).at[bi, ni, pi, idx].set(1.0)
            A = corr * mask
            A = 0.5 * (A + jnp.swapaxes(A, -1, -2))
            A = A + jnp.eye(P, dtype=A.dtype)
            deg = jnp.clip(A.sum(-1), 1e-06, None)
            dinv = deg ** (-0.5)
            return dinv[..., :, None] * A * dinv[..., None, :]

        def _rhs(A, L, theta_w, alpha_raw, x):
            alpha = jnp.minimum(jax.nn.softplus(alpha_raw), 2.0)
            diff = alpha * jnp.einsum('bnpr,bnrd->bnpd', L, x)
            react = jnp.einsum('bnpr,bnrd->bnpd', A, x) @ theta_w.T
            return diff + react

        def _odeint(A, theta_w, alpha_raw, y0):
            P = A.shape[-1]
            L = jnp.eye(P, dtype=A.dtype) - A
            h = jnp.asarray((T1 - T0) / NUM_STEPS, y0.dtype)
            f = lambda y: _rhs(A, L, theta_w, alpha_raw, y)

            def step(y, _):
                k1 = f(y)
                k2 = f(y + 0.5 * h * k1)
                k3 = f(y + 0.5 * h * k2)
                k4 = f(y + h * k3)
                return (y + h / 6.0 * (k1 + 2 * k2 + 2 * k3 + k4), None)
            y, _ = jax.lax.scan(step, y0, None, length=NUM_STEPS)
            return y
        A = _build_A(jax.lax.stop_gradient(patch_tokens), k)
        alpha_scalar = alpha_raw.reshape(())
        y = _odeint(A, theta_w, alpha_scalar, patch_tokens)
        return jax.nn.relu(y)

    def _L3_conv_ref(X, Ws, Wm, bm):
        import jax, jax.numpy as jnp
        import numpy as np
        B, N, DIN, DOUT = (16, 64, 64, 64)
        Bb, Nn = (X.shape[0], X.shape[1])
        L = lambda v, i: v @ Ws[i - 1]
        diag_part = jnp.diagonal(X, axis1=1, axis2=2).transpose(0, 2, 1)
        sum_of_rows = X.mean(axis=2)
        sum_of_cols = X.mean(axis=1)
        sum_diag_part = diag_part.mean(axis=1)
        sum_all = sum_of_rows.mean(axis=1)
        ret = L(X, 10) + L(X.transpose(0, 2, 1, 3), 11)
        ret = ret + (L(sum_of_rows, 6) + L(sum_of_cols, 8) + L(diag_part, 12))[:, :, None, :]
        ret = ret + (L(sum_of_rows, 7) + L(sum_of_cols, 9) + L(diag_part, 13))[:, None, :, :]
        ret = ret + 2.0 * L(sum_diag_part, 14)[:, None, None, :]
        diag_term = L(diag_part, 1) + L(sum_of_rows, 3) + L(sum_of_cols, 4) + (L(sum_diag_part, 2) + L(sum_all, 5))[:, None, :]
        eye = jnp.eye(Nn, dtype=X.dtype)
        ret = ret + diag_term[:, :, None, :] * eye[None, :, :, None]
        return jax.nn.relu(ret @ Wm + bm)

    def _gn(v, G=32, eps=1e-05):
        B_, H_, W_, C_ = v.shape
        g = v.reshape(B_, H_, W_, G, C_ // G)
        m = jnp.mean(g, axis=(1, 2, 4), keepdims=True)
        s = jnp.var(g, axis=(1, 2, 4), keepdims=True)
        return ((g - m) / jnp.sqrt(s + eps)).reshape(v.shape)

    def _ln_c(v, eps=1e-06):
        m = jnp.mean(v, axis=-1, keepdims=True)
        s = jnp.var(v, axis=-1, keepdims=True)
        return (v - m) / jnp.sqrt(s + eps)

    def _ln_t(v, eps=1e-05):
        m = jnp.mean(v, axis=-1, keepdims=True)
        s = jnp.var(v, axis=-1, keepdims=True)
        return (v - m) / jnp.sqrt(s + eps)

    def _to_tokens(v):
        B_, H_, W_, C_ = v.shape
        return v.reshape(B_, H_ * W_, C_)

    def _from_tokens(t, like):
        return t.reshape(like.shape)
    x = x + _L0_conv_ref(_gn(x), L0_conv_gamma, L0_conv_beta, L0_conv_Wq, L0_conv_Wk, L0_conv_Wv, L0_conv_Wb, L0_conv_Wg, L0_conv_bg, L0_conv_Wo, L0_conv_bo)
    x = x + _L1_conv_ref(_gn(x), L1_conv_qkv_w, L1_conv_qkv_b, L1_conv_wo_w, L1_conv_wo_b, L1_conv_dw_w, L1_conv_dw_b)
    x = x + _L2_conv_ref(_gn(x), L2_conv_theta_w, L2_conv_alpha_raw, 8)
    x = x + _L3_conv_ref(_gn(x), L3_conv_Ws, L3_conv_Wm, L3_conv_bm)
    return x

_drawn_inputs = setup_inputs


def setup_inputs(seed=0):
    import zlib

    import numpy as np

    out = dict(_drawn_inputs(seed))
    spreads = {'L0_conv_gamma': (1.0, 0.6),
     'L0_conv_beta': (0.0, 0.8),
     'L0_conv_bg': (1.0, 0.6),
     'L0_conv_bo': (0.0, 0.1),
     'L1_conv_qkv_b': (0.0, 0.8),
     'L1_conv_wo_b': (0.0, 0.8),
     'L1_conv_dw_b': (0.0, 2.0)}
    factors = {'L0_conv_Wq': 8.0,
     'L0_conv_Wk': 8.0,
     'L0_conv_Wv': 8.0,
     'L0_conv_Wb': 8.0,
     'L0_conv_Wg': 8.0,
     'L0_conv_Wo': 8.0,
     'L1_conv_qkv_w': 6.351,
     'L1_conv_wo_w': 3.646,
     'L1_conv_dw_w': 7.419,
     'L3_conv_bm': 64.0,
     'L2_conv_theta_w': 8.0}
    for name, (base, spread) in spreads.items():
        noise = np.random.default_rng([zlib.crc32(name.encode()), seed]).standard_normal(out[name].shape)
        drawn = base * np.exp(spread * noise) if base else spread * noise
        out[name] = jnp.asarray(drawn.astype(out[name].dtype))
    for name, factor in factors.items():
        out[name] = (out[name] * factor).astype(out[name].dtype)
    return out
```

```python
from contextlib import ExitStack
from math import comb

import concourse.bass as bass
import numpy as np
from concourse import mybir

F32 = mybir.dt.float32
ALU = mybir.AluOpType
ACT = mybir.ActivationFunctionType
AX = mybir.AxisListType
ds = bass.ds

L = 128
C = 64
HEADS, HD = 4, 32
ROWS = 4
GROUPS = L // ROWS
CH = ROWS * L
NWIN, KVW = 8, 4
TOPW = 4
QHEADS, QD = 8, 8
CELL = (L // NWIN // KVW) * (L // KVW)
TOPK = 8
STEPS, T_END = 8, 0.2
DEG = 4 * STEPS
H_STEP = T_END / STEPS
BABY = 4
GIANTS = DEG // BABY
BIG = 3.0e38
PW = L + 2

CONSTS = {}
_at = 0
for _name, _n in (("ident", 128), ("pair", 64), ("expand", 128), ("headmask", 64), ("earlier", 64), ("rk", DEG + 1)):
    CONSTS[_name] = slice(_at, _at + _n)
    _at += _n
NCONST = _at
CONSTS["minus"] = slice(CONSTS["pair"].start, CONSTS["pair"].start + L + 2)


def constants():
    k = np.zeros((128, NCONST), np.float32)
    k[:, CONSTS["ident"]] = np.eye(128)
    c = np.arange(C)
    k[:C, CONSTS["pair"]] = 0.5 * (c[:, None] // 2 == c[None, :] // 2)
    k[:NWIN, CONSTS["expand"]] = np.arange(NWIN)[:, None] == np.arange(128)[None, :] // (KVW * KVW)
    k[:C, CONSTS["headmask"]] = c[:, None] // QD == c[None, :] // QD
    k[:, CONSTS["earlier"]] = (np.arange(8)[None, :] < np.arange(8)[:, None]).reshape(1, 64)
    p = np.ones(1)
    for _ in range(STEPS):
        p = np.convolve(p, [1.0, 1.0, 1 / 2, 1 / 6, 1 / 24])
    for m in range(DEG + 1):
        for j in range(DEG + 1 - m):
            k[m, CONSTS["rk"].start + j] = p[m + j] * comb(m + j, j)
    k[C, CONSTS["minus"]] = -np.pad(np.ones(L), 1)
    return k


class Chain:

    def __init__(self, sem):
        self.eng, self.sem, self.n = None, sem, 0

    def __call__(self, ins):
        ins.then_inc(self.sem, 1)
        self.n += 1
        self.eng.wait_ge(self.sem, self.n)




class Memory:

    ARENA_COLS = 9088

    def __init__(self, nc, ctx):
        self.nc, self.ctx, self.sems, self.chains = nc, ctx, {}, {}

        def sb(name, shape):
            return ctx.enter_context(nc.sbuf_tensor(name, shape, F32))

        self.img = sb("img", [128, PW * PW])
        self.flat = sb("flat", [C + 1, L * L])
        self.nat = sb("nat", [L, L * C])
        self.arena = sb("arena", [128, self.ARENA_COLS])
        self.const = sb("const", [128, NCONST])
        self.w0 = sb("w0", [C + 1, 4 * 128])
        self.w0b = sb("w0b", [C + 1, HEADS])
        self.theta = sb("theta", [128, 2, 512])
        self.theta_top = sb("theta_top", [C, C])
        self.stats = sb("stats", [C, GROUPS * 6])
        self.scale = sb("scale", [C + 1, 1])
        self.shift = sb("shift", [C, 1])
        self.cells = sb("cells", [C, GROUPS * KVW])
        self.eps = sb("eps", [128, 1])
        self.bo = sb("bo", [C, 1])
        self.one = sb("one", [1, 128])
        self.bank = [ctx.enter_context(nc.psum_tensor(f"bank{i}", [128, 512], F32)) for i in range(4)]
        self.quad = ctx.enter_context(nc.psum_tensor("quad", [128, 4, 512], F32))
        self.bank += [self.quad[:, i, :] for i in range(4)]
        self.img3 = self.img[:, :].rearrange("p (r c) -> p r c", c=PW)
        self.nat3 = self.nat[:, :].rearrange("p (i c) -> p i c", c=C)
        self.arena_at = 0

    def sem(self, name):
        if name not in self.sems:
            self.sems[name] = self.ctx.enter_context(self.nc.semaphore(name))
        return self.sems[name]

    def chain(self, eng, name):
        if name not in self.chains:
            self.chains[name] = Chain(self.sem(name + "_chain"))
        self.chains[name].eng = eng
        return self.chains[name]

    def need(self, eng, sem, value):
        if isinstance(value, int):
            if value > 0:
                eng.wait_ge(sem, value)
            return
        eng.wait_ge(sem, value)
        eng.sem_inc(self.sem("passed"))

    def k(self, name, rows):
        return self.const[0:rows, CONSTS[name]]

    def inner(self, row, rows=ROWS):
        return self.img3[0:C, ds(row + 1, rows), 1:L + 1]

    def open_arena(self):
        self.arena_at = 0

    def take(self, cols, rows=128):
        assert self.arena_at + cols <= self.ARENA_COLS, "the arena is full"
        at = self.arena_at
        self.arena_at += cols
        return self.arena[0:rows, at:at + cols]


def load_and_prepare(nc, m, args):
    S = m.sem
    ident = m.k("ident", 128)
    ident64 = ident[0:C, 0:C]
    m.open_arena()
    w_raw = m.take(4 * 128, C)
    wb_raw = m.take(HEADS, C)
    fold0 = m.take(C + 1, C)
    gamma = m.take(1, C)
    bg_row = m.take(128, C + 1)
    theta_raw = m.take(C, C)
    alpha = m.take(8)
    powers = m.take(DEG + 1)
    power_col = m.take(1)
    picked = m.take(DEG + 1)
    coef = m.take(DEG + 1)
    turn = m.take(2 * C, C)
    pw = m.take((DEG + 1) * C).rearrange("p (j e) -> p j e", e=C)
    PIECES = 4
    per = L // PIECES
    vectors = [
        (w_raw[:, 0:128], args["L0_conv_Wq"]), (w_raw[:, 128:256], args["L0_conv_Wk"]),
        (w_raw[:, 256:384], args["L0_conv_Wv"]), (w_raw[:, 384:512], args["L0_conv_Wg"]),
        (wb_raw, args["L0_conv_Wb"]),
        (gamma, args["L0_conv_gamma"].rearrange("(c a) -> c a", a=1)),
        (fold0[:, C:C + 1], args["L0_conv_beta"].rearrange("(c a) -> c a", a=1)),
        (bg_row[C:C + 1, :], args["L0_conv_bg"].rearrange("(a c) -> a c", a=1)),
        (m.bo[:, :], args["L0_conv_bo"].rearrange("(c a) -> c a", a=1)),
        (theta_raw, args["L2_conv_theta_w"]),
        (alpha[:, 0:1], args["L2_conv_alpha_raw"].rearrange("(a c) -> a c", a=1).to_broadcast([128, 1])),
    ]
    weights_in, consts_in, copied, chunk_turned = S("a_weights_in"), S("a_consts_in"), S("a_copied"), S("a_chunk_turned")
    piece_in = [S(f"a_x_in{n}") for n in range(PIECES)]
    x_nat = args["x"].rearrange("b i j c -> (b j) i c")
    DOUBLINGS = [1, 2, 4, 8, 16]
    with nc.Block() as block:

        @block.sync
        def _(sp):
            sp.dma_start(m.const[:, :], args["constants"]).then_inc(consts_in, 16)
            for n in range(PIECES):
                sp.dma_start(m.nat3[:, n * per:(n + 1) * per, :], x_nat[:, n * per:(n + 1) * per, :]).then_inc(piece_in[n], 16)

        @block.gpsimd
        def _(pool):
            step = m.chain(pool, "pool")
            step(pool.memset(m.img3[0:C, 0, :], 0.0))
            step(pool.memset(m.img3[0:C, L + 1, :], 0.0))
            step(pool.memset(m.img3[C:128, L, :], 0.0))
            step(pool.memset(m.img3[0:C, 1:L + 1, 0:1], 0.0))
            step(pool.memset(m.img3[0:C, 1:L + 1, L + 1:L + 2], 0.0))
            step(pool.memset(m.flat[C:C + 1, :], 1.0))
            step(pool.memset(m.eps[:, :], 1e-5))
            step(pool.memset(m.one[:, :], 1.0))
            step(pool.memset(m.scale[C:C + 1, :], 1.0))

        @block.scalar
        def _(act):
            for dst, src in vectors:
                act.dma_start(dst, src).then_inc(weights_in, 16)
            act.wait_ge(weights_in, 16 * len(vectors))
            step = m.chain(act, "act")
            step(act.activation(alpha[:, 1:2], alpha[:, 0:1], ACT.Abs))
            step(act.activation(alpha[:, 2:3], alpha[:, 1:2], ACT.Exp, scale=-1.0))
            act.activation(alpha[:, 3:4], alpha[:, 2:3], ACT.Ln, bias=1.0).then_inc(S("a_ln"), 1)
            for q in range(GROUPS):
                act.wait_ge(chunk_turned, q + 1)
                act.activation(m.inner(ROWS * q), m.bank[q % 4][0:C, :].rearrange("p (r c) -> p r c", c=L),
                               ACT.Copy).then_inc(copied, 1)

        @block.vector
        def _(dve):
            step = m.chain(dve, "dve")
            dve.wait_ge(consts_in, 16)
            dve.wait_ge(weights_in, 16 * len(vectors))
            dve.tensor_scalar(fold0[:, 0:C], ident64, gamma, None, ALU.mult).then_inc(S("a_fold0"), 1)
            dve.wait_ge(S("a_ln"), 1)
            step(dve.tensor_scalar(alpha[:, 4:5], alpha[:, 0:1], 0.0, alpha[:, 3:4], ALU.max, ALU.add))
            step(dve.tensor_scalar(alpha[:, 5:6], alpha[:, 4:5], 2.0, None, ALU.min))
            step(dve.memset(powers[:, 0:1], 1.0))
            step(dve.tensor_scalar(powers[:, 1:2], alpha[:, 5:6], H_STEP, None, ALU.mult))
            have = 2
            while have < DEG + 1:
                n = min(have - 1, DEG + 1 - have)
                step(dve.tensor_scalar(powers[:, have:have + n], powers[:, 1:1 + n], powers[:, have - 1:have], None, ALU.mult))
                have += n
            n = DEG + 1
            step(dve.tensor_tensor(picked[0:n, :], powers[0:n, :], ident[0:n, 0:n], ALU.mult))
            dve.tensor_reduce(power_col[0:n, :], picked[0:n, :], AX.X, ALU.add).then_inc(S("a_power_col"), 1)
            step(dve.tensor_scalar(theta_raw, theta_raw, H_STEP, None, ALU.mult))
            step(dve.tensor_scalar(turn[:, C:2 * C], ident64, powers[0:C, 1:2], None, ALU.mult))
            step(dve.tensor_tensor(turn[:, 0:C], theta_raw, turn[:, C:2 * C], ALU.subtract))
            dve.tensor_copy(turn[:, C:2 * C], turn[:, 0:C]).then_inc(S("a_turn"), 1)
            dve.wait_ge(S("a_w0_made"), 1)
            step(dve.tensor_copy(m.w0[:, :], m.bank[4][0:C + 1, :]))
            dve.tensor_scalar(m.w0[:, 0:128], m.w0[:, 0:128], float(1.0 / np.sqrt(HD)), None, ALU.mult)
            dve.tensor_tensor(m.w0[C:C + 1, 384:512], m.w0[C:C + 1, 384:512], bg_row[C:C + 1, :], ALU.add)
            dve.wait_ge(S("a_w0b_made"), 1)
            dve.tensor_copy(m.w0b[:, :], m.bank[5][0:C + 1, 0:HEADS])
            dve.wait_ge(S("a_coef_made"), 1)
            dve.tensor_copy(coef, m.bank[6][:, 0:DEG + 1]).then_inc(S("a_coef"), 1)
            step(dve.tensor_copy(pw[0:C, 0, :], ident64))
            step(dve.tensor_copy(pw[C:128, 0, :], ident[C:128, C:128]))
            dve.wait_ge(S("a_first_power"), 1)
            dve.tensor_copy(pw[:, 1, :], m.bank[7][:, 0:C]).then_inc(S("a_powers"), 1)
            for i, d in enumerate(DOUBLINGS):
                if d > 1:
                    dve.wait_ge(S("a_power_turned"), i)
                    for half in range(2):
                        dve.tensor_copy(turn[:, half * C:(half + 1) * C], m.bank[7][0:C, 0:C]).then_inc(S("a_power_turn"), 1)
                for at in range(0, d, 8):
                    n = min(8, d - at)
                    dve.wait_ge(S("a_doubled"), i + 1 + (at > 0))
                    dve.tensor_copy(pw[:, d + 1 + at:d + 1 + at + n, :],
                                    m.bank[5 + (at > 0)][:, 0:n * C].rearrange("p (j e) -> p j e", e=C)).then_inc(S("a_powers"), 1)
            dve.wait_ge(S("a_powers"), 1 + len(DOUBLINGS) + 1)
            dve.wait_ge(S("a_coef"), 1)
            for j in range(DEG):
                half = slice(0, C) if j % 2 == 0 else slice(C, 128)
                g, b = divmod(j, BABY)
                dve.tensor_scalar(m.theta[half, b // 2, g * C:(g + 1) * C], pw[half, j, :], coef[half, j:j + 1], None, ALU.mult)
            dve.tensor_scalar(m.theta_top[:, :], pw[0:C, DEG, :], coef[0:C, DEG:DEG + 1], None, ALU.mult)
            for q in range(GROUPS):
                dve.wait_ge(copied, q + 1)
                dve.bn_stats(m.stats[:, 6 * q:6 * q + 6], m.inner(ROWS * q))

        @block.tensor
        def _(pe):
            pe.wait_ge(consts_in, 16)
            pe.wait_ge(S("a_fold0"), 1)
            pe.matmul(m.bank[4][0:C + 1, :], fold0, w_raw, start=True, stop=True).then_inc(S("a_w0_made"), 1)
            pe.matmul(m.bank[5][0:C + 1, 0:HEADS], fold0, wb_raw, start=True, stop=True).then_inc(S("a_w0b_made"), 1)
            pe.wait_ge(S("a_power_col"), 1)
            n = DEG + 1
            pe.matmul(m.bank[6][:, 0:n], power_col[0:n, :].to_broadcast([n, 128]), m.k("rk", n),
                      start=True, stop=True).then_inc(S("a_coef_made"), 1)
            pe.wait_ge(S("a_turn"), 1)
            pe.matmul(m.bank[7][:, 0:C], turn, ident64, start=True, stop=True).then_inc(S("a_first_power"), 1)
            pe.wait_ge(S("a_coef"), 1)
            for i, d in enumerate(DOUBLINGS):
                pe.wait_ge(S("a_powers"), i + 1)
                if d > 1:
                    pe.wait_ge(S("a_power_turn"), 2 * i)
                for at in range(0, d, 8):
                    n = min(8, d - at)
                    pe.matmul(m.bank[5 + (at > 0)][:, 0:n * C], turn, pw[0:C, 1 + at:1 + at + n, :],
                              start=True, stop=True).then_inc(S("a_doubled"), 1)
                if i + 1 < len(DOUBLINGS):
                    pe.wait_ge(S("a_powers"), i + 2)
                    pe.transpose(m.bank[7][0:C, 0:C], pw[0:C, 2 * d, :], ident64).then_inc(S("a_power_turned"), 1)
            for q in range(GROUPS):
                for r in range(ROWS):
                    i = ROWS * q + r
                    if i % per == 0:
                        pe.wait_ge(piece_in[i // per], 16)
                    if r == 0:
                        m.need(pe, copied, q - 3)
                    last = pe.transpose(m.bank[q % 4][0:C, r * L:(r + 1) * L], m.nat3[:, i, :], ident)
                last.then_inc(chunk_turned, 1)


def group_norm(nc, m, layer):
    mv, d, mg, e, std = (m.take(n, C) for n in (2, 1, 1, 1, 1))
    S = lambda name: m.sem("gn_" + name)
    acc = m.bank[0]
    with nc.Block() as block:

        @block.vector
        def _(dve):
            step = m.chain(dve, "dve")
            dve.bn_aggr(mv, m.stats[:, :]).then_inc(S("mean"), 1)
            dve.wait_ge(S("group_mean"), layer + 1)
            step(dve.tensor_copy(mg, acc[0:C, 0:1]))
            step(dve.tensor_tensor(d, mv[:, 0:1], mg, ALU.subtract))
            dve.scalar_tensor_tensor(out=e, in0=d, scalar=d, in1=mv[:, 1:2], op0=ALU.mult, op1=ALU.add).then_inc(S("var"), 1)
            dve.wait_ge(S("std"), layer + 1)
            step(dve.reciprocal(m.scale[0:C, :], std))
            dve.scalar_tensor_tensor(out=m.shift[:, :], in0=mg, scalar=-1.0, in1=m.scale[0:C, :], op0=ALU.mult, op1=ALU.mult)

        @block.tensor
        def _(pe):
            pe.wait_ge(S("mean"), layer + 1)
            pe.matmul(acc[0:C, 0:1], m.k("pair", C), mv[:, 0:1], start=True, stop=True).then_inc(S("group_mean"), 1)
            pe.wait_ge(S("var"), layer + 1)
            pe.matmul(acc[0:C, 1:2], m.k("pair", C), e, start=True, stop=True).then_inc(S("group_var"), 1)

        @block.scalar
        def _(act):
            act.wait_ge(S("group_var"), layer + 1)
            act.activation(std, acc[0:C, 1:2], ACT.Sqrt, bias=m.eps[0:C, :]).then_inc(S("std"), 1)


def layer0_norm(nc, m):
    ident = m.k("ident", 128)
    m.open_arena()
    m.bias = m.take(HEADS * L)
    bias_t = m.take(HEADS * L)
    y = [m.take(CH, C) for _ in range(2)]
    mv = [m.take(2 * ROWS).rearrange("p (r s) -> p r s", s=2) for _ in range(2)]
    st = [m.take(6 * ROWS) for _ in range(2)]
    rstd = [m.take(ROWS) for _ in range(2)]
    std = [m.take(ROWS) for _ in range(2)]
    z = [m.take(ROWS * C).rearrange("p (r c) -> p r c", c=C) for _ in range(2)]
    S = lambda name: m.sem(f"z_{name}")
    y_ready, y_turned, measured, std_ready = S("y_ready"), S("y_turned"), S("measured"), S("std_ready")
    rstd_ready, z_ready, z_turned, z_stored, aggr = S("rstd_ready"), S("z_ready"), S("z_turned"), S("z_stored"), S("stats_ready")

    def over_chunks(eng, emit):
        for q in range(4):
            emit(q, q % 2)
        with eng.Fori(0, (GROUPS - 4) // 2, 1) as it:
            for b in range(2):
                emit(it * 2 + (4 + b), b)
        for q in (GROUPS, GROUPS + 1):
            emit(q, q % 2)

    def live(q, lo, hi):
        return not isinstance(q, int) or lo <= q < hi

    with nc.Block() as block:

        @block.scalar
        def _(act):
            def emit(q, b):
                if live(q, 0, GROUPS):
                    m.need(act, y_turned, q - 1)
                    act.activation(y[b].rearrange("p (r c) -> p r c", c=L), m.inner(q * ROWS), ACT.Identity,
                                   scale=m.scale[0:C, :], bias=m.shift[:, :]).then_inc(y_ready, 1)
                if live(q, 1, GROUPS + 1):
                    o = 1 - b
                    m.need(act, measured, q)
                    act.activation(std[o], mv[o][:, :, 1], ACT.Sqrt, bias=m.eps[:, :]).then_inc(std_ready, 1)
                if live(q, 2, GROUPS + 2):
                    m.need(act, z_turned, q - 1)
                    act.activation(m.flat[0:C, ds((q - 2) * CH, CH)], m.bank[2 + b][0:C, :], ACT.Copy).then_inc(z_stored, 1)
            over_chunks(act, emit)

        @block.tensor
        def _(pe):
            def emit(q, b):
                if live(q, 0, GROUPS):
                    m.need(pe, y_ready, q + 1)
                    m.need(pe, z_ready, q - 1)
                    for r in range(ROWS):
                        last = pe.transpose(m.bank[b][:, r * C:(r + 1) * C], y[b][:, r * L:(r + 1) * L], ident[0:C, 0:C])
                    last.then_inc(y_turned, 1)
                if live(q, 2, GROUPS + 2):
                    m.need(pe, z_ready, q - 1)
                    m.need(pe, z_stored, q - 3)
                    for r in range(ROWS):
                        last = pe.transpose(m.bank[2 + b][0:C, r * L:(r + 1) * L], z[b][:, r, :], ident)
                    last.then_inc(z_turned, 1)
            over_chunks(pe, emit)
            pe.wait_ge(z_stored, GROUPS)
            for j in range(L):
                last = pe.matmul(m.bank[4][:, j:HEADS * L:L], m.flat[:, j * L:(j + 1) * L], m.w0b[:, :],
                                 start=True, stop=True, skip_group_check=True)
            last.then_inc(S("bias_made"), 1)
            pe.wait_ge(S("bias_copied"), 1)
            for h in range(HEADS):
                last = pe.transpose(m.bank[5][:, h * L:(h + 1) * L], bias_t[:, h * L:(h + 1) * L], ident)
            last.then_inc(S("bias_turned"), 1)

        @block.vector
        def _(dve):
            def emit(q, b):
                if live(q, 0, GROUPS):
                    m.need(dve, y_turned, q + 1)
                    m.need(dve, std_ready, q - 1)
                    for r in range(ROWS):
                        dve.bn_stats(st[b][:, 6 * r:6 * r + 6], m.bank[b][:, r * C:(r + 1) * C]).then_inc(aggr, 1)
                    for r in range(ROWS):
                        m.need(dve, aggr, q * ROWS + (r + 1))
                        last = dve.bn_aggr(mv[b][:, r, :], st[b][:, 6 * r:6 * r + 6])
                    last.then_inc(measured, 1)
                if live(q, 1, GROUPS + 1):
                    o = 1 - b
                    m.need(dve, std_ready, q)
                    dve.reciprocal(rstd[o], std[o]).then_inc(rstd_ready, 1)
                    m.need(dve, rstd_ready, q)
                    m.need(dve, z_turned, q - 2)
                    for r in range(ROWS):
                        last = dve.tensor_scalar(z[o][:, r, :], m.bank[o][:, r * C:(r + 1) * C], mv[o][:, r, 0:1],
                                                 rstd[o][:, r:r + 1], ALU.subtract, ALU.mult)
                    last.then_inc(z_ready, 1)
            over_chunks(dve, emit)
            dve.wait_ge(S("bias_made"), 1)
            dve.tensor_copy(bias_t, m.bank[4][:, :]).then_inc(S("bias_copied"), 1)
            dve.wait_ge(S("bias_turned"), 1)
            dve.tensor_copy(m.bias, m.bank[5][:, :])


def layer0_attention(nc, m, args):
    ident = m.k("ident", 128)
    m.arena_at = HEADS * L
    spare = [m.nat[:, i * 2048:(i + 1) * 2048] for i in range(4)]
    prob = [spare[0], spare[1]]
    qT = [spare[2][:, i * CH:(i + 1) * CH] for i in (0, 1)]
    kT = [spare[2][:, i * CH:(i + 1) * CH] for i in (2, 3)]
    v = [spare[3][:, i * CH:(i + 1) * CH] for i in (0, 1)]
    th = [spare[3][:, i * CH:(i + 1) * CH] for i in (2, 3)]
    zs = [m.take(CH, C + 1) for _ in range(2)]
    pT = [m.take(HEADS * L) for _ in range(2)]
    gated = m.take(CH)
    o_nat = m.take(CH)
    oT = m.take(CH)
    wo = m.take(C)
    least = [m.take(ROWS * HEADS) for _ in range(2)]
    total = [m.take(ROWS * HEADS) for _ in range(2)]
    rtotal = m.take(ROWS * HEADS)
    S = lambda name: m.sem(f"l0_{name}")
    z_staged, wo_ready = S("z_staged"), S("wo_ready")
    q_made, k_made, v_made, g_made = S("q_made"), S("k_made"), S("v_made"), S("g_made")
    q_ready, k_ready, v_ready, th_ready = S("q_ready"), S("k_ready"), S("v_ready"), S("th_ready")
    scores_made, shifted, probs_ready = S("scores_made"), S("shifted"), S("probs_ready")
    probs_turned, turned_even, turned_odd = S("probs_turned"), S("turned_even"), S("turned_odd")
    av_made, rtotal_ready, gated_ready, o_ready = S("av_made"), S("rtotal_ready"), S("gated_ready"), S("o_ready")
    o_turned, oT_ready, out_made, x1_ready = S("o_turned"), S("oT_ready"), S("out_made"), S("x1_ready")
    STEPS0 = GROUPS + 2
    PEEL = 3

    def over_steps(eng, emit):
        for g in range(PEEL + 1):
            emit(g, g % 2)
        with eng.Fori(0, (GROUPS - PEEL - 3) // 2, 1) as it:
            for b in range(2):
                emit(it * 2 + (PEEL + 1 + b), b)
        for g in range(GROUPS - 2, STEPS0):
            emit(g, g % 2)

    def live(g, lo, hi):
        return not isinstance(g, int) or lo <= g < hi

    def rows(t):
        return t.rearrange("p (r x) -> p r x", r=ROWS)

    with nc.Block() as block:

        @block.sync
        def _(sp):
            sp.dma_start(wo, args["L0_conv_Wo"]).then_inc(wo_ready, 16)

        @block.gpsimd
        def _(pool):
            for g in (0, 1):
                pool.tensor_copy(zs[g], m.flat[:, g * CH:(g + 1) * CH]).then_inc(z_staged, 1)

            def emit(g, b):
                if live(g, 1, GROUPS + 1):
                    m.need(pool, gated_ready, g)
                    m.need(pool, o_turned, g - 1)
                    pool.tensor_tensor(o_nat.rearrange("p (x d) -> p x d", d=HD), gated.rearrange("p (x d) -> p x d", d=HD),
                                       rtotal.unsqueeze(2).broadcast_to([128, ROWS * HEADS, HD]), ALU.mult).then_inc(o_ready, 1)
                if live(g, 0, GROUPS - 2):
                    m.need(pool, g_made, g + 1)
                    pool.tensor_copy(zs[b], m.flat[:, ds((g + 2) * CH, CH)]).then_inc(z_staged, 1)
            over_steps(pool, emit)

        @block.scalar
        def _(act):
            def copy_q(g, b):
                m.need(act, q_made, g + 1)
                act.activation(qT[b], m.bank[2][:, :], ACT.Copy).then_inc(q_ready, 1)

            def emit(g, b):
                if live(g, 2, GROUPS + 2):
                    m.need(act, o_turned, g - 1)
                    m.need(act, out_made, g - 2)
                    act.activation(oT, m.bank[3][:, :], ACT.Copy).then_inc(oT_ready, 1)
                if live(g, 0, GROUPS - 1):
                    copy_q(g + 1, 1 - b)
                for r in range(ROWS):
                    if live(g, 0, GROUPS):
                        m.need(act, shifted, g * ROWS + (r + 1))
                        for h in range(HEADS):
                            t = prob[b][:, (r * HEADS + h) * L:(r * HEADS + h + 1) * L]
                            last = act.activation(t, t, ACT.Exp, scale=-1.0, bias=least[b][:, r * HEADS + h:r * HEADS + h + 1],
                                                  accum_out=total[b][:, r * HEADS + h:r * HEADS + h + 1])
                        last.then_inc(probs_ready, 1)
                    if r < 2 and live(g, 1, GROUPS + 1):
                        m.need(act, probs_turned, (g - 1) * ROWS + (2 * r + 1))
                        m.need(act, av_made, (g - 1) * ROWS + (2 * r - 1))
                        act.activation(pT[0], m.bank[0][:, :], ACT.Copy).then_inc(turned_even, 1)
                    if r == 2 and live(g, 0, GROUPS):
                        m.need(act, g_made, g + 1)
                        m.need(act, gated_ready, g - 1)
                        act.activation(th[b], m.bank[2][:, :], ACT.Tanh, scale=0.5).then_inc(th_ready, 1)
            copy_q(0, 0)
            over_steps(act, emit)

        @block.vector
        def _(dve):
            dve.wait_ge(wo_ready, 16)
            dve.tensor_scalar(wo, wo, 0.5, None, ALU.mult).then_inc(S("wo_halved"), 1)

            def copy_k(g, b):
                m.need(dve, k_made, g + 1)
                dve.tensor_copy(kT[b], m.bank[2][:, :]).then_inc(k_ready, 1)

            def shift_row(g, b, r):
                for h in range(HEADS):
                    at = (r * HEADS + h) * L
                    last = dve.tensor_tensor_reduce(prob[b][:, at:at + L], m.quad[:, h, r * L:(r + 1) * L],
                                                    m.bias[:, h * L:(h + 1) * L], -1.0, BIG, ALU.add, ALU.min,
                                                    least[b][:, r * HEADS + h:r * HEADS + h + 1])
                last.then_inc(shifted, 1)

            def turn_odd(g, r):
                m.need(dve, probs_turned, (g - 1) * ROWS + (r + 1))
                m.need(dve, av_made, (g - 1) * ROWS + (r - 1))
                dve.tensor_copy(pT[1], m.bank[1][:, :]).then_inc(turned_odd, 1)

            def emit(g, b):
                own, before, older = live(g, 0, GROUPS), live(g, 1, GROUPS + 1), live(g, 2, GROUPS + 2)
                if own:
                    m.need(dve, scores_made, g + 1)
                    m.need(dve, probs_turned, (g - 1) * ROWS)
                    shift_row(g, b, 0)
                if older:
                    m.need(dve, out_made, g - 1)
                    inner = m.inner((g - 2) * ROWS)
                    dve.scalar_tensor_tensor(out=inner, in0=rows(m.bank[3][0:C, :]), scalar=m.bo[:, :], in1=inner,
                                             op0=ALU.add, op1=ALU.add).then_inc(x1_ready, 1)
                if own:
                    shift_row(g, b, 1)
                if live(g, 0, GROUPS - 1):
                    copy_k(g + 1, 1 - b)
                if own:
                    shift_row(g, b, 2)
                if before:
                    turn_odd(g, 1)
                if own:
                    shift_row(g, b, 3)
                    m.need(dve, v_made, g + 1)
                    m.need(dve, av_made, (g - 1) * ROWS)
                    dve.tensor_copy(v[b], m.bank[2][:, :]).then_inc(v_ready, 1)
                if before:
                    turn_odd(g, 3)
                    m.need(dve, probs_ready, g * ROWS)
                    m.need(dve, o_ready, g - 1)
                    dve.reciprocal(rtotal, total[1 - b])
                    m.need(dve, av_made, g * ROWS)
                    m.need(dve, th_ready, g)
                    dve.scalar_tensor_tensor(out=gated, in0=th[1 - b], scalar=1.0, in1=m.bank[3][:, :],
                                             op0=ALU.add, op1=ALU.mult).then_inc(gated_ready, 1)
                if older:
                    m.need(dve, x1_ready, g - 1)
                    dve.bn_stats(m.stats[:, ds((g - 2) * 6, 6)], m.inner((g - 2) * ROWS))
                    dve.tensor_reduce(m.cells[:, ds((g - 2) * KVW, KVW)],
                                      m.inner((g - 2) * ROWS).rearrange("p r (k w) -> p k r w", k=KVW), AX.XY, ALU.add)
            copy_k(0, 0)
            over_steps(dve, emit)

        @block.tensor
        def _(pe):
            def project(g, b, w, made):
                if w < 2:
                    last = pe.matmul(m.bank[2][:, :], m.w0[:, w * 128:(w + 1) * 128], zs[b], start=True, stop=True)
                else:
                    for r in range(ROWS):
                        last = pe.matmul(m.bank[2][:, r * L:(r + 1) * L], zs[b][:, r * L:(r + 1) * L],
                                         m.w0[:, w * 128:(w + 1) * 128], start=True, stop=True)
                last.then_inc(made, 1)

            def turn(g, b, r):
                m.need(pe, probs_ready, (g - 1) * ROWS + (r + 1))
                m.need(pe, turned_odd if r % 2 else turned_even, (g - 1) * 2 + r // 2)
                for h in range(HEADS):
                    at = (r * HEADS + h) * L
                    last = pe.transpose(m.bank[r % 2][:, h * L:(h + 1) * L], prob[1 - b][:, at:at + L], ident)
                last.then_inc(probs_turned, 1)

            def weigh(g, b, r):
                m.need(pe, turned_odd if r % 2 else turned_even, (g - 1) * 2 + (r // 2 + 1))
                if r == 0:
                    m.need(pe, v_ready, g)
                    m.need(pe, x1_ready, g - 1)
                for h in range(HEADS):
                    at = (r * HEADS + h) * HD
                    last = pe.matmul(m.bank[3][:, at:at + HD], pT[r % 2][:, h * L:(h + 1) * L],
                                     v[1 - b][:, at:at + HD], start=True, stop=True)
                last.then_inc(av_made, 1)

            def emit(g, b):
                own, before, older = live(g, 0, GROUPS), live(g, 1, GROUPS + 1), live(g, 2, GROUPS + 2)
                ahead = live(g, 0, GROUPS - 1)
                if own:
                    m.need(pe, q_ready, g + 1)
                    m.need(pe, k_ready, g + 1)
                    m.need(pe, shifted, g * ROWS)
                    for r in range(ROWS):
                        for h in range(HEADS):
                            part = slice(h * HD, (h + 1) * HD)
                            last = pe.matmul(m.quad[:, h, r * L:(r + 1) * L], qT[b][part, r * L:(r + 1) * L],
                                             kT[b][part, r * L:(r + 1) * L], start=True, stop=True)
                    last.then_inc(scores_made, 1)
                if older:
                    m.need(pe, o_ready, g - 1)
                    m.need(pe, gated_ready, g - 1)
                    for r in range(ROWS):
                        last = pe.transpose(m.bank[3][:, r * L:(r + 1) * L], o_nat[:, r * L:(r + 1) * L], ident)
                    last.then_inc(o_turned, 1)
                if ahead:
                    m.need(pe, z_staged, g + 2)
                    m.need(pe, th_ready, g)
                    project(g + 1, 1 - b, 0, q_made)
                if older:
                    m.need(pe, oT_ready, g - 1)
                    pe.matmul(m.bank[3][0:C, :], wo, oT, start=True, stop=True).then_inc(out_made, 1)
                if before:
                    turn(g, b, 0)
                if ahead:
                    m.need(pe, q_ready, g + 2)
                    project(g + 1, 1 - b, 1, k_made)
                if before:
                    turn(g, b, 1)
                    weigh(g, b, 0)
                if own:
                    m.need(pe, k_ready, g + 2 if ahead else g + 1)
                    if not ahead:
                        m.need(pe, th_ready, g)
                    project(g, b, 2, v_made)
                if before:
                    turn(g, b, 2)
                    weigh(g, b, 1)
                if own:
                    m.need(pe, v_ready, g + 1)
                    project(g, b, 3, g_made)
                if before:
                    turn(g, b, 3)
                    weigh(g, b, 2)
                    weigh(g, b, 3)
            pe.wait_ge(z_staged, 1)
            project(0, 0, 0, q_made)
            pe.wait_ge(q_ready, 1)
            project(0, 0, 1, k_made)
            pe.wait_ge(k_ready, 1)
            pe.wait_ge(S("wo_halved"), 1)
            over_steps(pe, emit)


def layer1(nc, m, args):
    ident = m.k("ident", 128)
    ident64 = ident[0:C, 0:C]
    TAPS = 9
    TOKENS = NWIN * KVW * KVW
    m.open_arena()
    kv_raw = m.take(C + 1)
    q_raw = m.take(C + 1, C)
    v_raw = m.take(C + 1, C)
    wo_raw = m.take(C, C)
    dw_raw = m.take(C, TAPS)
    dw_b, wo_b = m.take(1, C), m.take(1, C)
    turned = m.take(192 + C + TAPS, C + 1)
    kvT, qT = turned[:, 0:128], turned[:, 128:192]
    woT, dwT = turned[0:C, 192:256], turned[0:C, 256:256 + TAPS]
    spread = m.take(TAPS * C, C)
    taps = m.take(TAPS * C, C + 1)
    folded = m.take(TAPS * C, C + 1)
    centre = m.take(NWIN * C, C + 1)
    centre_folded = m.take(NWIN * C, C + 1)
    fold = m.take(C + 1, C + 1)
    pooled = m.take(TOKENS, C + 1)
    pooled_win = m.take(NWIN, C + 1)
    kv = m.take(128)
    q_win = m.take(NWIN, C)
    logits = m.take(NWIN, NWIN)
    above = m.take(64, NWIN).rearrange("p (j k) -> p j k", k=NWIN)
    same = m.take(64, NWIN).rearrange("p (j k) -> p j k", k=NWIN)
    rank, chosen, chosen_t = m.take(NWIN, NWIN), m.take(NWIN, NWIN), m.take(NWIN, NWIN)
    token_mask = m.take(NWIN)
    k_masked = m.take(NWIN * C)
    mT = m.take(NWIN * C, C)
    m_wo = m.take(NWIN * C, C)
    const_out = m.take(1, C)
    packed = m.nat[:, 0:2 * (2 + NWIN) * 128].rearrange("p (i k e o) -> p i k e o", i=2, k=2 + NWIN, e=2)
    outer = [packed[:, i, 0:2, :, :] for i in range(2)]
    middle = [packed[:, i, 2:2 + NWIN, :, :] for i in range(2)]
    bias_sum = m.take(C, C + 1)[C:C + 1, :]
    bias_rows = m.take(NWIN * 128, C + 1)[C:C + 1, :].rearrange("p (w e o) -> p w e o", w=NWIN, e=2)
    col_rows = m.take(3 * 128, C + 1)[C:C + 1, :].rearrange("p (x e o) -> p x e o", x=3, e=2)
    edge_rows = m.take(2 * 3 * 128, C + 1)[C:C + 1, :].rearrange("p (t x e o) -> p t x e o", t=2, x=3, e=2)
    bias = m.take(NWIN)
    BANKS = L // 8
    S = lambda name: m.sem(f"l1_{name}")
    loads = [
        (kv_raw[:, 0:C], args["L1_conv_qkv_w"][C:3 * C, :]),
        (kv_raw[:, C:C + 1], args["L1_conv_qkv_b"].rearrange("(o a) -> o a", a=1)[C:3 * C, :]),
        (q_raw[:, 0:C], args["L1_conv_qkv_w"][0:C, :]),
        (q_raw[:, C:C + 1], args["L1_conv_qkv_b"].rearrange("(o a) -> o a", a=1)[0:C, :]),
        (v_raw[:, 0:C], args["L1_conv_qkv_w"][2 * C:3 * C, :]),
        (v_raw[:, C:C + 1], args["L1_conv_qkv_b"].rearrange("(o a) -> o a", a=1)[2 * C:3 * C, :]),
        (wo_raw, args["L1_conv_wo_w"]),
        (dw_raw, args["L1_conv_dw_w"].rearrange("kh kw a m -> (kh kw a) m")),
        (dw_b, args["L1_conv_dw_b"].rearrange("(c a) -> c a", a=1)),
        (wo_b, args["L1_conv_wo_b"].rearrange("(c a) -> c a", a=1)),
    ]
    B = m.bank
    by_window = lambda t: t.rearrange("p (w c) -> p w c", w=NWIN)
    in_pairs = lambda t: t.rearrange("p (m c) -> p m c", c=L)

    def out_rows(g, parity):
        return m.flat[0:C, 8 * g * L:8 * (g + 1) * L].rearrange("p (m e c) -> p m e c", e=2, c=L)[:, :, parity, :]

    def tap(dy, dx, lo=0, hi=C):
        return folded[lo:hi, (3 * dy + dx) * C:(3 * dy + dx + 1) * C]

    with nc.Block() as block:

        @block.sync
        def _(sp):
            for dst, src in loads:
                sp.dma_start(dst, src).then_inc(S("loaded"), 16)

        @block.vector
        def _(dve):
            step = m.chain(dve, "dve")
            step(dve.tensor_scalar(fold, ident[0:C + 1, 0:C + 1], m.scale[:, :], None, ALU.mult))
            dve.tensor_copy(fold[0:C, C:C + 1], m.shift[:, :]).then_inc(S("fold_ready"), 1)
            step(dve.tensor_scalar(pooled[0:C, :], m.cells[:, :], 1.0 / CELL, None, ALU.mult))
            step(dve.tensor_scalar(pooled[0:C, :], pooled[0:C, :], m.scale[0:C, :], m.shift[:, :], ALU.mult, ALU.add))
            step(dve.memset(pooled[C:C + 1, :], 1.0))
            step(dve.tensor_reduce(pooled_win, pooled.rearrange("p (w t) -> p w t", w=NWIN), AX.X, ALU.add))
            dve.tensor_scalar(pooled_win, pooled_win, 1.0 / (KVW * KVW), None, ALU.mult).then_inc(S("pooled_ready"), 1)
            dve.wait_ge(S("raw_turned"), 1)
            dve.tensor_copy(turned[:, 0:192], B[0][0:C + 1, 0:192])
            step(dve.tensor_copy(turned[0:C, 192:256 + TAPS], B[0][0:C, 192:256 + TAPS]))
            dve.tensor_tensor(spread.rearrange("p (t o) -> p t o", t=TAPS), woT.unsqueeze(1).broadcast_to([C, TAPS, C]),
                              dwT.unsqueeze(2).broadcast_to([C, TAPS, C]), ALU.mult).then_inc(S("turned_ready"), 1)
            dve.wait_ge(S("tokens_made"), 1)
            dve.tensor_copy(kv, B[1][:, 0:128])
            dve.tensor_copy(q_win, B[2][0:C, 0:NWIN]).then_inc(S("q_win_ready"), 1)
            dve.wait_ge(S("taps_made"), 1)
            dve.tensor_copy(taps[:, 0:512], B[3][0:C + 1, :])
            step(dve.tensor_copy(taps[:, 512:TAPS * C], B[4][0:C + 1, 0:C]))
            dve.sem_inc(S("taps_ready"), 1)
            dve.wait_ge(S("window_made"), 1)
            step(dve.tensor_scalar(logits, B[5][0:NWIN, 0:NWIN], float(C) ** -0.5, None, ALU.mult))
            of_j = logits.unsqueeze(2).broadcast_to([NWIN, NWIN, NWIN])
            of_k = logits.unsqueeze(1).broadcast_to([NWIN, NWIN, NWIN])
            step(dve.tensor_tensor(above, of_k, of_j, ALU.is_gt))
            step(dve.tensor_tensor(same, of_k, of_j, ALU.is_equal))
            step(dve.tensor_tensor(same, same, m.k("earlier", NWIN).rearrange("p (j k) -> p j k", k=NWIN), ALU.mult))
            step(dve.tensor_tensor(above, above, same, ALU.add))
            step(dve.tensor_reduce(rank, above, AX.X, ALU.add))
            dve.tensor_scalar(chosen, rank, TOPW - 0.5, None, ALU.is_lt).then_inc(S("window_ready"), 1)
            dve.wait_ge(S("window_made"), 2)
            dve.tensor_copy(chosen_t, B[5][0:NWIN, 16:16 + NWIN]).then_inc(S("window_ready"), 1)
            dve.wait_ge(S("window_made"), 3)
            step(dve.tensor_copy(token_mask, B[6][:, 0:NWIN]))
            dve.tensor_tensor(by_window(k_masked), kv[:, 0:C].unsqueeze(1).broadcast_to([128, NWIN, C]),
                              token_mask.unsqueeze(2).broadcast_to([128, NWIN, C]), ALU.mult).then_inc(S("window_ready"), 1)
            dve.wait_ge(S("window_made"), 4)
            dve.scalar_tensor_tensor(out=by_window(mT), in0=by_window(B[7][0:C, :]), scalar=float(C) ** -0.5,
                                     in1=m.k("headmask", C).unsqueeze(1).broadcast_to([C, NWIN, C]),
                                     op0=ALU.mult, op1=ALU.mult).then_inc(S("window_ready"), 1)
            dve.wait_ge(S("window_made"), 5)
            dve.tensor_copy(m_wo, B[0][0:C, :]).then_inc(S("window_ready"), 1)
            dve.wait_ge(S("window_made"), 6)
            dve.tensor_tensor(by_window(centre), by_window(B[1][0:C + 1, :]),
                              taps[:, 4 * C:5 * C].unsqueeze(1).broadcast_to([C + 1, NWIN, C]), ALU.add).then_inc(S("window_ready"), 1)
            dve.wait_ge(S("folded_made"), 1)
            dve.tensor_tensor(by_window(centre_folded[0:C, :]), by_window(B[2][0:C, :]),
                              ident64.unsqueeze(1).broadcast_to([C, NWIN, C]), ALU.add)
            dve.tensor_copy(centre_folded[C:C + 1, :], B[2][C:C + 1, :])
            dve.tensor_copy(folded[:, 0:512], B[3][0:C + 1, :])
            dve.tensor_copy(folded[:, 512:TAPS * C], B[4][0:C + 1, 0:C])
            step(dve.tensor_scalar(const_out, B[5][0:C, 32:33], wo_b, None, ALU.add))
            dve.sem_inc(S("weights_ready"), 1)
            row = folded[C:C + 1, :]
            for e in range(2):
                last = dve.tensor_reduce(col_rows[:, :, e, :], row.rearrange("p (y x o) -> p x o y", y=3, x=3), AX.X, ALU.add)
                dve.tensor_copy(edge_rows[:, e, :, e, :], row.rearrange("p (y x o) -> p y x o", y=3, x=3)[:, 2 * e, :, :])
            step(last)
            step(dve.tensor_reduce(bias_sum, col_rows[:, :, 0, :].rearrange("p x o -> p o x"), AX.X, ALU.add))
            step(dve.tensor_tensor(bias_sum, bias_sum, tap(1, 1, C, C + 1), ALU.subtract))
            for e in range(2):
                last = dve.tensor_tensor(bias_rows[:, :, e, :], by_window(centre_folded[C:C + 1, :]),
                                         bias_sum.unsqueeze(1).broadcast_to([1, NWIN, C]), ALU.add)
            last.then_inc(S("bias_rows_ready"), 1)
            dve.wait_ge(S("bias_turned"), 1)
            dve.tensor_scalar(bias[0:C, :], B[6][0:C, 0:NWIN], const_out, None, ALU.add)
            step(dve.tensor_scalar(bias[C:128, :], B[6][C:128, 0:NWIN], const_out, None, ALU.add))
            dve.sem_inc(S("bias_ready"), 1)
            for g in range(BANKS):
                dve.wait_ge(S("conv_made"), g + 1)
                dve.tensor_scalar(out_rows(g, 1), in_pairs(B[g % 8][C:128, :]), bias[C:128, g // 2:g // 2 + 1], None,
                                  ALU.add).then_inc(S("odd_ready"), 1)
                dve.wait_ge(S("odd_ready"), g + 1)
                dve.wait_ge(S("even_ready"), g + 1)
                for half in range(2):
                    at = 2 * g + half
                    dve.bn_stats(m.stats[:, 6 * at:6 * at + 6], m.flat[0:C, at * CH:(at + 1) * CH])

        @block.gpsimd
        def _(pool):
            step = m.chain(pool, "pool")
            for part in (outer, middle):
                step(pool.memset(part[0][0:C, :, 1, :], 0.0))
                step(pool.memset(part[1][C:128, :, 0, :], 0.0))
            step(pool.memset(edge_rows[:, 0, :, 1, :], 0.0))
            step(pool.memset(edge_rows[:, 1, :, 0, :], 0.0))
            pool.wait_ge(S("weights_ready"), 1)
            for pair, dy in ((0, 0), (1, 2)):
                step(pool.tensor_copy(middle[pair][0:C, :, 0, :], tap(dy, 1).unsqueeze(1).broadcast_to([C, NWIN, C])))
                step(pool.tensor_copy(middle[pair][C:128, :, 1, :], tap(dy, 1).unsqueeze(1).broadcast_to([C, NWIN, C])))
            step(pool.tensor_copy(middle[0][C:128, :, 0, :], by_window(centre_folded[0:C, :])))
            pool.tensor_copy(middle[1][0:C, :, 1, :], by_window(centre_folded[0:C, :])).then_inc(S("middle_ready"), 1)

        @block.scalar
        def _(act):
            quarter = L // 4
            for n in range(4):
                last = act.activation(m.img3[C:128, n * quarter:(n + 1) * quarter:2, :],
                                      m.img3[0:C, n * quarter + 1:(n + 1) * quarter + 1:2, :], ACT.Copy)
            last.then_inc(S("rows_paired"), 1)
            act.wait_ge(S("weights_ready"), 1)
            for dx in (0, 2):
                for pair, dy in ((0, 0), (1, 2)):
                    act.activation(outer[pair][0:C, dx // 2, 0, :], tap(dy, dx), ACT.Copy)
                    act.activation(outer[pair][C:128, dx // 2, 1, :], tap(dy, dx), ACT.Copy)
                act.activation(outer[0][C:128, dx // 2, 0, :], tap(1, dx), ACT.Copy)
                last = act.activation(outer[1][0:C, dx // 2, 1, :], tap(1, dx), ACT.Copy)
            last.then_inc(S("outer_ready"), 1)
            act.wait_ge(S("bias_ready"), 1)
            for g in range(BANKS):
                act.wait_ge(S("conv_made"), g + 1)
                act.activation(out_rows(g, 0), in_pairs(B[g % 8][0:C, :]), ACT.Identity,
                               bias=bias[0:C, g // 2:g // 2 + 1]).then_inc(S("even_ready"), 1)

        @block.tensor
        def _(pe):
            pe.wait_ge(S("loaded"), 16 * len(loads))
            pe.transpose(B[0][0:C + 1, 0:128], kv_raw, ident)
            pe.transpose(B[0][0:C + 1, 128:192], q_raw, ident64)
            pe.transpose(B[0][0:C, 192:256], wo_raw, ident64)
            pe.transpose(B[0][0:C, 256:256 + TAPS], dw_raw, ident[0:TAPS, 0:TAPS]).then_inc(S("raw_turned"), 1)
            pe.wait_ge(S("turned_ready"), 1)
            pe.wait_ge(S("pooled_ready"), 1)
            pe.matmul(B[1][:, 0:128], pooled, kvT, start=True, stop=True)
            pe.matmul(B[2][0:C, 0:NWIN], qT, pooled_win, start=True, stop=True).then_inc(S("tokens_made"), 1)
            pe.matmul(B[3][0:C + 1, :], v_raw, spread[:, 0:512], start=True, stop=True)
            pe.matmul(B[4][0:C + 1, 0:C], v_raw, spread[:, 512:TAPS * C], start=True, stop=True).then_inc(S("taps_made"), 1)
            pe.wait_ge(S("q_win_ready"), 1)
            pe.matmul(B[5][0:NWIN, 0:NWIN], q_win, q_win, start=True, stop=True).then_inc(S("window_made"), 1)
            pe.wait_ge(S("window_ready"), 1)
            pe.transpose(B[5][0:NWIN, 16:16 + NWIN], chosen, ident[0:NWIN, 0:NWIN]).then_inc(S("window_made"), 1)
            pe.wait_ge(S("window_ready"), 2)
            pe.matmul(B[6][:, 0:NWIN], m.k("expand", NWIN), chosen_t, start=True, stop=True).then_inc(S("window_made"), 1)
            pe.wait_ge(S("window_ready"), 3)
            pe.matmul(B[7][0:C, :], kv[:, C:128], k_masked, start=True, stop=True).then_inc(S("window_made"), 1)
            pe.wait_ge(S("window_ready"), 4)
            for w in range(NWIN):
                last = pe.matmul(B[0][0:C, w * C:(w + 1) * C], mT[:, w * C:(w + 1) * C], woT, start=True, stop=True)
            last.then_inc(S("window_made"), 1)
            pe.wait_ge(S("window_ready"), 5)
            pe.matmul(B[1][0:C + 1, :], q_raw, m_wo, start=True, stop=True).then_inc(S("window_made"), 1)
            pe.wait_ge(S("window_ready"), 6)
            pe.wait_ge(S("taps_ready"), 1)
            pe.wait_ge(S("fold_ready"), 1)
            pe.matmul(B[2][0:C + 1, :], fold, centre, start=True, stop=True)
            pe.matmul(B[3][0:C + 1, :], fold, taps[:, 0:512], start=True, stop=True)
            pe.matmul(B[4][0:C + 1, 0:C], fold, taps[:, 512:TAPS * C], start=True, stop=True)
            pe.matmul(B[5][0:C, 32:33], woT, dw_b, start=True, stop=True).then_inc(S("folded_made"), 1)
            pe.wait_ge(S("weights_ready"), 1)
            pe.wait_ge(S("bias_rows_ready"), 1)
            for w in range(NWIN):
                last = pe.matmul(B[6][:, w:w + 1], bias_rows[:, w, :, :], m.scale[C:C + 1, :], start=True, stop=True)
            last.then_inc(S("bias_turned"), 1)
            pe.wait_ge(S("rows_paired"), 1)
            pe.wait_ge(S("outer_ready"), 1)
            pe.wait_ge(S("middle_ready"), 1)
            minus = m.const[C:C + 1, CONSTS["minus"]]
            for g in range(BANKS):
                if g == 6:
                    pe.wait_ge(S("bias_ready"), 1)
                if g >= 8:
                    pe.wait_ge(S("even_ready"), g - 7)
                    pe.wait_ge(S("odd_ready"), g - 7)
                for n, (pair, dx) in enumerate((p, dx) for p in range(2) for dx in range(3)):
                    weights = middle[pair][:, g // 2, :, :] if dx == 1 else outer[pair][:, dx // 2, :, :]
                    first = 8 * g + 2 * pair
                    pe.matmul(B[g % 8][:, :], weights, m.img3[:, first:first + 7:2, dx:dx + L],
                              start=(n == 0), stop=False, skip_group_check=True)
                for dx, column in ((0, 0), (2, L - 1)):
                    last = pe.matmul(B[g % 8][:, column:column + 3 * L + 1:L], col_rows[:, dx, :, :], minus[:, 1:5],
                                     start=False, stop=True, skip_group_check=True)
                if g in (0, BANKS - 1):
                    e = g // (BANKS - 1)
                    for dx in range(3):
                        last = pe.matmul(B[g % 8][:, e * 3 * L:(e * 3 + 1) * L], edge_rows[:, e, dx, :, :],
                                         minus[:, dx:dx + L], start=False, stop=True, skip_group_check=True)
                last.then_inc(S("conv_made"), 1)


def layer2(nc, m):
    ident = m.k("ident", 128)
    m.open_arena()
    m.colsum = m.take(ROWS * C)
    x_in = m.take(CH, C)
    vt = [m.take(ROWS * 256).rearrange("p (n x) -> p n x", n=ROWS) for _ in range(2)]
    yx = [m.take(2 * ROWS * C) for _ in range(2)]
    xs = m.take(ROWS * C)
    xsT = m.take(CH, C)
    cor = m.take(CH)
    rem = m.take(CH)
    a1 = [m.take(CH) for _ in range(2)]
    a2, a3, a4 = (m.take(CH) for _ in range(3))
    zs = [m.take(ROWS * C) for _ in range(2)]
    x3 = m.take(ROWS * C)
    st = m.take(6 * ROWS)
    mv = m.take(2 * ROWS).rearrange("p (r s) -> p r s", s=2)
    std, rstd, deg, dsq, dinv = (m.take(ROWS) for _ in range(5))
    top = m.take(8 * ROWS)
    S = lambda name: m.sem(f"l2_{name}")
    names = ("a2_made v1_made y_turned a3_made a4_made v2_made xs_turned z8_made cor_made horner_made m_turned b_turned "
             "x3_turned y_ready a2_ready yx_ready a3_ready v2_ready xsT_ready z8_ready z_ready cor_ready std_ready "
             "dsq_ready a_ready x3T_ready v1_ready a4_ready stats_ready measured rstd_ready xs_ready topk_step rem_ready "
             "deg_ready dinv_ready b_ready x3_ready x_staged diag_added x3_kept col_added deg_summed std_eased").split()
    (a2_made, v1_made, y_turned, a3_made, a4_made, v2_made, xs_turned, z8_made, cor_made, horner_made, m_turned, b_turned,
     x3_turned, y_ready, a2_ready, yx_ready, a3_ready, v2_ready, xsT_ready, z8_ready, z_ready, cor_ready, std_ready,
     dsq_ready, a_ready, x3T_ready, v1_ready, a4_ready, stats_ready, measured, rstd_ready, xs_ready, topk_step, rem_ready,
     deg_ready, dinv_ready, b_ready, x3_ready, x_staged, diag_added, x3_kept, col_added, deg_summed, std_eased) = map(S, names)
    B = m.bank
    PAIRS = 2
    Z_COPIES = (GIANTS - 1) * PAIRS

    def over_steps(eng, emit):
        for s in range(4):
            emit(s, s % 2)
        with eng.Fori(0, (GROUPS - 6) // 2, 1) as it:
            for b in range(2):
                emit(it * 2 + (4 + b), b)
        for s in range(GROUPS - 2, GROUPS + 1):
            emit(s, s % 2)

    def live(s, lo, hi):
        return not isinstance(s, int) or lo <= s < hi

    def quarters(t):
        return t.rearrange("p (n x) -> p n x", n=ROWS)

    def horner_count(q, g, pair):
        return q * (GIANTS * PAIRS) + (PAIRS * (GIANTS - 1 - g) + pair + 1)

    def z_count(q, g, pair):
        return q * Z_COPIES + (PAIRS * (GIANTS - 1 - g) + pair + 1)

    with nc.Block() as block:

        @block.gpsimd
        def _(pool):
            step = m.chain(pool, "pool")
            step(pool.memset(m.colsum, 0.0))
            pool.tensor_copy(x_in, m.flat[0:C, 0:CH]).then_inc(x_staged, 1)

            def emit(s, b):
                if live(s, 0, GROUPS):
                    m.need(pool, rem_ready, s + 1)
                    pool.tensor_tensor(quarters(rem), quarters(rem), ident.unsqueeze(1).broadcast_to([128, ROWS, 128]),
                                       ALU.add).then_inc(diag_added, 1)
                if live(s, 0, GROUPS - 1):
                    m.need(pool, y_turned, s + 1)
                    pool.tensor_copy(x_in, m.flat[0:C, ds((s + 1) * CH, CH)]).then_inc(x_staged, 1)
                if live(s, 1, GROUPS + 1):
                    m.need(pool, x3_ready, s)
                    pool.tensor_copy(m.nat[:, ds((s - 1) * ROWS * C, ROWS * C)], x3).then_inc(x3_kept, 1)
                    m.need(pool, col_added, s - 1)
                    pool.tensor_tensor(m.colsum, m.colsum, x3, ALU.add).then_inc(col_added, 1)
            over_steps(pool, emit)

        @block.scalar
        def _(act):
            def emit(s, b):
                p, q = live(s, 0, GROUPS), live(s, 1, GROUPS + 1)
                o = 1 - b
                if p:
                    act.activation(vt[b][0:C, :, 0:L], quarters(m.flat[0:C, ds(s * CH, CH)]), ACT.Identity,
                                   scale=m.scale[0:C, :], bias=m.shift[:, :]).then_inc(y_ready, 1)
                if q:
                    m.need(act, a2_made, s)
                    act.activation(a2, B[0][:, :], ACT.Copy).then_inc(a2_ready, 1)
                if p:
                    m.need(act, y_turned, s + 1)
                    m.need(act, x3_ready, s - 1)
                    act.activation(yx[b], B[2][:, :], ACT.Copy).then_inc(yx_ready, 1)
                if q:
                    m.need(act, a3_made, s)
                    act.activation(a3, B[3][:, :], ACT.Copy).then_inc(a3_ready, 1)
                    m.need(act, v2_made, s)
                    act.activation(vt[o][:, :, L:2 * L], quarters(B[1][:, :]), ACT.Copy).then_inc(v2_ready, 1)
                if p:
                    m.need(act, measured, s + 1)
                    act.activation(std, mv[:, :, 1], ACT.Sqrt, scale=C / (C - 1)).then_inc(std_ready, 1)
                    m.need(act, xs_turned, s + 1)
                    act.activation(xsT, B[2][0:C, :], ACT.Copy).then_inc(xsT_ready, 1)
                if q:
                    m.need(act, z8_made, s)
                    act.activation(zs[0], B[3][:, 0:ROWS * C], ACT.Copy).then_inc(z8_ready, 1)
                if p:
                    m.need(act, cor_made, s + 1)
                    m.need(act, b_turned, s)
                    act.activation(cor, B[0][:, :], ACT.Copy, scale=1.0 / (C - 1 + 1e-6)).then_inc(cor_ready, 1)
                if q:
                    for g in range(GIANTS - 1, 0, -1):
                        for pair in range(PAIRS):
                            m.need(act, horner_made, horner_count(s - 1, g, pair))
                            act.activation(quarters(zs[g % 2])[:, 2 * pair:2 * pair + 2, :],
                                           m.quad[:, 2 * pair:2 * pair + 2, g * C:(g + 1) * C], ACT.Copy).then_inc(z_ready, 1)
                if p:
                    m.need(act, deg_ready, s + 1)
                    act.activation(dsq, deg, ACT.Sqrt).then_inc(dsq_ready, 1)
                    m.need(act, b_turned, s + 1)
                    for n in range(ROWS):
                        last = act.activation(a1[b][:, n * L:(n + 1) * L], B[2][:, n * L:(n + 1) * L], ACT.Copy,
                                              scale=dinv[:, n:n + 1])
                    last.then_inc(a_ready, 1)
                if q:
                    m.need(act, x3_turned, s)
                    act.activation(m.inner((s - 1) * ROWS), B[3][0:C, :].rearrange("p (r c) -> p r c", c=L),
                                   ACT.Copy).then_inc(x3T_ready, 1)
            over_steps(act, emit)

        @block.vector
        def _(dve):
            def emit(s, b):
                p, q = live(s, 0, GROUPS), live(s, 1, GROUPS + 1)
                o = 1 - b
                yN = quarters(yx[b][:, 0:ROWS * C])
                if q:
                    m.need(dve, v1_made, s)
                    dve.tensor_copy(vt[o][C:128, :, 0:L], quarters(B[1][C:128, :])).then_inc(v1_ready, 1)
                if p:
                    m.need(dve, yx_ready, s + 1)
                    for n in range(ROWS):
                        last = dve.bn_stats(st[:, 6 * n:6 * n + 6], yN[:, n, :])
                    last.then_inc(stats_ready, 1)
                    m.need(dve, stats_ready, s + 1)
                    m.need(dve, xs_ready, s)
                    for n in range(ROWS):
                        last = dve.bn_aggr(mv[:, n, :], st[:, 6 * n:6 * n + 6])
                    last.then_inc(measured, 1)
                if q:
                    m.need(dve, a4_made, s)
                    dve.tensor_copy(a4, B[0][:, :]).then_inc(a4_ready, 1)
                if p:
                    m.need(dve, std_ready, s + 1)
                    dve.tensor_scalar(std, std, 1e-6, None, ALU.add).then_inc(std_eased, 1)
                    m.need(dve, std_eased, s + 1)
                    dve.reciprocal(rstd, std).then_inc(rstd_ready, 1)
                    m.need(dve, rstd_ready, s + 1)
                    m.need(dve, xs_turned, s)
                    for n in range(ROWS):
                        last = dve.tensor_scalar(xs[:, n * C:(n + 1) * C], yN[:, n, :], mv[:, n, 0:1], rstd[:, n:n + 1],
                                                 ALU.subtract, ALU.mult)
                    last.then_inc(xs_ready, 1)
                    m.need(dve, cor_ready, s + 1)
                    for n in range(ROWS):
                        dve.max(top[:, 8 * n:8 * n + 8], cor[:, n * L:(n + 1) * L]).then_inc(topk_step, 1)
                    m.need(dve, m_turned, s)
                    for n in range(ROWS):
                        m.need(dve, topk_step, s * (4 * ROWS + 1) + (n + 1))
                        dve.match_replace(rem[:, n * L:(n + 1) * L], top[:, 8 * n:8 * n + 8], cor[:, n * L:(n + 1) * L],
                                          -BIG).then_inc(topk_step, 1)
                    for n in range(ROWS):
                        m.need(dve, topk_step, s * (4 * ROWS + 1) + (ROWS + n + 1))
                        dve.max(top[:, 8 * n:8 * n + 8], rem[:, n * L:(n + 1) * L]).then_inc(topk_step, 1)
                    m.need(dve, topk_step, s * (4 * ROWS + 1) + 3 * ROWS)
                    dve.memset(top.rearrange("p (n k) -> p n k", k=8)[:, :, 1:8], -BIG).then_inc(topk_step, 1)
                    m.need(dve, topk_step, s * (4 * ROWS + 1) + (3 * ROWS + 1))
                    for n in range(ROWS):
                        dve.match_replace(rem[:, n * L:(n + 1) * L], top[:, 8 * n:8 * n + 8], rem[:, n * L:(n + 1) * L],
                                          -BIG).then_inc(topk_step, 1)
                    m.need(dve, topk_step, s * (4 * ROWS + 1) + (4 * ROWS + 1))
                    dve.scalar_tensor_tensor(out=rem, in0=rem, scalar=-BIG, in1=cor, op0=ALU.is_equal, op1=ALU.mult).then_inc(rem_ready, 1)
                    m.need(dve, m_turned, s + 1)
                    m.need(dve, diag_added, s + 1)
                    for n in range(ROWS):
                        last = dve.tensor_tensor_reduce(cor[:, n * L:(n + 1) * L], rem[:, n * L:(n + 1) * L],
                                                        B[1][:, n * L:(n + 1) * L], 1.0, 0.0, ALU.add, ALU.add, deg[:, n:n + 1])
                    last.then_inc(deg_summed, 1)
                    m.need(dve, deg_summed, s + 1)
                    dve.tensor_scalar(deg, deg, 0.5, 1e-6, ALU.mult, ALU.max).then_inc(deg_ready, 1)
                    m.need(dve, dsq_ready, s + 1)
                    m.need(dve, a_ready, s)
                    dve.reciprocal(dinv, dsq).then_inc(dinv_ready, 1)
                    m.need(dve, dinv_ready, s + 1)
                    for n in range(ROWS):
                        last = dve.tensor_scalar(cor[:, n * L:(n + 1) * L], cor[:, n * L:(n + 1) * L], dinv[:, n:n + 1], 0.5,
                                                 ALU.mult, ALU.mult)
                    last.then_inc(b_ready, 1)
                if q:
                    m.need(dve, horner_made, s * (GIANTS * PAIRS))
                    m.need(dve, x3_turned, s - 1)
                    m.need(dve, col_added, s - 1)
                    dve.scalar_tensor_tensor(out=quarters(x3), in0=m.quad[:, :, 0:C], scalar=0.0,
                                             in1=quarters(yx[o][:, ROWS * C:2 * ROWS * C]), op0=ALU.max, op1=ALU.add).then_inc(x3_ready, 1)
                    m.need(dve, x3T_ready, s)
                    dve.bn_stats(m.stats[:, ds((s - 1) * 6, 6)], m.inner((s - 1) * ROWS))
                    dve.tensor_reduce(m.cells[:, ds((s - 1) * ROWS, ROWS)], m.inner((s - 1) * ROWS), AX.X, ALU.add)
            over_steps(dve, emit)

        @block.tensor
        def _(pe):
            def col(n, w=L):
                return slice(n * w, (n + 1) * w)

            def emit(s, b):
                p, q = live(s, 0, GROUPS), live(s, 1, GROUPS + 1)
                o = 1 - b
                if q:
                    m.need(pe, a_ready, s)
                    m.need(pe, cor_ready, s)
                    for n in range(ROWS):
                        last = pe.matmul(B[0][:, col(n)], a1[o][:, col(n)], a1[o][:, col(n)], start=True, stop=True)
                    last.then_inc(a2_made, 1)
                    m.need(pe, b_ready, s)
                    for n in range(ROWS):
                        last = pe.matmul(B[1][C:128, col(n)], yx[o][:, col(n, C)], a1[o][:, col(n)], start=True, stop=True)
                    last.then_inc(v1_made, 1)
                if p:
                    m.need(pe, y_ready, s + 1)
                    m.need(pe, x_staged, s + 1)
                    m.need(pe, a_ready, s)
                    for n in range(ROWS):
                        pe.transpose(B[2][:, col(n, C)], vt[b][0:C, n, 0:L], ident[0:C, 0:C])
                    for n in range(ROWS):
                        last = pe.transpose(B[2][:, col(ROWS + n, C)], x_in[:, col(n)], ident[0:C, 0:C])
                    last.then_inc(y_turned, 1)
                if q:
                    m.need(pe, a2_ready, s)
                    m.need(pe, x3T_ready, s - 1)
                    for n in range(ROWS):
                        last = pe.matmul(B[3][:, col(n)], a2[:, col(n)], a1[o][:, col(n)], start=True, stop=True)
                    last.then_inc(a3_made, 1)
                    for n in range(ROWS):
                        last = pe.matmul(B[0][:, col(n)], a2[:, col(n)], a2[:, col(n)], start=True, stop=True)
                    last.then_inc(a4_made, 1)
                    m.need(pe, v1_ready, s)
                    for n in range(ROWS):
                        pe.matmul(B[1][0:C, col(n)], yx[o][:, col(n, C)], a2[:, col(n)], start=True, stop=True)
                    m.need(pe, a3_ready, s)
                    for n in range(ROWS):
                        last = pe.matmul(B[1][C:128, col(n)], yx[o][:, col(n, C)], a3[:, col(n)], start=True, stop=True)
                    last.then_inc(v2_made, 1)
                    m.need(pe, x3_ready, s - 1)
                    for n in range(ROWS):
                        pe.matmul(m.quad[:, n, :], vt[o][:, n, 0:L], m.theta[:, 0, :], start=True, stop=False, skip_group_check=True)
                if p:
                    m.need(pe, xs_ready, s + 1)
                    m.need(pe, yx_ready, s + 1)
                    for n in range(ROWS):
                        last = pe.transpose(B[2][0:C, col(n)], xs[:, col(n, C)], ident)
                    last.then_inc(xs_turned, 1)
                if q:
                    for n in range(ROWS):
                        last = pe.matmul(B[3][:, col(n, C)], vt[o][0:C, n, 0:L], m.theta_top[:, :], start=True, stop=True)
                    last.then_inc(z8_made, 1)
                    m.need(pe, v2_ready, s)
                    for n in range(ROWS):
                        pe.matmul(m.quad[:, n, :], vt[o][:, n, L:2 * L], m.theta[:, 1, :], start=False, stop=False, skip_group_check=True)
                if p:
                    m.need(pe, xsT_ready, s + 1)
                    m.need(pe, a4_ready, s)
                    for n in range(ROWS):
                        last = pe.matmul(B[0][:, col(n)], xsT[:, col(n)], xsT[:, col(n)], start=True, stop=True)
                    last.then_inc(cor_made, 1)
                if q:
                    m.need(pe, z8_ready, s)
                for g in range(GIANTS - 1, -1, -1):
                    if q:
                        for pair in range(PAIRS):
                            if g < GIANTS - 1:
                                m.need(pe, z_ready, z_count(s - 1, g + 1, pair))
                            elif pair == 0:
                                m.need(pe, a4_ready, s)
                            for n in (2 * pair, 2 * pair + 1):
                                last = pe.matmul(m.quad[:, n, g * C:(g + 1) * C], a4[:, col(n)], zs[(g + 1) % 2][:, col(n, C)],
                                                 start=False, stop=(g == 0), skip_group_check=True)
                            last.then_inc(horner_made, 1)
                    if g == 1 and p:
                        m.need(pe, rem_ready, s + 1)
                        m.need(pe, diag_added, s + 1)
                        m.need(pe, v2_ready, s)
                        for n in range(ROWS):
                            last = pe.transpose(B[1][:, col(n)], rem[:, col(n)], ident)
                        last.then_inc(m_turned, 1)
                if p:
                    m.need(pe, b_ready, s + 1)
                    m.need(pe, xsT_ready, s + 1)
                    for n in range(ROWS):
                        last = pe.transpose(B[2][:, col(n)], cor[:, col(n)], ident)
                    last.then_inc(b_turned, 1)
                if q:
                    m.need(pe, x3_ready, s)
                    m.need(pe, z8_ready, s)
                    for n in range(ROWS):
                        last = pe.transpose(B[3][0:C, col(n)], x3[:, col(n, C)], ident)
                    last.then_inc(x3_turned, 1)
            over_steps(pe, emit)


def layer3(nc, m, args, out):
    ident = m.k("ident", 128)
    ident64 = ident[0:C, 0:C]
    KINDS = 15
    COLS = 8
    STEPS3 = L // COLS
    m.arena_at = ROWS * C
    ws = m.take(KINDS * C, C)
    wm = m.take(C, C)
    bm = m.take(C, 1)
    wsT = m.take(KINDS * C, C)
    w = m.take(KINDS * C, C)
    spread_scale = m.take(C, C)
    both = m.take(C)
    rows_x, cols_x, diag_raw, diag_x = (m.take(L, C) for _ in range(4))
    col_mean = m.take(C)
    mean_diag, mean_all, mean_diag2 = (m.take(1, C) for _ in range(3))
    of_row, of_col = m.take(C), m.take(C)
    diag_ret, diag_out = m.take(C), m.take(C)
    xx = [m.take(COLS * L) for _ in range(2)]
    before = [m.take(COLS * C) for _ in range(2)]
    ready = [m.take(COLS * C) for _ in range(2)]
    s_flat = m.nat[0:1, :]
    S = lambda name: m.sem(f"l3_{name}")
    B = m.bank
    kind = lambda k: w[:, (k - 1) * C:k * C]
    by_col = lambda t: t.rearrange("p (j x) -> p j x", j=COLS)
    with nc.Block() as block:

        @block.sync
        def _(sp):
            sp.dma_start(ws.rearrange("d (k e) -> d k e", k=KINDS), args["L3_conv_Ws"].rearrange("k d e -> d k e")).then_inc(S("loaded"), 16)
            sp.dma_start(wm, args["L3_conv_Wm"]).then_inc(S("loaded"), 16)
            sp.dma_start(bm, args["L3_conv_bm"].rearrange("(a c) -> a c", a=1)).then_inc(S("loaded"), 16)
            sp.wait_ge(S("of_col"), 1)
            sp.dma_start(s_flat.rearrange("a (j c) -> a j c", c=C), of_col).then_inc(S("flattened"), 16)
            sp.wait_ge(S("flattened"), 16)

        @block.scalar
        def _(act):
            act.wait_ge(S("ws_turned"), 2)
            act.activation(wsT[:, 512:KINDS * C], B[1][0:C, 0:KINDS * C - 512], ACT.Copy).then_inc(S("wsT_upper"), 1)
            act.wait_ge(S("w_made"), 2)
            act.activation(w[:, 512:KINDS * C], B[3][0:C, 0:KINDS * C - 512], ACT.Copy).then_inc(S("w_upper"), 1)

        @block.vector
        def _(dve):
            step = m.chain(dve, "dve")
            dve.tensor_reduce(col_mean, m.colsum.rearrange("p (r c) -> p c r", r=ROWS), AX.X, ALU.add).then_inc(S("col_summed"), 1)
            step(dve.tensor_scalar(rows_x, m.cells[:, :], 1.0 / L, None, ALU.mult))
            step(dve.tensor_scalar(rows_x, rows_x, m.scale[0:C, :], m.shift[:, :], ALU.mult, ALU.add))
            step(dve.tensor_copy(diag_raw, m.img[0:C, PW + 1:L * (PW + 1) + 1:PW + 1]))
            step(dve.tensor_scalar(diag_x, diag_raw, m.scale[0:C, :], m.shift[:, :], ALU.mult, ALU.add))
            step(dve.tensor_reduce(mean_diag, diag_x, AX.X, ALU.add))
            step(dve.tensor_reduce(mean_all, rows_x, AX.X, ALU.add))
            step(dve.tensor_scalar(mean_diag2, mean_diag, 2.0 / L, None, ALU.mult))
            step(dve.tensor_scalar(mean_diag, mean_diag, 1.0 / L, None, ALU.mult))
            step(dve.tensor_scalar(mean_all, mean_all, 1.0 / L, None, ALU.mult))
            step(dve.tensor_scalar(spread_scale, ident64, m.scale[0:C, :], None, ALU.mult))
            dve.wait_ge(S("cols_turned"), 1)
            step(dve.tensor_scalar(cols_x, B[4][0:C, 0:L], 1.0 / L, None, ALU.mult))
            dve.tensor_scalar(cols_x, cols_x, m.scale[0:C, :], m.shift[:, :], ALU.mult, ALU.add).then_inc(S("means_ready"), 1)
            dve.wait_ge(S("ws_turned"), 1)
            dve.tensor_copy(wsT[:, 0:512], B[0][0:C, :]).then_inc(S("wsT_lower"), 1)
            dve.wait_ge(S("w_made"), 1)
            dve.tensor_copy(w[:, 0:512], B[2][0:C, :]).then_inc(S("w_lower"), 1)
            dve.wait_ge(S("of_col_made"), 1)
            dve.tensor_copy(of_col, B[5][:, 0:C]).then_inc(S("of_col"), 1)
            dve.wait_ge(S("terms_made"), 1)
            dve.tensor_copy(of_row, B[6][:, 0:C])
            dve.tensor_copy(both, B[7][:, 0:C])
            step(dve.tensor_copy(diag_ret, B[0][:, 0:C]))
            dve.scalar_tensor_tensor(out=diag_out, in0=diag_ret, scalar=0.0, in1=B[1][:, 0:C], op0=ALU.max, op1=ALU.add).then_inc(S("diag_ready"), 1)

        @block.tensor
        def _(pe):
            pe.wait_ge(S("col_summed"), 1)
            pe.transpose(B[4][0:C, 0:L], col_mean, ident).then_inc(S("cols_turned"), 1)
            pe.wait_ge(S("loaded"), 16 * 3)
            for half, ks in enumerate((range(0, 8), range(8, KINDS))):
                for k in ks:
                    at = (k - 8 * half) * C
                    last = pe.transpose(B[half][0:C, at:at + C], ws[:, k * C:(k + 1) * C], ident64)
                last.then_inc(S("ws_turned"), 1)
            for half, ks in enumerate((range(0, 8), range(8, KINDS))):
                pe.wait_ge(S("wsT_upper" if half else "wsT_lower"), 1)
                for k in ks:
                    at = (k - 8 * half) * C
                    last = pe.matmul(B[2 + half][0:C, at:at + C], wsT[:, k * C:(k + 1) * C], wm, start=True, stop=True)
                last.then_inc(S("w_made"), 1)

            def total(bank, terms):
                for n, (vector, weights) in enumerate(terms):
                    last = pe.matmul(bank[:, 0:C], vector, weights, start=(n == 0), stop=(n == len(terms) - 1))
                return last

            everywhere = lambda t: t.to_broadcast([C, L])
            pe.wait_ge(S("means_ready"), 1)
            pe.wait_ge(S("w_lower"), 1)
            pe.wait_ge(S("w_upper"), 1)
            total(B[5], [(rows_x, kind(7)), (cols_x, kind(9)), (diag_x, kind(13))]).then_inc(S("of_col_made"), 1)
            total(B[6], [(rows_x, kind(6)), (cols_x, kind(8)), (diag_x, kind(12)), (everywhere(mean_diag2), kind(14)),
                         (everywhere(m.shift[:, :]), kind(10)), (everywhere(m.shift[:, :]), kind(11)), (m.one[:, :], bm)])
            pe.matmul(B[7][0:C, 0:C], spread_scale, kind(10), start=True, stop=True)
            pe.matmul(B[7][C:128, 0:C], spread_scale, kind(11), start=True, stop=True)
            total(B[0], [(diag_x, kind(k)) for k in (10, 11, 12, 13, 1)] + [(rows_x, kind(k)) for k in (6, 7, 3)]
                  + [(cols_x, kind(k)) for k in (8, 9, 4)]
                  + [(everywhere(mean_diag2), kind(14)), (everywhere(mean_diag), kind(2)), (everywhere(mean_all), kind(5)),
                     (m.one[:, :], bm)])
            pe.transpose(B[1][:, 0:C], diag_raw, ident64).then_inc(S("terms_made"), 1)

    top_ready, low_ready, ret_made, added, out_ready = (
        S(n) for n in ("top_ready", "low_ready", "ret_made", "added", "out_ready"))
    sent = [S("sent_even"), S("sent_odd")]

    def over_steps(eng, emit):
        for t in range(2):
            emit(t, t, 0)
        with eng.Fori(0, (STEPS3 - 2) // 2, 1) as it:
            for b in range(2):
                emit(it * 2 + (2 + b), b, it + 1)

    with nc.Block() as block:

        @block.gpsimd
        def _(pool):
            def emit(t, b, turn):
                m.need(pool, ret_made, t - 1)
                pool.tensor_copy(by_col(xx[b][0:C, :]), m.img3[0:C, 1:L + 1, ds(t * COLS + 1, COLS)].rearrange("p i j -> p j i")).then_inc(top_ready, 1)
            over_steps(pool, emit)

        @block.scalar
        def _(act):
            def emit(t, b, turn):
                m.need(act, ret_made, t - 1)
                act.activation(by_col(xx[b][C:128, :]), m.inner(t * COLS, COLS), ACT.Copy).then_inc(low_ready, 1)
            over_steps(act, emit)

        @block.tensor
        def _(pe):
            def emit(t, b, turn):
                m.need(pe, top_ready, t + 1)
                m.need(pe, low_ready, t + 1)
                m.need(pe, out_ready, t - 1)
                pe.matmul(B[b][:, :], m.one[:, :], s_flat[:, ds(t * COLS * C, COLS * C)], start=True, stop=False, skip_group_check=True)
                for j in range(COLS):
                    pe.matmul(B[b][:, j * C:(j + 1) * C], xx[b][:, j * L:(j + 1) * L], both, start=False, stop=True, skip_group_check=True)
                for j in range(COLS):
                    last = pe.transpose(B[2 + b][:, j * C:(j + 1) * C], xx[b][0:C, j * L:(j + 1) * L], ident64)
                last.then_inc(ret_made, 1)
            over_steps(pe, emit)

        @block.vector
        def _(dve):
            def emit(t, b, turn):
                m.need(dve, ret_made, t + 1)
                dve.tensor_tensor(by_col(before[b]), by_col(B[b][:, :]), of_row.unsqueeze(1).broadcast_to([128, COLS, C]),
                                  ALU.add).then_inc(added, 1)
                m.need(dve, added, t + 1)
                m.need(dve, sent[b], turn * 16)
                dve.scalar_tensor_tensor(out=ready[b], in0=before[b], scalar=0.0, in1=B[2 + b][:, :],
                                         op0=ALU.max, op1=ALU.add).then_inc(out_ready, 1)
            over_steps(dve, emit)

        @block.sync
        def _(sp):
            def emit(t, b, turn):
                m.need(sp, out_ready, t + 1)
                sp.dma_start(out.rearrange("b i j c -> (b i) j c")[:, ds(t * COLS, COLS), :], by_col(ready[b])).then_inc(sent[b], 16)
            over_steps(sp, emit)
            for b in range(2):
                sp.wait_ge(sent[b], 16 * STEPS3 // 2)
            sp.dma_start(out.rearrange("b i j c -> (b i j) c")[0:L * L:L + 1, :], diag_out).then_inc(S("diag_sent"), 16)
            sp.wait_ge(S("diag_sent"), 16)


def build(nc, args, out):
    with ExitStack() as ctx:
        m = Memory(nc, ctx)
        load_and_prepare(nc, m, args)
        m.open_arena(); m.arena_at = 9000
        group_norm(nc, m, 0)
        layer0_norm(nc, m)
        layer0_attention(nc, m, args)
        m.open_arena()
        group_norm(nc, m, 1)
        layer1(nc, m, args)
        m.open_arena()
        group_norm(nc, m, 2)
        layer2(nc, m)
        m.arena_at = ROWS * C
        group_norm(nc, m, 3)
        layer3(nc, m, args, out)


_INS = ['x', 'L0_conv_gamma', 'L0_conv_beta', 'L0_conv_Wq', 'L0_conv_Wk', 'L0_conv_Wv', 'L0_conv_Wb', 'L0_conv_Wg',
        'L0_conv_bg', 'L0_conv_Wo', 'L0_conv_bo', 'L1_conv_qkv_w', 'L1_conv_qkv_b', 'L1_conv_wo_w', 'L1_conv_wo_b',
        'L1_conv_dw_w', 'L1_conv_dw_b', 'L2_conv_theta_w', 'L2_conv_alpha_raw', 'L3_conv_Ws', 'L3_conv_Wm', 'L3_conv_bm']


def kernel(**inputs):
    import concourse.bacc as bacc
    from concourse.bass_utils import run_bass_kernel_spmd

    nc = bacc.Bacc("TRN2", target_bir_lowering=False, num_devices=1)
    arrays, args = {}, {}
    for name in _INS:
        a = np.ascontiguousarray(inputs[name])
        arrays[f"in_{name}"] = a
        args[name] = nc.dram_tensor(f"in_{name}", a.shape, mybir.dt.from_np(a.dtype), kind="ExternalInput").ap()
    arrays["in_constants"] = constants()
    args["constants"] = nc.dram_tensor("in_constants", (128, NCONST), F32, kind="ExternalInput").ap()
    out = nc.dram_tensor("out", (1, L, L, C), F32, kind="ExternalOutput").ap()
    build(nc, args, out)
    result = run_bass_kernel_spmd(nc, [arrays], core_ids=[0])
    return result.results[0]["out"]
```

```python
from contextlib import ExitStack
from math import comb

import concourse.bass as bass
import numpy as np
from concourse import mybir

F32 = mybir.dt.float32
ALU = mybir.AluOpType
ACT = mybir.ActivationFunctionType
AX = mybir.AxisListType
ds = bass.ds

L = 128
C = 64
HEADS, HD = 4, 32
ROWS = 4
GROUPS = L // ROWS
CH = ROWS * L
NWIN, KVW = 8, 4
TOPW = 4
QHEADS, QD = 8, 8
CELL = (L // NWIN // KVW) * (L // KVW)
TOPK = 8
STEPS, T_END = 8, 0.2
DEG = 4 * STEPS
H_STEP = T_END / STEPS
BABY = 4
GIANTS = DEG // BABY
BIG = 3.0e38
PW = L + 2

CONSTS = {}
_at = 0
for _name, _n in (("ident", 128), ("pair", 64), ("expand", 128), ("headmask", 64), ("earlier", 64), ("rk", DEG + 1)):
    CONSTS[_name] = slice(_at, _at + _n)
    _at += _n
NCONST = _at
CONSTS["minus"] = slice(CONSTS["pair"].start, CONSTS["pair"].start + L + 2)


def constants():
    k = np.zeros((128, NCONST), np.float32)
    k[:, CONSTS["ident"]] = np.eye(128)
    c = np.arange(C)
    k[:C, CONSTS["pair"]] = 0.5 * (c[:, None] // 2 == c[None, :] // 2)
    k[:NWIN, CONSTS["expand"]] = np.arange(NWIN)[:, None] == np.arange(128)[None, :] // (KVW * KVW)
    k[:C, CONSTS["headmask"]] = c[:, None] // QD == c[None, :] // QD
    k[:, CONSTS["earlier"]] = (np.arange(8)[None, :] < np.arange(8)[:, None]).reshape(1, 64)
    p = np.ones(1)
    for _ in range(STEPS):
        p = np.convolve(p, [1.0, 1.0, 1 / 2, 1 / 6, 1 / 24])
    for m in range(DEG + 1):
        for j in range(DEG + 1 - m):
            k[m, CONSTS["rk"].start + j] = p[m + j] * comb(m + j, j)
    k[C, CONSTS["minus"]] = -np.pad(np.ones(L), 1)
    return k


class Chain:

    def __init__(self, sem):
        self.eng, self.sem, self.n = None, sem, 0

    def __call__(self, ins):
        ins.then_inc(self.sem, 1)
        self.n += 1
        self.eng.wait_ge(self.sem, self.n)




class Memory:

    ARENA_COLS = 9088

    def __init__(self, nc, ctx):
        self.nc, self.ctx, self.sems, self.chains = nc, ctx, {}, {}

        def sb(name, shape):
            return ctx.enter_context(nc.sbuf_tensor(name, shape, F32))

        self.img = sb("img", [128, PW * PW])
        self.flat = sb("flat", [C + 1, L * L])
        self.nat = sb("nat", [L, L * C])
        self.arena = sb("arena", [128, self.ARENA_COLS])
        self.const = sb("const", [128, NCONST])
        self.w0 = sb("w0", [C + 1, 4 * 128])
        self.w0b = sb("w0b", [C + 1, HEADS])
        self.theta = sb("theta", [128, 2, 512])
        self.theta_top = sb("theta_top", [C, C])
        self.stats = sb("stats", [C, GROUPS * 6])
        self.scale = sb("scale", [C + 1, 1])
        self.shift = sb("shift", [C, 1])
        self.cells = sb("cells", [C, GROUPS * KVW])
        self.eps = sb("eps", [128, 1])
        self.bo = sb("bo", [C, 1])
        self.one = sb("one", [1, 128])
        self.bank = [ctx.enter_context(nc.psum_tensor(f"bank{i}", [128, 512], F32)) for i in range(4)]
        self.quad = ctx.enter_context(nc.psum_tensor("quad", [128, 4, 512], F32))
        self.bank += [self.quad[:, i, :] for i in range(4)]
        self.img3 = self.img[:, :].rearrange("p (r c) -> p r c", c=PW)
        self.nat3 = self.nat[:, :].rearrange("p (i c) -> p i c", c=C)
        self.arena_at = 0

    def sem(self, name):
        if name not in self.sems:
            self.sems[name] = self.ctx.enter_context(self.nc.semaphore(name))
        return self.sems[name]

    def chain(self, eng, name):
        if name not in self.chains:
            self.chains[name] = Chain(self.sem(name + "_chain"))
        self.chains[name].eng = eng
        return self.chains[name]

    def need(self, eng, sem, value):
        if isinstance(value, int):
            if value > 0:
                eng.wait_ge(sem, value)
            return
        eng.wait_ge(sem, value)
        eng.sem_inc(self.sem("passed"))

    def k(self, name, rows):
        return self.const[0:rows, CONSTS[name]]

    def inner(self, row, rows=ROWS):
        return self.img3[0:C, ds(row + 1, rows), 1:L + 1]

    def open_arena(self):
        self.arena_at = 0

    def take(self, cols, rows=128):
        assert self.arena_at + cols <= self.ARENA_COLS, "the arena is full"
        at = self.arena_at
        self.arena_at += cols
        return self.arena[0:rows, at:at + cols]


def load_and_prepare(nc, m, args):
    S = m.sem
    ident = m.k("ident", 128)
    ident64 = ident[0:C, 0:C]
    m.open_arena()
    w_raw = m.take(4 * 128, C)
    wb_raw = m.take(HEADS, C)
    fold0 = m.take(C + 1, C)
    gamma = m.take(1, C)
    bg_row = m.take(128, C + 1)
    theta_raw = m.take(C, C)
    alpha = m.take(8)
    powers = m.take(DEG + 1)
    power_col = m.take(1)
    picked = m.take(DEG + 1)
    coef = m.take(DEG + 1)
    turn = m.take(2 * C, C)
    pw = m.take((DEG + 1) * C).rearrange("p (j e) -> p j e", e=C)
    PIECES = 4
    per = L // PIECES
    vectors = [
        (w_raw[:, 0:128], args["L0_conv_Wq"]), (w_raw[:, 128:256], args["L0_conv_Wk"]),
        (w_raw[:, 256:384], args["L0_conv_Wv"]), (w_raw[:, 384:512], args["L0_conv_Wg"]),
        (wb_raw, args["L0_conv_Wb"]),
        (gamma, args["L0_conv_gamma"].rearrange("(c a) -> c a", a=1)),
        (fold0[:, C:C + 1], args["L0_conv_beta"].rearrange("(c a) -> c a", a=1)),
        (bg_row[C:C + 1, :], args["L0_conv_bg"].rearrange("(a c) -> a c", a=1)),
        (m.bo[:, :], args["L0_conv_bo"].rearrange("(c a) -> c a", a=1)),
        (theta_raw, args["L2_conv_theta_w"]),
        (alpha[:, 0:1], args["L2_conv_alpha_raw"].rearrange("(a c) -> a c", a=1).to_broadcast([128, 1])),
    ]
    weights_in, consts_in, copied, chunk_turned = S("a_weights_in"), S("a_consts_in"), S("a_copied"), S("a_chunk_turned")
    piece_in = [S(f"a_x_in{n}") for n in range(PIECES)]
    x_nat = args["x"].rearrange("b i j c -> (b j) i c")
    DOUBLINGS = [1, 2, 4, 8, 16]
    with nc.Block() as block:

        @block.sync
        def _(sp):
            sp.dma_start(m.const[:, :], args["constants"]).then_inc(consts_in, 16)
            for n in range(PIECES):
                sp.dma_start(m.nat3[:, n * per:(n + 1) * per, :], x_nat[:, n * per:(n + 1) * per, :]).then_inc(piece_in[n], 16)

        @block.gpsimd
        def _(pool):
            step = m.chain(pool, "pool")
            step(pool.memset(m.img3[0:C, 0, :], 0.0))
            step(pool.memset(m.img3[0:C, L + 1, :], 0.0))
            step(pool.memset(m.img3[C:128, L, :], 0.0))
            step(pool.memset(m.img3[0:C, 1:L + 1, 0:1], 0.0))
            step(pool.memset(m.img3[0:C, 1:L + 1, L + 1:L + 2], 0.0))
            step(pool.memset(m.flat[C:C + 1, :], 1.0))
            step(pool.memset(m.eps[:, :], 1e-5))
            step(pool.memset(m.one[:, :], 1.0))
            step(pool.memset(m.scale[C:C + 1, :], 1.0))

        @block.scalar
        def _(act):
            for dst, src in vectors:
                act.dma_start(dst, src).then_inc(weights_in, 16)
            act.wait_ge(weights_in, 16 * len(vectors))
            step = m.chain(act, "act")
            step(act.activation(alpha[:, 1:2], alpha[:, 0:1], ACT.Abs))
            step(act.activation(alpha[:, 2:3], alpha[:, 1:2], ACT.Exp, scale=-1.0))
            act.activation(alpha[:, 3:4], alpha[:, 2:3], ACT.Ln, bias=1.0).then_inc(S("a_ln"), 1)
            for q in range(GROUPS):
                act.wait_ge(chunk_turned, q + 1)
                act.activation(m.inner(ROWS * q), m.bank[q % 4][0:C, :].rearrange("p (r c) -> p r c", c=L),
                               ACT.Copy).then_inc(copied, 1)

        @block.vector
        def _(dve):
            step = m.chain(dve, "dve")
            dve.wait_ge(consts_in, 16)
            dve.wait_ge(weights_in, 16 * len(vectors))
            dve.tensor_scalar(fold0[:, 0:C], ident64, gamma, None, ALU.mult).then_inc(S("a_fold0"), 1)
            dve.wait_ge(S("a_ln"), 1)
            step(dve.tensor_scalar(alpha[:, 4:5], alpha[:, 0:1], 0.0, alpha[:, 3:4], ALU.max, ALU.add))
            step(dve.tensor_scalar(alpha[:, 5:6], alpha[:, 4:5], 2.0, None, ALU.min))
            step(dve.memset(powers[:, 0:1], 1.0))
            step(dve.tensor_scalar(powers[:, 1:2], alpha[:, 5:6], H_STEP, None, ALU.mult))
            have = 2
            while have < DEG + 1:
                n = min(have - 1, DEG + 1 - have)
                step(dve.tensor_scalar(powers[:, have:have + n], powers[:, 1:1 + n], powers[:, have - 1:have], None, ALU.mult))
                have += n
            n = DEG + 1
            step(dve.tensor_tensor(picked[0:n, :], powers[0:n, :], ident[0:n, 0:n], ALU.mult))
            dve.tensor_reduce(power_col[0:n, :], picked[0:n, :], AX.X, ALU.add).then_inc(S("a_power_col"), 1)
            step(dve.tensor_scalar(theta_raw, theta_raw, H_STEP, None, ALU.mult))
            step(dve.tensor_scalar(turn[:, C:2 * C], ident64, powers[0:C, 1:2], None, ALU.mult))
            step(dve.tensor_tensor(turn[:, 0:C], theta_raw, turn[:, C:2 * C], ALU.subtract))
            dve.tensor_copy(turn[:, C:2 * C], turn[:, 0:C]).then_inc(S("a_turn"), 1)
            dve.wait_ge(S("a_w0_made"), 1)
            step(dve.tensor_copy(m.w0[:, :], m.bank[4][0:C + 1, :]))
            dve.tensor_scalar(m.w0[:, 0:128], m.w0[:, 0:128], float(1.0 / np.sqrt(HD)), None, ALU.mult)
            dve.tensor_tensor(m.w0[C:C + 1, 384:512], m.w0[C:C + 1, 384:512], bg_row[C:C + 1, :], ALU.add)
            dve.wait_ge(S("a_w0b_made"), 1)
            dve.tensor_copy(m.w0b[:, :], m.bank[5][0:C + 1, 0:HEADS])
            dve.wait_ge(S("a_coef_made"), 1)
            dve.tensor_copy(coef, m.bank[6][:, 0:DEG + 1]).then_inc(S("a_coef"), 1)
            step(dve.tensor_copy(pw[0:C, 0, :], ident64))
            step(dve.tensor_copy(pw[C:128, 0, :], ident[C:128, C:128]))
            dve.wait_ge(S("a_first_power"), 1)
            dve.tensor_copy(pw[:, 1, :], m.bank[7][:, 0:C]).then_inc(S("a_powers"), 1)
            for i, d in enumerate(DOUBLINGS):
                if d > 1:
                    dve.wait_ge(S("a_power_turned"), i)
                    for half in range(2):
                        dve.tensor_copy(turn[:, half * C:(half + 1) * C], m.bank[7][0:C, 0:C]).then_inc(S("a_power_turn"), 1)
                for at in range(0, d, 8):
                    n = min(8, d - at)
                    dve.wait_ge(S("a_doubled"), i + 1 + (at > 0))
                    dve.tensor_copy(pw[:, d + 1 + at:d + 1 + at + n, :],
                                    m.bank[5 + (at > 0)][:, 0:n * C].rearrange("p (j e) -> p j e", e=C)).then_inc(S("a_powers"), 1)
            dve.wait_ge(S("a_powers"), 1 + len(DOUBLINGS) + 1)
            dve.wait_ge(S("a_coef"), 1)
            for j in range(DEG):
                half = slice(0, C) if j % 2 == 0 else slice(C, 128)
                g, b = divmod(j, BABY)
                dve.tensor_scalar(m.theta[half, b // 2, g * C:(g + 1) * C], pw[half, j, :], coef[half, j:j + 1], None, ALU.mult)
            dve.tensor_scalar(m.theta_top[:, :], pw[0:C, DEG, :], coef[0:C, DEG:DEG + 1], None, ALU.mult)
            for q in range(GROUPS):
                dve.wait_ge(copied, q + 1)
                dve.bn_stats(m.stats[:, 6 * q:6 * q + 6], m.inner(ROWS * q))

        @block.tensor
        def _(pe):
            pe.wait_ge(consts_in, 16)
            pe.wait_ge(S("a_fold0"), 1)
            pe.matmul(m.bank[4][0:C + 1, :], fold0, w_raw, start=True, stop=True).then_inc(S("a_w0_made"), 1)
            pe.matmul(m.bank[5][0:C + 1, 0:HEADS], fold0, wb_raw, start=True, stop=True).then_inc(S("a_w0b_made"), 1)
            pe.wait_ge(S("a_power_col"), 1)
            n = DEG + 1
            pe.matmul(m.bank[6][:, 0:n], power_col[0:n, :].to_broadcast([n, 128]), m.k("rk", n),
                      start=True, stop=True).then_inc(S("a_coef_made"), 1)
            pe.wait_ge(S("a_turn"), 1)
            pe.matmul(m.bank[7][:, 0:C], turn, ident64, start=True, stop=True).then_inc(S("a_first_power"), 1)
            pe.wait_ge(S("a_coef"), 1)
            for i, d in enumerate(DOUBLINGS):
                pe.wait_ge(S("a_powers"), i + 1)
                if d > 1:
                    pe.wait_ge(S("a_power_turn"), 2 * i)
                for at in range(0, d, 8):
                    n = min(8, d - at)
                    pe.matmul(m.bank[5 + (at > 0)][:, 0:n * C], turn, pw[0:C, 1 + at:1 + at + n, :],
                              start=True, stop=True).then_inc(S("a_doubled"), 1)
                if i + 1 < len(DOUBLINGS):
                    pe.wait_ge(S("a_powers"), i + 2)
                    pe.transpose(m.bank[7][0:C, 0:C], pw[0:C, 2 * d, :], ident64).then_inc(S("a_power_turned"), 1)
            for q in range(GROUPS):
                for r in range(ROWS):
                    i = ROWS * q + r
                    if i % per == 0:
                        pe.wait_ge(piece_in[i // per], 16)
                    if r == 0:
                        m.need(pe, copied, q - 3)
                    last = pe.transpose(m.bank[q % 4][0:C, r * L:(r + 1) * L], m.nat3[:, i, :], ident)
                last.then_inc(chunk_turned, 1)


def group_norm(nc, m, layer):
    mv, d, mg, e, std = (m.take(n, C) for n in (2, 1, 1, 1, 1))
    S = lambda name: m.sem("gn_" + name)
    acc = m.bank[0]
    with nc.Block() as block:

        @block.vector
        def _(dve):
            step = m.chain(dve, "dve")
            dve.bn_aggr(mv, m.stats[:, :]).then_inc(S("mean"), 1)
            dve.wait_ge(S("group_mean"), layer + 1)
            step(dve.tensor_copy(mg, acc[0:C, 0:1]))
            step(dve.tensor_tensor(d, mv[:, 0:1], mg, ALU.subtract))
            dve.scalar_tensor_tensor(out=e, in0=d, scalar=d, in1=mv[:, 1:2], op0=ALU.mult, op1=ALU.add).then_inc(S("var"), 1)
            dve.wait_ge(S("std"), layer + 1)
            step(dve.reciprocal(m.scale[0:C, :], std))
            dve.scalar_tensor_tensor(out=m.shift[:, :], in0=mg, scalar=-1.0, in1=m.scale[0:C, :], op0=ALU.mult, op1=ALU.mult)

        @block.tensor
        def _(pe):
            pe.wait_ge(S("mean"), layer + 1)
            pe.matmul(acc[0:C, 0:1], m.k("pair", C), mv[:, 0:1], start=True, stop=True).then_inc(S("group_mean"), 1)
            pe.wait_ge(S("var"), layer + 1)
            pe.matmul(acc[0:C, 1:2], m.k("pair", C), e, start=True, stop=True).then_inc(S("group_var"), 1)

        @block.scalar
        def _(act):
            act.wait_ge(S("group_var"), layer + 1)
            act.activation(std, acc[0:C, 1:2], ACT.Sqrt, bias=m.eps[0:C, :]).then_inc(S("std"), 1)


def layer0_norm(nc, m):
    ident = m.k("ident", 128)
    m.open_arena()
    m.bias = m.take(HEADS * L)
    bias_t = m.take(HEADS * L)
    y = [m.take(CH, C) for _ in range(2)]
    mv = [m.take(2 * ROWS).rearrange("p (r s) -> p r s", s=2) for _ in range(2)]
    st = [m.take(6 * ROWS) for _ in range(2)]
    rstd = [m.take(ROWS) for _ in range(2)]
    std = [m.take(ROWS) for _ in range(2)]
    z = [m.take(ROWS * C).rearrange("p (r c) -> p r c", c=C) for _ in range(2)]
    S = lambda name: m.sem(f"z_{name}")
    y_ready, y_turned, measured, std_ready = S("y_ready"), S("y_turned"), S("measured"), S("std_ready")
    rstd_ready, z_ready, z_turned, z_stored, aggr = S("rstd_ready"), S("z_ready"), S("z_turned"), S("z_stored"), S("stats_ready")

    def over_chunks(eng, emit):
        for q in range(4):
            emit(q, q % 2)
        with eng.Fori(0, (GROUPS - 4) // 2, 1) as it:
            for b in range(2):
                emit(it * 2 + (4 + b), b)
        for q in (GROUPS, GROUPS + 1):
            emit(q, q % 2)

    def live(q, lo, hi):
        return not isinstance(q, int) or lo <= q < hi

    with nc.Block() as block:

        @block.scalar
        def _(act):
            def emit(q, b):
                if live(q, 0, GROUPS):
                    m.need(act, y_turned, q - 1)
                    act.activation(y[b].rearrange("p (r c) -> p r c", c=L), m.inner(q * ROWS), ACT.Identity,
                                   scale=m.scale[0:C, :], bias=m.shift[:, :]).then_inc(y_ready, 1)
                if live(q, 1, GROUPS + 1):
                    o = 1 - b
                    m.need(act, measured, q)
                    act.activation(std[o], mv[o][:, :, 1], ACT.Sqrt, bias=m.eps[:, :]).then_inc(std_ready, 1)
                if live(q, 2, GROUPS + 2):
                    m.need(act, z_turned, q - 1)
                    act.activation(m.flat[0:C, ds((q - 2) * CH, CH)], m.bank[2 + b][0:C, :], ACT.Copy).then_inc(z_stored, 1)
            over_chunks(act, emit)

        @block.tensor
        def _(pe):
            def emit(q, b):
                if live(q, 0, GROUPS):
                    m.need(pe, y_ready, q + 1)
                    m.need(pe, z_ready, q - 1)
                    for r in range(ROWS):
                        last = pe.transpose(m.bank[b][:, r * C:(r + 1) * C], y[b][:, r * L:(r + 1) * L], ident[0:C, 0:C])
                    last.then_inc(y_turned, 1)
                if live(q, 2, GROUPS + 2):
                    m.need(pe, z_ready, q - 1)
                    m.need(pe, z_stored, q - 3)
                    for r in range(ROWS):
                        last = pe.transpose(m.bank[2 + b][0:C, r * L:(r + 1) * L], z[b][:, r, :], ident)
                    last.then_inc(z_turned, 1)
            over_chunks(pe, emit)
            pe.wait_ge(z_stored, GROUPS)
            for j in range(L):
                last = pe.matmul(m.bank[4][:, j:HEADS * L:L], m.flat[:, j * L:(j + 1) * L], m.w0b[:, :],
                                 start=True, stop=True, skip_group_check=True)
            last.then_inc(S("bias_made"), 1)
            pe.wait_ge(S("bias_copied"), 1)
            for h in range(HEADS):
                last = pe.transpose(m.bank[5][:, h * L:(h + 1) * L], bias_t[:, h * L:(h + 1) * L], ident)
            last.then_inc(S("bias_turned"), 1)

        @block.vector
        def _(dve):
            def emit(q, b):
                if live(q, 0, GROUPS):
                    m.need(dve, y_turned, q + 1)
                    m.need(dve, std_ready, q - 1)
                    for r in range(ROWS):
                        dve.bn_stats(st[b][:, 6 * r:6 * r + 6], m.bank[b][:, r * C:(r + 1) * C]).then_inc(aggr, 1)
                    for r in range(ROWS):
                        m.need(dve, aggr, q * ROWS + (r + 1))
                        last = dve.bn_aggr(mv[b][:, r, :], st[b][:, 6 * r:6 * r + 6])
                    last.then_inc(measured, 1)
                if live(q, 1, GROUPS + 1):
                    o = 1 - b
                    m.need(dve, std_ready, q)
                    dve.reciprocal(rstd[o], std[o]).then_inc(rstd_ready, 1)
                    m.need(dve, rstd_ready, q)
                    m.need(dve, z_turned, q - 2)
                    for r in range(ROWS):
                        last = dve.tensor_scalar(z[o][:, r, :], m.bank[o][:, r * C:(r + 1) * C], mv[o][:, r, 0:1],
                                                 rstd[o][:, r:r + 1], ALU.subtract, ALU.mult)
                    last.then_inc(z_ready, 1)
            over_chunks(dve, emit)
            dve.wait_ge(S("bias_made"), 1)
            dve.tensor_copy(bias_t, m.bank[4][:, :]).then_inc(S("bias_copied"), 1)
            dve.wait_ge(S("bias_turned"), 1)
            dve.tensor_copy(m.bias, m.bank[5][:, :])


def layer0_attention(nc, m, args):
    ident = m.k("ident", 128)
    m.arena_at = HEADS * L
    spare = [m.nat[:, i * 2048:(i + 1) * 2048] for i in range(4)]
    prob = [spare[0], spare[1]]
    qT = [spare[2][:, i * CH:(i + 1) * CH] for i in (0, 1)]
    th = spare[2][:, 3 * CH:4 * CH]
    v = [spare[3][:, i * CH:(i + 1) * CH] for i in (0, 1)]
    factor = spare[3][:, 2 * CH:3 * CH]
    gated = spare[3][:, 3 * CH:4 * CH]
    kb = [m.take(ROWS * HEADS * L).rearrange("p (r h k) -> p r h k", r=ROWS, h=HEADS) for _ in range(2)]
    zs = [m.take(CH, C + 1) for _ in range(2)]
    pT = [m.take(HEADS * L) for _ in range(2)]
    wo = m.take(C)
    least = [m.take(ROWS * HEADS) for _ in range(2)]
    total = [m.take(ROWS * HEADS) for _ in range(2)]
    rtotal = m.take(ROWS * HEADS)
    rwide = m.take(CH)
    S = lambda name: m.sem(f"l0_{name}")
    z_staged, wo_ready = S("z_staged"), S("wo_ready")
    q_made, k_made, v_made, g_made = S("q_made"), S("k_made"), S("v_made"), S("g_made")
    q_ready, v_ready, th_ready, k_low, k_high = S("q_ready"), S("v_ready"), S("th_ready"), S("k_low"), S("k_high")
    scores_made, shifted, probs_ready = S("scores_made"), S("shifted"), S("probs_ready")
    probs_turned, turned_even, turned_odd = S("probs_turned"), S("turned_even"), S("turned_odd")
    av_made, rtotal_ready, rwide_ready, r_turned = S("av_made"), S("rtotal_ready"), S("rwide_ready"), S("r_turned")
    factor_ready, gated_ready, out_made, x1_ready = S("factor_ready"), S("gated_ready"), S("out_made"), S("x1_ready")
    STEPS0 = GROUPS + 2
    PEEL = 3

    def over_steps(eng, emit):
        for g in range(PEEL + 1):
            emit(g, g % 2)
        with eng.Fori(0, (GROUPS - PEEL - 3) // 2, 1) as it:
            for b in range(2):
                emit(it * 2 + (PEEL + 1 + b), b)
        for g in range(GROUPS - 2, STEPS0):
            emit(g, g % 2)

    def live(g, lo, hi):
        return not isinstance(g, int) or lo <= g < hi

    def rows(t):
        return t.rearrange("p (r x) -> p r x", r=ROWS)

    def k_blocks(b, heads):
        for h in heads:
            part = slice(h * HD, (h + 1) * HD)
            yield kb[b][part, :, h, :], rows(m.bank[2][part, :])

    with nc.Block() as block:

        @block.sync
        def _(sp):
            sp.dma_start(wo, args["L0_conv_Wo"]).then_inc(wo_ready, 16)

        @block.gpsimd
        def _(pool):
            step = m.chain(pool, "pool")
            for b in range(2):
                step(pool.memset(kb[b], 0.0))
            pool.sem_inc(S("kb_zeroed"), 1)

            def stage_z(g, b):
                m.need(pool, v_made, g - 1)
                pool.tensor_copy(zs[b], m.flat[:, ds(g * CH, CH)]).then_inc(z_staged, 1)

            def emit(g, b):
                if live(g, 0, GROUPS - 1):
                    stage_z(g + 1, 1 - b)
                if live(g, 1, GROUPS + 1):
                    m.need(pool, rtotal_ready, g)
                    m.need(pool, r_turned, g - 1)
                    m.need(pool, z_staged, g + 2 if live(g, 0, GROUPS - 1) else GROUPS)
                    pool.tensor_copy(rwide.rearrange("p (x d) -> p x d", d=HD),
                                     rtotal.unsqueeze(2).broadcast_to([128, ROWS * HEADS, HD])).then_inc(rwide_ready, 1)
            stage_z(0, 0)
            over_steps(pool, emit)

        @block.scalar
        def _(act):
            def copy_q(g, b):
                m.need(act, q_made, g + 1)
                act.activation(qT[b], m.bank[2][:, :], ACT.Copy).then_inc(q_ready, 1)

            def copy_k(g, b):
                m.need(act, k_made, g + 1)
                for to, of in k_blocks(b, (0, 1)):
                    last = act.activation(to, of, ACT.Copy)
                last.then_inc(k_low, 1)

            def turn_even(g, r):
                m.need(act, probs_turned, (g - 1) * ROWS + (r + 1))
                m.need(act, av_made, (g - 1) * ROWS + (r - 1))
                act.activation(pT[0], m.bank[0][:, :], ACT.Copy).then_inc(turned_even, 1)

            def exponentials(g, b, r):
                m.need(act, shifted, g * ROWS + (r + 1))
                for h in range(HEADS):
                    t = prob[b][:, (r * HEADS + h) * L:(r * HEADS + h + 1) * L]
                    last = act.activation(t, t, ACT.Exp, scale=-1.0, bias=least[b][:, r * HEADS + h:r * HEADS + h + 1],
                                          accum_out=total[b][:, r * HEADS + h:r * HEADS + h + 1])
                last.then_inc(probs_ready, 1)

            def emit(g, b):
                own, before = live(g, 0, GROUPS), live(g, 1, GROUPS + 1)
                if own:
                    exponentials(g, b, 0)
                if before:
                    turn_even(g, 0)
                if live(g, 0, GROUPS - 1):
                    copy_k(g + 1, 1 - b)
                if own:
                    exponentials(g, b, 1)
                if live(g, 0, GROUPS - 1):
                    copy_q(g + 1, 1 - b)
                if before:
                    turn_even(g, 2)
                if own:
                    exponentials(g, b, 2)
                    exponentials(g, b, 3)
                    m.need(act, g_made, g + 1)
                    m.need(act, factor_ready, g)
                    act.activation(th, m.bank[2][:, :], ACT.Tanh, scale=0.5).then_inc(th_ready, 1)
            act.wait_ge(S("kb_zeroed"), 1)
            copy_k(0, 0)
            copy_q(0, 0)
            over_steps(act, emit)

        @block.vector
        def _(dve):
            dve.wait_ge(wo_ready, 16)
            dve.tensor_scalar(wo, wo, 0.5, None, ALU.mult).then_inc(S("wo_halved"), 1)

            def copy_k(g, b):
                m.need(dve, k_made, g + 1)
                for to, of in k_blocks(b, (2, 3)):
                    last = dve.tensor_copy(to, of)
                last.then_inc(k_high, 1)

            def shift_row(g, b, r):
                for h in range(HEADS):
                    at = (r * HEADS + h) * L
                    last = dve.tensor_tensor_reduce(prob[b][:, at:at + L], m.quad[:, r, h * L:(h + 1) * L],
                                                    m.bias[:, h * L:(h + 1) * L], -1.0, BIG, ALU.add, ALU.min,
                                                    least[b][:, r * HEADS + h:r * HEADS + h + 1])
                last.then_inc(shifted, 1)

            def turn_odd(g, r):
                m.need(dve, probs_turned, (g - 1) * ROWS + (r + 1))
                m.need(dve, av_made, (g - 1) * ROWS + (r - 1))
                dve.tensor_copy(pT[1], m.bank[1][:, :]).then_inc(turned_odd, 1)

            def emit(g, b):
                own, before, older = live(g, 0, GROUPS), live(g, 1, GROUPS + 1), live(g, 2, GROUPS + 2)
                if own:
                    m.need(dve, scores_made, g * ROWS + 1)
                    m.need(dve, probs_turned, (g - 1) * ROWS)
                    shift_row(g, b, 0)
                    m.need(dve, scores_made, g * ROWS + 2)
                    shift_row(g, b, 1)
                if before:
                    m.need(dve, probs_ready, g * ROWS)
                    m.need(dve, rwide_ready, g - 1)
                    dve.reciprocal(rtotal, total[1 - b]).then_inc(rtotal_ready, 1)
                if older:
                    m.need(dve, out_made, g - 1)
                    inner = m.inner((g - 2) * ROWS)
                    dve.scalar_tensor_tensor(out=inner, in0=rows(m.bank[3][0:C, :]), scalar=m.bo[:, :], in1=inner,
                                             op0=ALU.add, op1=ALU.add).then_inc(x1_ready, 1)
                if live(g, 0, GROUPS - 1):
                    copy_k(g + 1, 1 - b)
                if own:
                    m.need(dve, scores_made, g * ROWS + 3)
                    shift_row(g, b, 2)
                if before:
                    turn_odd(g, 1)
                if own:
                    m.need(dve, scores_made, g * ROWS + 4)
                    shift_row(g, b, 3)
                if before:
                    m.need(dve, r_turned, g)
                    m.need(dve, th_ready, g)
                    dve.scalar_tensor_tensor(out=factor, in0=th, scalar=1.0, in1=m.bank[2][:, :],
                                             op0=ALU.add, op1=ALU.mult).then_inc(factor_ready, 1)
                    turn_odd(g, 3)
                if own:
                    m.need(dve, v_made, g + 1)
                    m.need(dve, av_made, (g - 1) * ROWS)
                    dve.tensor_copy(v[b], m.bank[2][:, :]).then_inc(v_ready, 1)
                if before:
                    m.need(dve, av_made, g * ROWS)
                    m.need(dve, factor_ready, g)
                    m.need(dve, out_made, g - 1)
                    dve.tensor_tensor(gated, m.bank[3][:, :], factor, ALU.mult).then_inc(gated_ready, 1)
                if older:
                    m.need(dve, x1_ready, g - 1)
                    dve.bn_stats(m.stats[:, ds((g - 2) * 6, 6)], m.inner((g - 2) * ROWS))
                    dve.tensor_reduce(m.cells[:, ds((g - 2) * KVW, KVW)],
                                      m.inner((g - 2) * ROWS).rearrange("p r (k w) -> p k r w", k=KVW), AX.XY, ALU.add)
            dve.wait_ge(S("kb_zeroed"), 1)
            copy_k(0, 0)
            over_steps(dve, emit)

        @block.tensor
        def _(pe):
            def project(g, w, made):
                pe.matmul(m.bank[2][:, :], m.w0[:, w * 128:(w + 1) * 128], m.flat[:, ds(g * CH, CH)],
                          start=True, stop=True).then_inc(made, 1)

            def project_v(g, b):
                m.need(pe, z_staged, g + 1)
                for r in range(ROWS):
                    last = pe.matmul(m.bank[2][:, r * L:(r + 1) * L], zs[b][:, r * L:(r + 1) * L],
                                     m.w0[:, 256:384], start=True, stop=True)
                last.then_inc(v_made, 1)

            def scores(b, r):
                pe.matmul(m.quad[:, r, :], qT[b][:, r * L:(r + 1) * L], kb[b][:, r, :, :],
                          start=True, stop=True).then_inc(scores_made, 1)

            def turn(g, b, r):
                m.need(pe, probs_ready, (g - 1) * ROWS + (r + 1))
                m.need(pe, turned_odd if r % 2 else turned_even, (g - 1) * 2 + r // 2)
                for h in range(HEADS):
                    at = (r * HEADS + h) * L
                    last = pe.transpose(m.bank[r % 2][:, h * L:(h + 1) * L], prob[1 - b][:, at:at + L], ident)
                last.then_inc(probs_turned, 1)

            def weigh(g, b, r):
                m.need(pe, turned_odd if r % 2 else turned_even, (g - 1) * 2 + (r // 2 + 1))
                if r == 0:
                    m.need(pe, v_ready, g)
                    m.need(pe, x1_ready, g - 1)
                for h in range(HEADS):
                    at = (r * HEADS + h) * HD
                    last = pe.matmul(m.bank[3][h * HD:(h + 1) * HD, r * L:(r + 1) * L], v[1 - b][:, at:at + HD],
                                     pT[r % 2][:, h * L:(h + 1) * L], start=True, stop=True, skip_group_check=True)
                last.then_inc(av_made, 1)

            def emit(g, b):
                own, before, older = live(g, 0, GROUPS), live(g, 1, GROUPS + 1), live(g, 2, GROUPS + 2)
                ahead = live(g, 0, GROUPS - 1)
                if own:
                    m.need(pe, q_ready, g + 1)
                    m.need(pe, k_low, g + 1)
                    m.need(pe, k_high, g + 1)
                    m.need(pe, shifted, g * ROWS)
                    scores(b, 0)
                    scores(b, 1)
                if before:
                    turn(g, b, 0)
                if older:
                    m.need(pe, gated_ready, g - 1)
                    pe.matmul(m.bank[3][0:C, :], wo, gated, start=True, stop=True).then_inc(out_made, 1)
                if ahead:
                    m.need(pe, th_ready, g)
                    project(g + 1, 1, k_made)
                if own:
                    scores(b, 2)
                    scores(b, 3)
                if before:
                    turn(g, b, 1)
                if ahead:
                    m.need(pe, k_low, g + 2)
                    m.need(pe, k_high, g + 2)
                    project(g + 1, 0, q_made)
                if before:
                    weigh(g, b, 0)
                    turn(g, b, 2)
                    m.need(pe, rwide_ready, g)
                    m.need(pe, q_ready, g + 2 if ahead else GROUPS)
                    m.need(pe, th_ready, g)
                    for r in range(ROWS):
                        last = pe.transpose(m.bank[2][:, r * L:(r + 1) * L], rwide[:, r * L:(r + 1) * L], ident)
                    last.then_inc(r_turned, 1)
                    weigh(g, b, 1)
                    turn(g, b, 3)
                if own:
                    m.need(pe, factor_ready, g)
                    m.need(pe, q_ready, g + 2 if ahead else GROUPS)
                    project_v(g, b)
                if before:
                    weigh(g, b, 2)
                    weigh(g, b, 3)
                if own:
                    m.need(pe, v_ready, g + 1)
                    project(g, 3, g_made)
            project(0, 1, k_made)
            pe.wait_ge(k_low, 1)
            pe.wait_ge(k_high, 1)
            project(0, 0, q_made)
            pe.wait_ge(S("wo_halved"), 1)
            over_steps(pe, emit)


def layer1(nc, m, args):
    ident = m.k("ident", 128)
    ident64 = ident[0:C, 0:C]
    TAPS = 9
    TOKENS = NWIN * KVW * KVW
    m.open_arena()
    kv_raw = m.take(C + 1)
    q_raw = m.take(C + 1, C)
    v_raw = m.take(C + 1, C)
    wo_raw = m.take(C, C)
    dw_raw = m.take(C, TAPS)
    dw_b, wo_b = m.take(1, C), m.take(1, C)
    turned = m.take(192 + C + TAPS, C + 1)
    kvT, qT = turned[:, 0:128], turned[:, 128:192]
    woT, dwT = turned[0:C, 192:256], turned[0:C, 256:256 + TAPS]
    spread = m.take(TAPS * C, C)
    taps = m.take(TAPS * C, C + 1)
    folded = m.take(TAPS * C, C + 1)
    centre = m.take(NWIN * C, C + 1)
    centre_folded = m.take(NWIN * C, C + 1)
    fold = m.take(C + 1, C + 1)
    pooled = m.take(TOKENS, C + 1)
    pooled_win = m.take(NWIN, C + 1)
    kv = m.take(128)
    q_win = m.take(NWIN, C)
    logits = m.take(NWIN, NWIN)
    above = m.take(64, NWIN).rearrange("p (j k) -> p j k", k=NWIN)
    same = m.take(64, NWIN).rearrange("p (j k) -> p j k", k=NWIN)
    rank, chosen, chosen_t = m.take(NWIN, NWIN), m.take(NWIN, NWIN), m.take(NWIN, NWIN)
    token_mask = m.take(NWIN)
    k_masked = m.take(NWIN * C)
    mT = m.take(NWIN * C, C)
    m_wo = m.take(NWIN * C, C)
    const_out = m.take(1, C)
    packed = m.nat[:, 0:2 * (2 + NWIN) * 128].rearrange("p (i k e o) -> p i k e o", i=2, k=2 + NWIN, e=2)
    outer = [packed[:, i, 0:2, :, :] for i in range(2)]
    middle = [packed[:, i, 2:2 + NWIN, :, :] for i in range(2)]
    bias_sum = m.take(C, C + 1)[C:C + 1, :]
    bias_rows = m.take(NWIN * 128, C + 1)[C:C + 1, :].rearrange("p (w e o) -> p w e o", w=NWIN, e=2)
    col_rows = m.take(3 * 128, C + 1)[C:C + 1, :].rearrange("p (x e o) -> p x e o", x=3, e=2)
    edge_rows = m.take(2 * 3 * 128, C + 1)[C:C + 1, :].rearrange("p (t x e o) -> p t x e o", t=2, x=3, e=2)
    bias = m.take(NWIN)
    BANKS = L // 8
    S = lambda name: m.sem(f"l1_{name}")
    loads = [
        (kv_raw[:, 0:C], args["L1_conv_qkv_w"][C:3 * C, :]),
        (kv_raw[:, C:C + 1], args["L1_conv_qkv_b"].rearrange("(o a) -> o a", a=1)[C:3 * C, :]),
        (q_raw[:, 0:C], args["L1_conv_qkv_w"][0:C, :]),
        (q_raw[:, C:C + 1], args["L1_conv_qkv_b"].rearrange("(o a) -> o a", a=1)[0:C, :]),
        (v_raw[:, 0:C], args["L1_conv_qkv_w"][2 * C:3 * C, :]),
        (v_raw[:, C:C + 1], args["L1_conv_qkv_b"].rearrange("(o a) -> o a", a=1)[2 * C:3 * C, :]),
        (wo_raw, args["L1_conv_wo_w"]),
        (dw_raw, args["L1_conv_dw_w"].rearrange("kh kw a m -> (kh kw a) m")),
        (dw_b, args["L1_conv_dw_b"].rearrange("(c a) -> c a", a=1)),
        (wo_b, args["L1_conv_wo_b"].rearrange("(c a) -> c a", a=1)),
    ]
    B = m.bank
    by_window = lambda t: t.rearrange("p (w c) -> p w c", w=NWIN)
    in_pairs = lambda t: t.rearrange("p (m c) -> p m c", c=L)

    def out_rows(g, parity):
        return m.flat[0:C, 8 * g * L:8 * (g + 1) * L].rearrange("p (m e c) -> p m e c", e=2, c=L)[:, :, parity, :]

    def tap(dy, dx, lo=0, hi=C):
        return folded[lo:hi, (3 * dy + dx) * C:(3 * dy + dx + 1) * C]

    with nc.Block() as block:

        @block.sync
        def _(sp):
            for dst, src in loads:
                sp.dma_start(dst, src).then_inc(S("loaded"), 16)

        @block.vector
        def _(dve):
            step = m.chain(dve, "dve")
            step(dve.tensor_scalar(fold, ident[0:C + 1, 0:C + 1], m.scale[:, :], None, ALU.mult))
            dve.tensor_copy(fold[0:C, C:C + 1], m.shift[:, :]).then_inc(S("prep_ready"), 1)
            step(dve.tensor_scalar(pooled[0:C, :], m.cells[:, :], 1.0 / CELL, None, ALU.mult))
            step(dve.tensor_scalar(pooled[0:C, :], pooled[0:C, :], m.scale[0:C, :], m.shift[:, :], ALU.mult, ALU.add))
            step(dve.memset(pooled[C:C + 1, :], 1.0))
            step(dve.tensor_reduce(pooled_win, pooled.rearrange("p (w t) -> p w t", w=NWIN), AX.X, ALU.add))
            dve.tensor_scalar(pooled_win, pooled_win, 1.0 / (KVW * KVW), None, ALU.mult).then_inc(S("prep_ready"), 1)
            dve.wait_ge(S("prep_made"), 1)
            dve.tensor_copy(turned[:, 0:192], B[0][0:C + 1, 0:192])
            step(dve.tensor_copy(turned[0:C, 192:256 + TAPS], B[0][0:C, 192:256 + TAPS]))
            dve.tensor_tensor(spread.rearrange("p (t o) -> p t o", t=TAPS), woT.unsqueeze(1).broadcast_to([C, TAPS, C]),
                              dwT.unsqueeze(2).broadcast_to([C, TAPS, C]), ALU.mult).then_inc(S("prep_ready"), 1)
            dve.wait_ge(S("prep_made"), 2)
            dve.tensor_copy(kv, B[1][:, 0:128])
            dve.tensor_copy(q_win, B[2][0:C, 0:NWIN]).then_inc(S("prep_ready"), 1)
            dve.wait_ge(S("prep_made"), 3)
            dve.tensor_copy(taps[:, 0:512], B[3][0:C + 1, :])
            step(dve.tensor_copy(taps[:, 512:TAPS * C], B[4][0:C + 1, 0:C]))
            dve.sem_inc(S("prep_ready"), 1)
            dve.wait_ge(S("window_made"), 1)
            step(dve.tensor_scalar(logits, B[5][0:NWIN, 0:NWIN], float(C) ** -0.5, None, ALU.mult))
            of_j = logits.unsqueeze(2).broadcast_to([NWIN, NWIN, NWIN])
            of_k = logits.unsqueeze(1).broadcast_to([NWIN, NWIN, NWIN])
            step(dve.tensor_tensor(above, of_k, of_j, ALU.is_gt))
            step(dve.tensor_tensor(same, of_k, of_j, ALU.is_equal))
            step(dve.tensor_tensor(same, same, m.k("earlier", NWIN).rearrange("p (j k) -> p j k", k=NWIN), ALU.mult))
            step(dve.tensor_tensor(above, above, same, ALU.add))
            step(dve.tensor_reduce(rank, above, AX.X, ALU.add))
            dve.tensor_scalar(chosen, rank, TOPW - 0.5, None, ALU.is_lt).then_inc(S("window_ready"), 1)
            dve.wait_ge(S("window_made"), 2)
            dve.tensor_copy(chosen_t, B[5][0:NWIN, 16:16 + NWIN]).then_inc(S("window_ready"), 1)
            dve.wait_ge(S("window_made"), 3)
            step(dve.tensor_copy(token_mask, B[6][:, 0:NWIN]))
            dve.tensor_tensor(by_window(k_masked), kv[:, 0:C].unsqueeze(1).broadcast_to([128, NWIN, C]),
                              token_mask.unsqueeze(2).broadcast_to([128, NWIN, C]), ALU.mult).then_inc(S("window_ready"), 1)
            dve.wait_ge(S("window_made"), 4)
            dve.scalar_tensor_tensor(out=by_window(mT), in0=by_window(B[7][0:C, :]), scalar=float(C) ** -0.5,
                                     in1=m.k("headmask", C).unsqueeze(1).broadcast_to([C, NWIN, C]),
                                     op0=ALU.mult, op1=ALU.mult).then_inc(S("window_ready"), 1)
            dve.wait_ge(S("window_made"), 5)
            dve.tensor_copy(m_wo, B[0][0:C, :]).then_inc(S("window_ready"), 1)
            dve.wait_ge(S("window_made"), 6)
            dve.tensor_tensor(by_window(centre), by_window(B[1][0:C + 1, :]),
                              taps[:, 4 * C:5 * C].unsqueeze(1).broadcast_to([C + 1, NWIN, C]), ALU.add).then_inc(S("window_ready"), 1)
            dve.wait_ge(S("folded_made"), 1)
            dve.tensor_tensor(by_window(centre_folded[0:C, :]), by_window(B[2][0:C, :]),
                              ident64.unsqueeze(1).broadcast_to([C, NWIN, C]), ALU.add)
            dve.tensor_copy(centre_folded[C:C + 1, :], B[2][C:C + 1, :])
            dve.tensor_copy(folded[:, 0:512], B[3][0:C + 1, :])
            dve.tensor_copy(folded[:, 512:TAPS * C], B[4][0:C + 1, 0:C])
            step(dve.tensor_scalar(const_out, B[5][0:C, 32:33], wo_b, None, ALU.add))
            dve.sem_inc(S("weights_ready"), 1)
            row = folded[C:C + 1, :]
            for e in range(2):
                last = dve.tensor_reduce(col_rows[:, :, e, :], row.rearrange("p (y x o) -> p x o y", y=3, x=3), AX.X, ALU.add)
                dve.tensor_copy(edge_rows[:, e, :, e, :], row.rearrange("p (y x o) -> p y x o", y=3, x=3)[:, 2 * e, :, :])
            step(last)
            step(dve.tensor_reduce(bias_sum, col_rows[:, :, 0, :].rearrange("p x o -> p o x"), AX.X, ALU.add))
            step(dve.tensor_tensor(bias_sum, bias_sum, tap(1, 1, C, C + 1), ALU.subtract))
            for e in range(2):
                last = dve.tensor_tensor(bias_rows[:, :, e, :], by_window(centre_folded[C:C + 1, :]),
                                         bias_sum.unsqueeze(1).broadcast_to([1, NWIN, C]), ALU.add)
            last.then_inc(S("bias_rows_ready"), 1)
            dve.wait_ge(S("bias_turned"), 1)
            dve.tensor_scalar(bias[0:C, :], B[6][0:C, 0:NWIN], const_out, None, ALU.add)
            step(dve.tensor_scalar(bias[C:128, :], B[6][C:128, 0:NWIN], const_out, None, ALU.add))
            dve.sem_inc(S("bias_ready"), 1)
            for g in range(BANKS):
                dve.wait_ge(S("conv_made"), g + 1)
                dve.tensor_scalar(out_rows(g, 1), in_pairs(B[g % 8][C:128, :]), bias[C:128, g // 2:g // 2 + 1], None,
                                  ALU.add).then_inc(S("odd_ready"), 1)
                dve.wait_ge(S("odd_ready"), g + 1)
                dve.wait_ge(S("even_ready"), g + 1)
                for half in range(2):
                    at = 2 * g + half
                    dve.bn_stats(m.stats[:, 6 * at:6 * at + 6], m.flat[0:C, at * CH:(at + 1) * CH])

        @block.gpsimd
        def _(pool):
            step = m.chain(pool, "pool")
            for part in (outer, middle):
                step(pool.memset(part[0][0:C, :, 1, :], 0.0))
                step(pool.memset(part[1][C:128, :, 0, :], 0.0))
            step(pool.memset(edge_rows[:, 0, :, 1, :], 0.0))
            step(pool.memset(edge_rows[:, 1, :, 0, :], 0.0))
            pool.wait_ge(S("weights_ready"), 1)
            for pair, dy in ((0, 0), (1, 2)):
                step(pool.tensor_copy(middle[pair][0:C, :, 0, :], tap(dy, 1).unsqueeze(1).broadcast_to([C, NWIN, C])))
                step(pool.tensor_copy(middle[pair][C:128, :, 1, :], tap(dy, 1).unsqueeze(1).broadcast_to([C, NWIN, C])))
            step(pool.tensor_copy(middle[0][C:128, :, 0, :], by_window(centre_folded[0:C, :])))
            pool.tensor_copy(middle[1][0:C, :, 1, :], by_window(centre_folded[0:C, :])).then_inc(S("middle_ready"), 1)

        @block.scalar
        def _(act):
            quarter = L // 4
            for n in range(4):
                last = act.activation(m.img3[C:128, n * quarter:(n + 1) * quarter:2, :],
                                      m.img3[0:C, n * quarter + 1:(n + 1) * quarter + 1:2, :], ACT.Copy)
            last.then_inc(S("rows_paired"), 1)
            act.wait_ge(S("weights_ready"), 1)
            for dx in (0, 2):
                for pair, dy in ((0, 0), (1, 2)):
                    act.activation(outer[pair][0:C, dx // 2, 0, :], tap(dy, dx), ACT.Copy)
                    act.activation(outer[pair][C:128, dx // 2, 1, :], tap(dy, dx), ACT.Copy)
                act.activation(outer[0][C:128, dx // 2, 0, :], tap(1, dx), ACT.Copy)
                last = act.activation(outer[1][0:C, dx // 2, 1, :], tap(1, dx), ACT.Copy)
            last.then_inc(S("outer_ready"), 1)
            act.wait_ge(S("bias_ready"), 1)
            for g in range(BANKS):
                act.wait_ge(S("conv_made"), g + 1)
                act.activation(out_rows(g, 0), in_pairs(B[g % 8][0:C, :]), ACT.Identity,
                               bias=bias[0:C, g // 2:g // 2 + 1]).then_inc(S("even_ready"), 1)

        @block.tensor
        def _(pe):
            pe.wait_ge(S("loaded"), 16 * len(loads))
            pe.transpose(B[0][0:C + 1, 0:128], kv_raw, ident)
            pe.transpose(B[0][0:C + 1, 128:192], q_raw, ident64)
            pe.transpose(B[0][0:C, 192:256], wo_raw, ident64)
            pe.transpose(B[0][0:C, 256:256 + TAPS], dw_raw, ident[0:TAPS, 0:TAPS]).then_inc(S("prep_made"), 1)
            pe.wait_ge(S("prep_ready"), 3)
            pe.wait_ge(S("prep_ready"), 2)
            pe.matmul(B[1][:, 0:128], pooled, kvT, start=True, stop=True)
            pe.matmul(B[2][0:C, 0:NWIN], qT, pooled_win, start=True, stop=True).then_inc(S("prep_made"), 1)
            pe.matmul(B[3][0:C + 1, :], v_raw, spread[:, 0:512], start=True, stop=True)
            pe.matmul(B[4][0:C + 1, 0:C], v_raw, spread[:, 512:TAPS * C], start=True, stop=True).then_inc(S("prep_made"), 1)
            pe.wait_ge(S("prep_ready"), 4)
            pe.matmul(B[5][0:NWIN, 0:NWIN], q_win, q_win, start=True, stop=True).then_inc(S("window_made"), 1)
            pe.wait_ge(S("window_ready"), 1)
            pe.transpose(B[5][0:NWIN, 16:16 + NWIN], chosen, ident[0:NWIN, 0:NWIN]).then_inc(S("window_made"), 1)
            pe.wait_ge(S("window_ready"), 2)
            pe.matmul(B[6][:, 0:NWIN], m.k("expand", NWIN), chosen_t, start=True, stop=True).then_inc(S("window_made"), 1)
            pe.wait_ge(S("window_ready"), 3)
            pe.matmul(B[7][0:C, :], kv[:, C:128], k_masked, start=True, stop=True).then_inc(S("window_made"), 1)
            pe.wait_ge(S("window_ready"), 4)
            for w in range(NWIN):
                last = pe.matmul(B[0][0:C, w * C:(w + 1) * C], mT[:, w * C:(w + 1) * C], woT, start=True, stop=True)
            last.then_inc(S("window_made"), 1)
            pe.wait_ge(S("window_ready"), 5)
            pe.matmul(B[1][0:C + 1, :], q_raw, m_wo, start=True, stop=True).then_inc(S("window_made"), 1)
            pe.wait_ge(S("window_ready"), 6)
            pe.wait_ge(S("prep_ready"), 5)
            pe.wait_ge(S("prep_ready"), 1)
            pe.matmul(B[2][0:C + 1, :], fold, centre, start=True, stop=True)
            pe.matmul(B[3][0:C + 1, :], fold, taps[:, 0:512], start=True, stop=True)
            pe.matmul(B[4][0:C + 1, 0:C], fold, taps[:, 512:TAPS * C], start=True, stop=True)
            pe.matmul(B[5][0:C, 32:33], woT, dw_b, start=True, stop=True).then_inc(S("folded_made"), 1)
            pe.wait_ge(S("weights_ready"), 1)
            pe.wait_ge(S("bias_rows_ready"), 1)
            for w in range(NWIN):
                last = pe.matmul(B[6][:, w:w + 1], bias_rows[:, w, :, :], m.scale[C:C + 1, :], start=True, stop=True)
            last.then_inc(S("bias_turned"), 1)
            pe.wait_ge(S("rows_paired"), 1)
            pe.wait_ge(S("outer_ready"), 1)
            pe.wait_ge(S("middle_ready"), 1)
            minus = m.const[C:C + 1, CONSTS["minus"]]
            for g in range(BANKS):
                if g == 6:
                    pe.wait_ge(S("bias_ready"), 1)
                if g >= 8:
                    pe.wait_ge(S("even_ready"), g - 7)
                    pe.wait_ge(S("odd_ready"), g - 7)
                for n, (pair, dx) in enumerate((p, dx) for p in range(2) for dx in range(3)):
                    weights = middle[pair][:, g // 2, :, :] if dx == 1 else outer[pair][:, dx // 2, :, :]
                    first = 8 * g + 2 * pair
                    pe.matmul(B[g % 8][:, :], weights, m.img3[:, first:first + 7:2, dx:dx + L],
                              start=(n == 0), stop=False, skip_group_check=True)
                for dx, column in ((0, 0), (2, L - 1)):
                    last = pe.matmul(B[g % 8][:, column:column + 3 * L + 1:L], col_rows[:, dx, :, :], minus[:, 1:5],
                                     start=False, stop=True, skip_group_check=True)
                if g in (0, BANKS - 1):
                    e = g // (BANKS - 1)
                    for dx in range(3):
                        last = pe.matmul(B[g % 8][:, e * 3 * L:(e * 3 + 1) * L], edge_rows[:, e, dx, :, :],
                                         minus[:, dx:dx + L], start=False, stop=True, skip_group_check=True)
                last.then_inc(S("conv_made"), 1)


def layer2(nc, m):
    ident = m.k("ident", 128)
    HALF = ROWS // 2
    RULE = GIANTS // 2 + 1
    m.open_arena()
    nat_tiles = iter(m.nat[:, n:n + CH] for n in range(0, L * C, CH))
    m.colsum = m.take(CH, C)
    vt = [m.take(ROWS * 256).rearrange("p (n x) -> p n x", n=ROWS) for _ in range(2)]
    yv = [m.take(2 * ROWS * C).rearrange("p (n k d) -> p n k d", n=ROWS, k=2) for _ in range(2)]
    xs = m.take(ROWS * C)
    xsT = m.take(CH, C)
    cor = m.take(CH)
    rem = m.take(CH)
    a1 = m.take(CH)
    a2 = m.take(CH)
    a4, a8 = ([next(nat_tiles) for _ in range(2)] for _ in range(2))
    z_top = m.take(ROWS * C)
    zs = [[next(nat_tiles)[:, 0:HALF * 2 * C].rearrange("p (n x) -> p n x", n=HALF) for _ in range(2)]
          for _ in range(2)]
    st = m.take(6 * ROWS)
    mv = m.take(2 * ROWS).rearrange("p (r s) -> p r s", s=2)
    std, rstd, deg, dsq, dinv = (m.take(ROWS) for _ in range(5))
    top = m.take(8 * ROWS)
    S = lambda name: m.sem(f"l2_{name}")
    y_ready, y_turned, yn_ready, stats_ready, measured, std_ready, std_eased, rstd_ready, xs_ready, xs_turned, xsT_ready = map(
        S, "y_ready y_turned yn_ready stats_ready measured std_ready std_eased rstd_ready xs_ready xs_turned xsT_ready".split())
    cor_made, cor_ready, topk_step, rem_ready, diag_added, m_turned, deg_summed, deg_ready, dsq_ready, dinv_ready, b_ready = map(
        S, "cor_made cor_ready topk_step rem_ready diag_added m_turned deg_summed deg_ready dsq_ready dinv_ready b_ready".split())
    b_turned, a2_made, a2_ready, ay_made, ay_ready, v1_turned, v1_ready, a4_made, a4_ready, a8_made, a8_ready, v23_made, v23_ready = map(
        S, "b_turned a2_made a2_ready ay_made ay_ready v1_turned v1_ready a4_made a4_ready a8_made a8_ready v23_made v23_ready".split())
    low_used, col_added = S("low_used"), S("col_added")
    horner_made, z_ready, z_turned, x3_ready, a_ready = ([S(f"{name}_{half}") for half in ("first", "last")]
                                                for name in ("horner_made", "z_ready", "z_turned", "x3_ready", "a_ready"))
    B = m.bank

    def over_steps(eng, emit):
        for s in range(4):
            emit(s, s % 2)
        with eng.Fori(0, (GROUPS - 6) // 2, 1) as it:
            for b in range(2):
                emit(it * 2 + (4 + b), b)
        for s in range(GROUPS - 2, GROUPS + 2):
            emit(s, s % 2)

    def live(s, lo, hi):
        return not isinstance(s, int) or lo <= s < hi

    def parts(s):
        return live(s, 0, GROUPS), live(s, 1, GROUPS + 1), live(s, 2, GROUPS + 2)

    def quarters(t):
        return t.rearrange("p (n x) -> p n x", n=ROWS)

    def halves(t):
        return t.rearrange("p (n x) -> p n x", n=HALF)

    def done(s, half, k):
        return (s - 1 - half) * RULE + k

    def place(k):
        return (GIANTS - 2 - 2 * k, 2) if k < RULE - 1 else (0, 1)

    with nc.Block() as block:

        @block.gpsimd
        def _(pool):
            step = m.chain(pool, "pool")
            step(pool.memset(m.colsum, 0.0))

            def emit(s, b):
                p, q, r = parts(s)
                if p:
                    m.need(pool, rem_ready, s + 1)
                    pool.tensor_tensor(quarters(rem), quarters(rem), ident.unsqueeze(1).broadcast_to([128, ROWS, 128]),
                                       ALU.add).then_inc(diag_added, 1)
                if r:
                    m.need(pool, x3_ready[1], s - 1)
                    m.need(pool, col_added, s - 2)
                    pool.tensor_tensor(quarters(m.colsum), quarters(m.colsum), m.inner((s - 2) * ROWS), ALU.add).then_inc(col_added, 1)
            over_steps(pool, emit)

        @block.scalar
        def _(act):
            def take_y(s, b):
                act.activation(vt[b][0:C, :, 0:L], quarters(m.flat[0:C, ds(s * CH, CH)]), ACT.Identity,
                               scale=m.scale[0:C, :], bias=m.shift[:, :]).then_inc(y_ready, 1)

            def keep_z(s, half, k):
                g, n = place(k)
                m.need(act, horner_made[half], done(s, half, k + 1))
                act.activation(zs[half][k % 2][:, :, 0:n * C], m.quad[:, HALF * half:HALF * (half + 1), g * C:(g + n) * C],
                               ACT.Copy if k < RULE - 1 else ACT.Relu).then_inc(z_ready[half], 1)

            def turned_y(s, b):
                m.need(act, y_turned, s + 1)
                act.activation(yv[b][:, :, 0, :], quarters(B[0][:, 0:ROWS * C]), ACT.Copy).then_inc(yn_ready, 1)

            def deviation(s):
                m.need(act, measured, s + 1)
                act.activation(std, mv[:, :, 1], ACT.Sqrt, scale=C / (C - 1)).then_inc(std_ready, 1)

            def emit(s, b):
                p, q, r = parts(s)
                ahead = live(s, 0, GROUPS - 1)
                o = 1 - b
                if r:
                    keep_z(s, 1, 0)
                if q:
                    m.need(act, a2_made, s)
                    act.activation(a2, B[0][:, :], ACT.Copy).then_inc(a2_ready, 1)
                if r:
                    keep_z(s, 1, 1)
                if p:
                    m.need(act, xs_turned, s + 1)
                    act.activation(xsT, B[2][0:C, :], ACT.Copy).then_inc(xsT_ready, 1)
                if r:
                    keep_z(s, 1, 2)
                if p:
                    m.need(act, cor_made, s + 1)
                    m.need(act, b_turned, s)
                    act.activation(cor, B[2][:, :], ACT.Copy, scale=1.0 / (C - 1 + 1e-6)).then_inc(cor_ready, 1)
                if q:
                    m.need(act, a4_made, s)
                    act.activation(a4[o], B[0][:, :], ACT.Copy).then_inc(a4_ready, 1)
                if r:
                    keep_z(s, 1, 3)
                    keep_z(s, 1, 4)
                if q:
                    m.need(act, a8_made, s)
                    act.activation(a8[o], B[0][:, :], ACT.Copy).then_inc(a8_ready, 1)
                    m.need(act, v23_made, s)
                    act.activation(vt[o][:, :, L:2 * L], quarters(B[1][:, :]), ACT.Copy).then_inc(v23_ready, 1)
                if ahead:
                    m.need(act, low_used, s)
                    take_y(s + 1, o)
                if p:
                    m.need(act, deg_ready, s + 1)
                    act.activation(dsq, deg, ACT.Sqrt).then_inc(dsq_ready, 1)
                if q:
                    keep_z(s, 0, 0)
                if ahead:
                    turned_y(s + 1, o)
                if q:
                    keep_z(s, 0, 1)
                for half in range(2):
                    if q:
                        keep_z(s, 0, 2 + half)
                    if p:
                        m.need(act, b_turned, s + 1)
                        for n in range(HALF * half, HALF * (half + 1)):
                            last = act.activation(a1[:, n * L:(n + 1) * L], B[2][:, n * L:(n + 1) * L], ACT.Copy,
                                                  scale=dinv[:, n:n + 1])
                        last.then_inc(a_ready[half], 1)
                if ahead:
                    deviation(s + 1)
                if q:
                    keep_z(s, 0, 4)
            take_y(0, 0)
            turned_y(0, 0)
            deviation(0)
            over_steps(act, emit)

        @block.vector
        def _(dve):
            def finish(s, half):
                row = (s - 1 - half) * ROWS + HALF * half
                m.need(dve, z_turned[half], s - half)
                dve.tensor_tensor(m.inner(row, HALF), halves(B[3][0:C, 0:HALF * L]), halves(m.flat[0:C, ds(row * L, HALF * L)]),
                                  ALU.add).then_inc(x3_ready[half], 1)

            def standardise(s, b):
                m.need(dve, yn_ready, s + 1)
                for n in range(ROWS):
                    last = dve.bn_stats(st[:, 6 * n:6 * n + 6], yv[b][:, n, 0, :])
                last.then_inc(stats_ready, 1)
                m.need(dve, stats_ready, s + 1)
                m.need(dve, xs_ready, s)
                for n in range(ROWS):
                    last = dve.bn_aggr(mv[:, n, :], st[:, 6 * n:6 * n + 6])
                last.then_inc(measured, 1)
                m.need(dve, std_ready, s + 1)
                dve.tensor_scalar(std, std, 1e-6, None, ALU.add).then_inc(std_eased, 1)
                m.need(dve, std_eased, s + 1)
                dve.reciprocal(rstd, std).then_inc(rstd_ready, 1)
                m.need(dve, rstd_ready, s + 1)
                m.need(dve, xs_turned, s)
                for n in range(ROWS):
                    last = dve.tensor_scalar(xs[:, n * C:(n + 1) * C], yv[b][:, n, 0, :], mv[:, n, 0:1], rstd[:, n:n + 1],
                                             ALU.subtract, ALU.mult)
                last.then_inc(xs_ready, 1)

            def emit(s, b):
                p, q, r = parts(s)
                o = 1 - b
                before = s * (4 * ROWS + 1)
                if q:
                    m.need(dve, ay_made, s)
                    dve.tensor_copy(yv[o][:, :, 1, :], quarters(B[3][:, 0:ROWS * C]))
                    dve.tensor_copy(z_top, B[3][:, ROWS * C:2 * ROWS * C]).then_inc(ay_ready, 1)
                if p:
                    m.need(dve, cor_ready, s + 1)
                    for n in range(ROWS):
                        dve.max(top[:, 8 * n:8 * n + 8], cor[:, n * L:(n + 1) * L]).then_inc(topk_step, 1)
                    m.need(dve, m_turned, s)
                    for n in range(ROWS):
                        m.need(dve, topk_step, before + (n + 1))
                        dve.match_replace(rem[:, n * L:(n + 1) * L], top[:, 8 * n:8 * n + 8], cor[:, n * L:(n + 1) * L],
                                          -BIG).then_inc(topk_step, 1)
                if q:
                    m.need(dve, v1_turned, s)
                    dve.tensor_copy(vt[o][C:128, :, 0:L], quarters(B[1][C:128, :])).then_inc(v1_ready, 1)
                if p:
                    for n in range(ROWS):
                        m.need(dve, topk_step, before + (ROWS + n + 1))
                        dve.max(top[:, 8 * n:8 * n + 8], rem[:, n * L:(n + 1) * L]).then_inc(topk_step, 1)
                    m.need(dve, topk_step, before + 3 * ROWS)
                    dve.memset(top.rearrange("p (n k) -> p n k", k=8)[:, :, 1:8], -BIG).then_inc(topk_step, 1)
                if p:
                    m.need(dve, topk_step, before + (3 * ROWS + 1))
                    for n in range(ROWS):
                        dve.match_replace(rem[:, n * L:(n + 1) * L], top[:, 8 * n:8 * n + 8], rem[:, n * L:(n + 1) * L],
                                          -BIG).then_inc(topk_step, 1)
                    m.need(dve, topk_step, before + (4 * ROWS + 1))
                    dve.scalar_tensor_tensor(out=rem, in0=rem, scalar=-BIG, in1=cor, op0=ALU.is_equal, op1=ALU.mult).then_inc(rem_ready, 1)
                    m.need(dve, m_turned, s + 1)
                    for n in range(ROWS):
                        last = dve.tensor_tensor_reduce(cor[:, n * L:(n + 1) * L], rem[:, n * L:(n + 1) * L],
                                                        B[1][:, n * L:(n + 1) * L], 1.0, 0.0, ALU.add, ALU.add, deg[:, n:n + 1])
                    last.then_inc(deg_summed, 1)
                    m.need(dve, deg_summed, s + 1)
                    dve.tensor_scalar(deg, deg, 0.5, 1e-6, ALU.mult, ALU.max).then_inc(deg_ready, 1)
                    m.need(dve, dsq_ready, s + 1)
                    m.need(dve, a_ready[1], s)
                    dve.reciprocal(dinv, dsq).then_inc(dinv_ready, 1)
                    m.need(dve, dinv_ready, s + 1)
                    for n in range(ROWS):
                        last = dve.tensor_scalar(cor[:, n * L:(n + 1) * L], cor[:, n * L:(n + 1) * L], dinv[:, n:n + 1], 0.5,
                                                 ALU.mult, ALU.mult)
                    last.then_inc(b_ready, 1)
                if r:
                    finish(s, 1)
                if live(s, 0, GROUPS - 1):
                    standardise(s + 1, o)
                if r:
                    m.need(dve, x3_ready[1], s - 1)
                    dve.bn_stats(m.stats[:, ds((s - 2) * 6, 6)], m.inner((s - 2) * ROWS))
                    dve.tensor_reduce(m.cells[:, ds((s - 2) * ROWS, ROWS)], m.inner((s - 2) * ROWS), AX.X, ALU.add)
                if q:
                    finish(s, 0)
            standardise(0, 0)
            over_steps(dve, emit)

        @block.tensor
        def _(pe):
            def col(n, w=L):
                return slice(n * w, (n + 1) * w)

            def horner(s, half, k, chunk):
                g, width = place(k)
                if k:
                    m.need(pe, z_ready[half], done(s, half, k))
                for n in range(HALF):
                    row = HALF * half + n
                    if k == 0:
                        value, width = z_top[:, col(row, C)], 1
                    elif k < RULE - 1:
                        value = zs[half][(k - 1) % 2][:, n, :]
                    else:
                        value = zs[half][(k - 1) % 2][:, n, C:2 * C]
                    power = a8[chunk] if k < RULE - 1 else a4[chunk]
                    last = pe.matmul(m.quad[:, row, g * C:(g + width) * C], power[:, col(row)], value,
                                     start=False, stop=(k == RULE - 1), skip_group_check=True)
                last.then_inc(horner_made[half], 1)

            def low(n, o):
                return pe.matmul(m.quad[:, n, :], vt[o][:, n, 0:L], m.theta[:, 0, :], start=True, stop=False, skip_group_check=True)

            def high(n, o):
                return pe.matmul(m.quad[:, n, :], vt[o][:, n, L:2 * L], m.theta[:, 1, :], start=False, stop=False, skip_group_check=True)

            def turn_z(s, half):
                m.need(pe, z_ready[half], done(s, half, RULE))
                for n in range(HALF):
                    last = pe.transpose(B[3][0:C, col(n)], zs[half][0][:, n, 0:C], ident)
                last.then_inc(z_turned[half], 1)

            def turn_y(s, b):
                m.need(pe, y_ready, s + 1)
                for n in range(ROWS):
                    last = pe.transpose(B[0][:, col(n, C)], vt[b][0:C, n, 0:L], ident[0:C, 0:C])
                last.then_inc(y_turned, 1)

            def emit(s, b):
                p, q, r = parts(s)
                o = 1 - b

                def square(source):
                    for n in range(ROWS):
                        last = pe.matmul(B[0][:, col(n)], source[:, col(n)], source[:, col(n)], start=True, stop=True)
                    return last

                def slot(half, k):
                    if half and r:
                        horner(s, 1, k, b)
                    if not half and q:
                        horner(s, 0, k, o)

                slot(1, 0)
                if q:
                    m.need(pe, a_ready[1], s)
                    m.need(pe, yn_ready, s + 1 if p else s)
                    square(a1).then_inc(a2_made, 1)
                slot(1, 1)
                if p:
                    m.need(pe, xs_ready, s + 1)
                    m.need(pe, a_ready[1], s)
                    for n in range(ROWS):
                        last = pe.transpose(B[2][0:C, col(n)], xs[:, col(n, C)], ident)
                    last.then_inc(xs_turned, 1)
                if q:
                    m.need(pe, x3_ready[0], s - 1)
                    for n in range(ROWS):
                        pe.matmul(B[3][:, col(n, C)], a1[:, col(n)], yv[o][:, n, 0, :], start=True, stop=True)
                    for n in range(ROWS):
                        last = pe.matmul(B[3][:, col(ROWS + n, C)], vt[o][0:C, n, 0:L], m.theta_top[:, :], start=True, stop=True)
                    last.then_inc(ay_made, 1)
                slot(1, 2)
                if p:
                    m.need(pe, xsT_ready, s + 1)
                    for n in range(ROWS):
                        last = pe.matmul(B[2][:, col(n)], xsT[:, col(n)], xsT[:, col(n)], start=True, stop=True)
                    last.then_inc(cor_made, 1)
                if q:
                    m.need(pe, a2_ready, s)
                    square(a2).then_inc(a4_made, 1)
                slot(1, 3)
                if q:
                    m.need(pe, ay_ready, s)
                    m.need(pe, deg_summed, s)
                    for n in range(ROWS):
                        last = pe.transpose(B[1][:, col(n)], yv[o][:, n, :, :], ident)
                    last.then_inc(v1_turned, 1)
                slot(1, 4)
                if q:
                    m.need(pe, a4_ready, s)
                    square(a4[o]).then_inc(a8_made, 1)
                    m.need(pe, v1_ready, s)
                    for n in range(ROWS):
                        last = pe.matmul(B[1][:, col(n)], yv[o][:, n, :, :], a2[:, col(n)], start=True, stop=True)
                    last.then_inc(v23_made, 1)
                    m.need(pe, z_ready[0], done(s, 0, 0))
                    low(0, o)
                    low(1, o)
                    m.need(pe, z_ready[1], done(s, 1, RULE))
                    low(2, o)
                    low(3, o).then_inc(low_used, 1)
                    m.need(pe, v23_ready, s)
                if p:
                    m.need(pe, diag_added, s + 1)
                    for n in range(ROWS):
                        last = pe.transpose(B[1][:, col(n)], rem[:, col(n)], ident)
                    last.then_inc(m_turned, 1)
                if q:
                    high(0, o)
                    high(1, o)
                    m.need(pe, a8_ready, s)
                slot(0, 0)
                if r:
                    m.need(pe, ay_ready if q else x3_ready[0], s if q else s - 1)
                    turn_z(s, 1)
                if live(s, 0, GROUPS - 1):
                    turn_y(s + 1, o)
                slot(0, 1)
                if p:
                    m.need(pe, b_ready, s + 1)
                    m.need(pe, cor_ready, s + 1)
                    for n in range(ROWS):
                        last = pe.transpose(B[2][:, col(n)], cor[:, col(n)], ident)
                    last.then_inc(b_turned, 1)
                slot(0, 2)
                if q:
                    high(2, o)
                slot(0, 3)
                if q:
                    high(3, o)
                slot(0, 4)
                if q:
                    m.need(pe, x3_ready[1], s - 1)
                    turn_z(s, 0)
            turn_y(0, 0)
            over_steps(pe, emit)


def layer3(nc, m, args, out):
    ident = m.k("ident", 128)
    ident64 = ident[0:C, 0:C]
    KINDS = 15
    COLS = 8
    STEPS3 = L // COLS
    m.arena_at = CH
    ws = m.take(KINDS * C, C)
    wm = m.take(C, C)
    bm = m.take(C, 1)
    wsT = m.take(KINDS * C, C)
    w = m.take(KINDS * C, C)
    spread_scale = m.take(C, C)
    both = m.take(C)
    rows_x, cols_x, diag_raw, diag_x = (m.take(L, C) for _ in range(4))
    mean_diag, mean_all, mean_diag2 = (m.take(1, C) for _ in range(3))
    of_row, of_col = m.take(C), m.take(C)
    diag_ret, diag_out = m.take(C), m.take(C)
    xx = [m.take(COLS * L) for _ in range(2)]
    before = [m.take(COLS * C) for _ in range(2)]
    ready = [m.take(COLS * C) for _ in range(2)]
    s_flat = m.nat[0:1, :]
    S = lambda name: m.sem(f"l3_{name}")
    B = m.bank
    kind = lambda k: w[:, (k - 1) * C:k * C]
    by_col = lambda t: t.rearrange("p (j x) -> p j x", j=COLS)
    with nc.Block() as block:

        @block.sync
        def _(sp):
            sp.dma_start(ws.rearrange("d (k e) -> d k e", k=KINDS), args["L3_conv_Ws"].rearrange("k d e -> d k e")).then_inc(S("loaded"), 16)
            sp.dma_start(wm, args["L3_conv_Wm"]).then_inc(S("loaded"), 16)
            sp.dma_start(bm, args["L3_conv_bm"].rearrange("(a c) -> a c", a=1)).then_inc(S("loaded"), 16)
            sp.wait_ge(S("of_col"), 1)
            sp.dma_start(s_flat.rearrange("a (j c) -> a j c", c=C), of_col).then_inc(S("flattened"), 16)
            sp.wait_ge(S("flattened"), 16)

        @block.scalar
        def _(act):
            act.wait_ge(S("ws_turned"), 2)
            act.activation(wsT[:, 512:KINDS * C], B[1][0:C, 0:KINDS * C - 512], ACT.Copy).then_inc(S("copied_upper"), 1)
            act.wait_ge(S("w_made"), 2)
            act.activation(w[:, 512:KINDS * C], B[3][0:C, 0:KINDS * C - 512], ACT.Copy).then_inc(S("copied_upper"), 1)

        @block.vector
        def _(dve):
            step = m.chain(dve, "dve")
            step(dve.tensor_reduce(cols_x, m.colsum.rearrange("p (r c) -> p c r", r=ROWS), AX.X, ALU.add))
            step(dve.tensor_scalar(cols_x, cols_x, 1.0 / L, None, ALU.mult))
            step(dve.tensor_scalar(rows_x, m.cells[:, :], 1.0 / L, None, ALU.mult))
            step(dve.tensor_scalar(rows_x, rows_x, m.scale[0:C, :], m.shift[:, :], ALU.mult, ALU.add))
            step(dve.tensor_copy(diag_raw, m.img[0:C, PW + 1:L * (PW + 1) + 1:PW + 1]))
            step(dve.tensor_scalar(diag_x, diag_raw, m.scale[0:C, :], m.shift[:, :], ALU.mult, ALU.add))
            step(dve.tensor_reduce(mean_diag, diag_x, AX.X, ALU.add))
            step(dve.tensor_reduce(mean_all, rows_x, AX.X, ALU.add))
            step(dve.tensor_scalar(mean_diag2, mean_diag, 2.0 / L, None, ALU.mult))
            step(dve.tensor_scalar(mean_diag, mean_diag, 1.0 / L, None, ALU.mult))
            step(dve.tensor_scalar(mean_all, mean_all, 1.0 / L, None, ALU.mult))
            step(dve.tensor_scalar(spread_scale, ident64, m.scale[0:C, :], None, ALU.mult))
            dve.tensor_scalar(cols_x, cols_x, m.scale[0:C, :], m.shift[:, :], ALU.mult, ALU.add).then_inc(S("means_ready"), 1)
            dve.wait_ge(S("ws_turned"), 1)
            dve.tensor_copy(wsT[:, 0:512], B[0][0:C, :]).then_inc(S("copied_lower"), 1)
            dve.wait_ge(S("w_made"), 1)
            dve.tensor_copy(w[:, 0:512], B[2][0:C, :]).then_inc(S("copied_lower"), 1)
            dve.wait_ge(S("of_col_made"), 1)
            dve.tensor_copy(of_col, B[5][:, 0:C]).then_inc(S("of_col"), 1)
            dve.wait_ge(S("terms_made"), 1)
            dve.tensor_copy(of_row, B[6][:, 0:C])
            dve.tensor_copy(both, B[7][:, 0:C])
            step(dve.tensor_copy(diag_ret, B[0][:, 0:C]))
            dve.scalar_tensor_tensor(out=diag_out, in0=diag_ret, scalar=0.0, in1=B[1][:, 0:C], op0=ALU.max, op1=ALU.add).then_inc(S("diag_ready"), 1)

        @block.tensor
        def _(pe):
            pe.wait_ge(S("loaded"), 16 * 3)
            for half, ks in enumerate((range(0, 8), range(8, KINDS))):
                for k in ks:
                    at = (k - 8 * half) * C
                    last = pe.transpose(B[half][0:C, at:at + C], ws[:, k * C:(k + 1) * C], ident64)
                last.then_inc(S("ws_turned"), 1)
            for half, ks in enumerate((range(0, 8), range(8, KINDS))):
                pe.wait_ge(S("copied_upper" if half else "copied_lower"), 1)
                for k in ks:
                    at = (k - 8 * half) * C
                    last = pe.matmul(B[2 + half][0:C, at:at + C], wsT[:, k * C:(k + 1) * C], wm, start=True, stop=True)
                last.then_inc(S("w_made"), 1)

            def total(bank, terms):
                for n, (vector, weights) in enumerate(terms):
                    last = pe.matmul(bank[:, 0:C], vector, weights, start=(n == 0), stop=(n == len(terms) - 1))
                return last

            everywhere = lambda t: t.to_broadcast([C, L])
            pe.wait_ge(S("means_ready"), 1)
            pe.wait_ge(S("copied_lower"), 2)
            pe.wait_ge(S("copied_upper"), 2)
            total(B[5], [(rows_x, kind(7)), (cols_x, kind(9)), (diag_x, kind(13))]).then_inc(S("of_col_made"), 1)
            total(B[6], [(rows_x, kind(6)), (cols_x, kind(8)), (diag_x, kind(12)), (everywhere(mean_diag2), kind(14)),
                         (everywhere(m.shift[:, :]), kind(10)), (everywhere(m.shift[:, :]), kind(11)), (m.one[:, :], bm)])
            pe.matmul(B[7][0:C, 0:C], spread_scale, kind(10), start=True, stop=True)
            pe.matmul(B[7][C:128, 0:C], spread_scale, kind(11), start=True, stop=True)
            total(B[0], [(diag_x, kind(k)) for k in (10, 11, 12, 13, 1)] + [(rows_x, kind(k)) for k in (6, 7, 3)]
                  + [(cols_x, kind(k)) for k in (8, 9, 4)]
                  + [(everywhere(mean_diag2), kind(14)), (everywhere(mean_diag), kind(2)), (everywhere(mean_all), kind(5)),
                     (m.one[:, :], bm)])
            pe.transpose(B[1][:, 0:C], diag_raw, ident64).then_inc(S("terms_made"), 1)

    top_ready, low_ready, ret_made, added, out_ready = (
        S(n) for n in ("top_ready", "low_ready", "ret_made", "added", "out_ready"))
    sent = [S("sent_even"), S("sent_odd")]

    def over_steps(eng, emit):
        for t in range(2):
            emit(t, t, 0)
        with eng.Fori(0, (STEPS3 - 2) // 2, 1) as it:
            for b in range(2):
                emit(it * 2 + (2 + b), b, it + 1)

    with nc.Block() as block:

        @block.gpsimd
        def _(pool):
            def emit(t, b, turn):
                m.need(pool, ret_made, t - 1)
                pool.tensor_copy(by_col(xx[b][0:C, :]), m.img3[0:C, 1:L + 1, ds(t * COLS + 1, COLS)].rearrange("p i j -> p j i")).then_inc(top_ready, 1)
            over_steps(pool, emit)

        @block.scalar
        def _(act):
            def emit(t, b, turn):
                m.need(act, ret_made, t - 1)
                act.activation(by_col(xx[b][C:128, :]), m.inner(t * COLS, COLS), ACT.Copy).then_inc(low_ready, 1)
            over_steps(act, emit)

        @block.tensor
        def _(pe):
            def emit(t, b, turn):
                m.need(pe, top_ready, t + 1)
                m.need(pe, low_ready, t + 1)
                m.need(pe, out_ready, t - 1)
                pe.matmul(B[b][:, :], m.one[:, :], s_flat[:, ds(t * COLS * C, COLS * C)], start=True, stop=False, skip_group_check=True)
                for j in range(COLS):
                    pe.matmul(B[b][:, j * C:(j + 1) * C], xx[b][:, j * L:(j + 1) * L], both, start=False, stop=True, skip_group_check=True)
                for j in range(COLS):
                    last = pe.transpose(B[2 + b][:, j * C:(j + 1) * C], xx[b][0:C, j * L:(j + 1) * L], ident64)
                last.then_inc(ret_made, 1)
            over_steps(pe, emit)

        @block.vector
        def _(dve):
            def emit(t, b, turn):
                m.need(dve, ret_made, t + 1)
                dve.tensor_tensor(by_col(before[b]), by_col(B[b][:, :]), of_row.unsqueeze(1).broadcast_to([128, COLS, C]),
                                  ALU.add).then_inc(added, 1)
                m.need(dve, added, t + 1)
                m.need(dve, sent[b], turn * 16)
                dve.scalar_tensor_tensor(out=ready[b], in0=before[b], scalar=0.0, in1=B[2 + b][:, :],
                                         op0=ALU.max, op1=ALU.add).then_inc(out_ready, 1)
            over_steps(dve, emit)

        @block.sync
        def _(sp):
            def emit(t, b, turn):
                m.need(sp, out_ready, t + 1)
                sp.dma_start(out.rearrange("b i j c -> (b i) j c")[:, ds(t * COLS, COLS), :], by_col(ready[b])).then_inc(sent[b], 16)
            over_steps(sp, emit)
            for b in range(2):
                sp.wait_ge(sent[b], 16 * STEPS3 // 2)
            sp.dma_start(out.rearrange("b i j c -> (b i j) c")[0:L * L:L + 1, :], diag_out).then_inc(S("diag_sent"), 16)
            sp.wait_ge(S("diag_sent"), 16)


def build(nc, args, out):
    with ExitStack() as ctx:
        m = Memory(nc, ctx)
        load_and_prepare(nc, m, args)
        m.open_arena(); m.arena_at = 9000
        group_norm(nc, m, 0)
        layer0_norm(nc, m)
        layer0_attention(nc, m, args)
        m.open_arena()
        group_norm(nc, m, 1)
        layer1(nc, m, args)
        m.open_arena()
        group_norm(nc, m, 2)
        layer2(nc, m)
        m.arena_at = CH
        group_norm(nc, m, 3)
        layer3(nc, m, args, out)


_INS = ['x', 'L0_conv_gamma', 'L0_conv_beta', 'L0_conv_Wq', 'L0_conv_Wk', 'L0_conv_Wv', 'L0_conv_Wb', 'L0_conv_Wg',
        'L0_conv_bg', 'L0_conv_Wo', 'L0_conv_bo', 'L1_conv_qkv_w', 'L1_conv_qkv_b', 'L1_conv_wo_w', 'L1_conv_wo_b',
        'L1_conv_dw_w', 'L1_conv_dw_b', 'L2_conv_theta_w', 'L2_conv_alpha_raw', 'L3_conv_Ws', 'L3_conv_Wm', 'L3_conv_bm']


def kernel(**inputs):
    import concourse.bacc as bacc
    from concourse.bass_utils import run_bass_kernel_spmd

    nc = bacc.Bacc("TRN2", target_bir_lowering=False, num_devices=1)
    arrays, args = {}, {}
    for name in _INS:
        a = np.ascontiguousarray(inputs[name])
        arrays[f"in_{name}"] = a
        args[name] = nc.dram_tensor(f"in_{name}", a.shape, mybir.dt.from_np(a.dtype), kind="ExternalInput").ap()
    arrays["in_constants"] = constants()
    args["constants"] = nc.dram_tensor("in_constants", (128, NCONST), F32, kind="ExternalInput").ap()
    out = nc.dram_tensor("out", (1, L, L, C), F32, kind="ExternalOutput").ap()
    build(nc, args, out)
    result = run_bass_kernel_spmd(nc, [arrays], core_ids=[0])
    return result.results[0]["out"]
```

```python
from contextlib import ExitStack
from math import comb

import concourse.bass as bass
import numpy as np
from concourse import mybir

F32 = mybir.dt.float32
BF16 = mybir.dt.bfloat16
ALU = mybir.AluOpType
ACT = mybir.ActivationFunctionType
AX = mybir.AxisListType
ds = bass.ds

L = 128
C = 64
HEADS, HD = 4, 32
ROWS = 4
GROUPS = L // ROWS
CH = ROWS * L
NWIN, KVW = 8, 4
TOPW = 4
QHEADS, QD = 8, 8
CELL = (L // NWIN // KVW) * (L // KVW)
TOPK = 8
STEPS, T_END = 8, 0.2
DEG = 4 * STEPS
H_STEP = T_END / STEPS
BABY = 4
GIANTS = DEG // BABY
BIG = 3.0e38
PW = L + 2

CONSTS = {}
_at = 0
for _name, _n in (("ident", 128), ("pair", 64), ("expand", 128), ("headmask", 64), ("earlier", 64), ("rk", DEG + 1)):
    CONSTS[_name] = slice(_at, _at + _n)
    _at += _n
NCONST = _at
CONSTS["minus"] = slice(CONSTS["pair"].start, CONSTS["pair"].start + L + 2)


def constants():
    k = np.zeros((128, NCONST), np.float32)
    k[:, CONSTS["ident"]] = np.eye(128)
    c = np.arange(C)
    k[:C, CONSTS["pair"]] = 0.5 * (c[:, None] // 2 == c[None, :] // 2)
    k[:NWIN, CONSTS["expand"]] = np.arange(NWIN)[:, None] == np.arange(128)[None, :] // (KVW * KVW)
    k[:C, CONSTS["headmask"]] = c[:, None] // QD == c[None, :] // QD
    k[:, CONSTS["earlier"]] = (np.arange(8)[None, :] < np.arange(8)[:, None]).reshape(1, 64)
    p = np.ones(1)
    for _ in range(STEPS):
        p = np.convolve(p, [1.0, 1.0, 1 / 2, 1 / 6, 1 / 24])
    for m in range(DEG + 1):
        for j in range(DEG + 1 - m):
            k[m, CONSTS["rk"].start + j] = p[m + j] * comb(m + j, j)
    k[C, CONSTS["minus"]] = -np.pad(np.ones(L), 1)
    return k


class Chain:

    def __init__(self, sem):
        self.eng, self.sem, self.n = None, sem, 0

    def __call__(self, ins):
        ins.then_inc(self.sem, 1)
        self.n += 1
        self.eng.wait_ge(self.sem, self.n)




class Memory:

    ARENA_COLS = 8280

    def __init__(self, nc, ctx):
        self.nc, self.ctx, self.sems, self.chains = nc, ctx, {}, {}

        def sb(name, shape):
            return ctx.enter_context(nc.sbuf_tensor(name, shape, F32))

        self.img = sb("img", [128, PW * PW])
        self.flat = sb("flat", [C + 1, L * L])
        self.nat = sb("nat", [L, L * C])
        self.arena = sb("arena", [128, self.ARENA_COLS])
        self.const = sb("const", [128, NCONST])
        self.w0 = sb("w0", [C + 1, 4 * 128])
        self.w0b = sb("w0b", [C + 1, 96])
        self.theta = sb("theta", [128, 2, 512])
        self.theta_top = sb("theta_top", [C, C])
        self.stats = sb("stats", [C, GROUPS * 6])
        self.scale = sb("scale", [C + 1, 1])
        self.shift = sb("shift", [C, 1])
        self.cells = sb("cells", [C, GROUPS * KVW])
        self.eps = sb("eps", [128, 1])
        self.bo = sb("bo", [C, 1])
        self.parts = [ctx.enter_context(nc.sbuf_tensor(f"parts{b}", [3, 512], BF16)) for b in range(2)]
        self.part_sum = ctx.enter_context(nc.sbuf_tensor("part_sum", [3, 128], BF16))
        self.rounded = ctx.enter_context(nc.sbuf_tensor("rounded", [128, C], BF16))
        self.one = sb("one", [1, 128])
        self.bank = [ctx.enter_context(nc.psum_tensor(f"bank{i}", [128, 512], F32)) for i in range(4)]
        self.quad = ctx.enter_context(nc.psum_tensor("quad", [128, 4, 512], F32))
        self.bank += [self.quad[:, i, :] for i in range(4)]
        self.img3 = self.img[:, :].rearrange("p (r c) -> p r c", c=PW)
        self.nat3 = self.nat[:, :].rearrange("p (i c) -> p i c", c=C)
        self.arena_at = 0

    def sem(self, name):
        if name not in self.sems:
            self.sems[name] = self.ctx.enter_context(self.nc.semaphore(name))
        return self.sems[name]

    def chain(self, eng, name):
        if name not in self.chains:
            self.chains[name] = Chain(self.sem(name + "_chain"))
        self.chains[name].eng = eng
        return self.chains[name]

    def need(self, eng, sem, value):
        if isinstance(value, int):
            if value > 0:
                eng.wait_ge(sem, value)
            return
        eng.wait_ge(sem, value)
        eng.sem_inc(self.sem("passed"))

    def k(self, name, rows):
        return self.const[0:rows, CONSTS[name]]

    def inner(self, row, rows=ROWS):
        return self.img3[0:C, ds(row + 1, rows), 1:L + 1]

    def open_arena(self):
        self.arena_at = 0

    def take(self, cols, rows=128):
        assert self.arena_at + cols <= self.ARENA_COLS, "the arena is full"
        at = self.arena_at
        self.arena_at += cols
        return self.arena[0:rows, at:at + cols]


def load_and_prepare(nc, m, args):
    S = m.sem
    ident = m.k("ident", 128)
    ident64 = ident[0:C, 0:C]
    m.open_arena()
    w_raw = m.take(4 * 128, C)
    wb_raw = m.take(HEADS, C)
    fold0 = m.take(C + 1, C)
    gamma = m.take(1, C)
    bg_row = m.take(128, C + 1)
    theta_raw = m.take(C, C)
    alpha = m.take(8)
    powers = m.take(DEG + 1)
    power_col = m.take(1)
    picked = m.take(DEG + 1)
    coef = m.take(DEG + 1)
    turn = m.take(2 * C, C)
    pw = m.take((DEG + 1) * C).rearrange("p (j e) -> p j e", e=C)
    PIECES = 4
    per = L // PIECES
    vectors = [
        (w_raw[:, 0:128], args["L0_conv_Wq"]), (w_raw[:, 128:256], args["L0_conv_Wk"]),
        (w_raw[:, 256:384], args["L0_conv_Wv"]), (w_raw[:, 384:512], args["L0_conv_Wg"]),
        (wb_raw, args["L0_conv_Wb"]),
        (gamma, args["L0_conv_gamma"].rearrange("(c a) -> c a", a=1)),
        (fold0[:, C:C + 1], args["L0_conv_beta"].rearrange("(c a) -> c a", a=1)),
        (bg_row[C:C + 1, :], args["L0_conv_bg"].rearrange("(a c) -> a c", a=1)),
        (m.bo[:, :], args["L0_conv_bo"].rearrange("(c a) -> c a", a=1)),
        (theta_raw, args["L2_conv_theta_w"]),
        (alpha[:, 0:1], args["L2_conv_alpha_raw"].rearrange("(a c) -> a c", a=1).to_broadcast([128, 1])),
    ]
    weights_in, consts_in, copied, chunk_turned = S("a_weights_in"), S("a_consts_in"), S("a_copied"), S("a_chunk_turned")
    piece_in = [S(f"a_x_in{n}") for n in range(PIECES)]
    x_nat = args["x"].rearrange("b i j c -> (b j) i c")
    DOUBLINGS = [1, 2, 4, 8, 16]
    with nc.Block() as block:

        @block.sync
        def _(sp):
            sp.dma_start(m.const[:, :], args["constants"]).then_inc(consts_in, 16)
            for dst, src in vectors:
                sp.dma_start(dst, src).then_inc(weights_in, 16)
            for n in range(PIECES):
                sp.dma_start(m.nat3[:, n * per:(n + 1) * per, :], x_nat[:, n * per:(n + 1) * per, :]).then_inc(piece_in[n], 16)

        @block.gpsimd
        def _(pool):
            step = m.chain(pool, "pool")
            step(pool.memset(m.img3[0:C, 0, :], 0.0))
            step(pool.memset(m.img3[0:C, L + 1, :], 0.0))
            step(pool.memset(m.img3[C:128, L, :], 0.0))
            step(pool.memset(m.img3[0:C, 1:L + 1, 0:1], 0.0))
            step(pool.memset(m.img3[0:C, 1:L + 1, L + 1:L + 2], 0.0))
            step(pool.memset(m.flat[C:C + 1, :], 1.0))
            step(pool.memset(m.eps[:, :], 1e-5))
            step(pool.memset(m.one[:, :], 1.0))
            step(pool.memset(m.scale[C:C + 1, :], 1.0))

        @block.scalar
        def _(act):
            act.wait_ge(weights_in, 16 * len(vectors))
            step = m.chain(act, "act")
            step(act.activation(alpha[:, 1:2], alpha[:, 0:1], ACT.Abs))
            step(act.activation(alpha[:, 2:3], alpha[:, 1:2], ACT.Exp, scale=-1.0))
            act.activation(alpha[:, 3:4], alpha[:, 2:3], ACT.Ln, bias=1.0).then_inc(S("a_ln"), 1)
            for q in range(GROUPS):
                act.wait_ge(chunk_turned, q + 1)
                act.activation(m.inner(ROWS * q), m.bank[q % 4][0:C, :].rearrange("p (r c) -> p r c", c=L),
                               ACT.Copy).then_inc(copied, 1)

        @block.vector
        def _(dve):
            step = m.chain(dve, "dve")

            def measure_piece(p):
                for q in range(p * per // ROWS, (p + 1) * per // ROWS):
                    dve.wait_ge(copied, q + 1)
                    dve.bn_stats(m.stats[:, 6 * q:6 * q + 6], m.inner(ROWS * q))

            dve.wait_ge(consts_in, 16)
            dve.wait_ge(weights_in, 16 * len(vectors))
            dve.tensor_scalar(fold0[:, 0:C], ident64, gamma, None, ALU.mult).then_inc(S("a_fold0"), 1)
            dve.wait_ge(S("a_ln"), 1)
            step(dve.tensor_scalar(alpha[:, 4:5], alpha[:, 0:1], 0.0, alpha[:, 3:4], ALU.max, ALU.add))
            step(dve.tensor_scalar(alpha[:, 5:6], alpha[:, 4:5], 2.0, None, ALU.min))
            step(dve.memset(powers[:, 0:1], 1.0))
            step(dve.tensor_scalar(powers[:, 1:2], alpha[:, 5:6], H_STEP, None, ALU.mult))
            have = 2
            while have < DEG + 1:
                n = min(have - 1, DEG + 1 - have)
                step(dve.tensor_scalar(powers[:, have:have + n], powers[:, 1:1 + n], powers[:, have - 1:have], None, ALU.mult))
                have += n
            n = DEG + 1
            step(dve.tensor_tensor(picked[0:n, :], powers[0:n, :], ident[0:n, 0:n], ALU.mult))
            dve.tensor_reduce(power_col[0:n, :], picked[0:n, :], AX.X, ALU.add).then_inc(S("a_power_col"), 1)
            step(dve.tensor_scalar(theta_raw, theta_raw, H_STEP, None, ALU.mult))
            step(dve.tensor_scalar(turn[:, C:2 * C], ident64, powers[0:C, 1:2], None, ALU.mult))
            step(dve.tensor_tensor(turn[:, 0:C], theta_raw, turn[:, C:2 * C], ALU.subtract))
            dve.tensor_copy(turn[:, C:2 * C], turn[:, 0:C]).then_inc(S("a_turn"), 1)
            dve.wait_ge(S("a_w0_made"), 1)
            step(dve.tensor_copy(m.w0[:, :], m.bank[4][0:C + 1, :]))
            dve.tensor_scalar(m.w0[:, 0:128], m.w0[:, 0:128], float(1.0 / np.sqrt(HD)), None, ALU.mult)
            dve.tensor_tensor(m.w0[C:C + 1, 384:512], m.w0[C:C + 1, 384:512], bg_row[C:C + 1, :], ALU.add)
            dve.wait_ge(S("a_w0b_made"), 1)
            dve.memset(m.w0b[:, 0:32], 0.0)
            dve.memset(m.w0b[:, 32 + HEADS:], 0.0)
            dve.tensor_copy(m.w0b[:, 32:32 + HEADS], m.bank[5][0:C + 1, 0:HEADS])
            dve.wait_ge(S("a_coef_made"), 1)
            dve.tensor_copy(coef, m.bank[6][:, 0:DEG + 1]).then_inc(S("a_coef"), 1)
            step(dve.tensor_copy(pw[0:C, 0, :], ident64))
            step(dve.tensor_copy(pw[C:128, 0, :], ident[C:128, C:128]))
            dve.wait_ge(S("a_first_power"), 1)
            dve.tensor_copy(pw[:, 1, :], m.bank[7][:, 0:C]).then_inc(S("a_powers"), 1)
            for i, d in enumerate(DOUBLINGS):
                if d > 1:
                    dve.wait_ge(S("a_power_turned"), i)
                    for half in range(2):
                        dve.tensor_copy(turn[:, half * C:(half + 1) * C], m.bank[7][0:C, 0:C]).then_inc(S("a_power_turn"), 1)
                for at in range(0, d, 8):
                    n = min(8, d - at)
                    dve.wait_ge(S("a_doubled"), i + 1 + (at > 0))
                    dve.tensor_copy(pw[:, d + 1 + at:d + 1 + at + n, :],
                                    m.bank[5 + (at > 0)][:, 0:n * C].rearrange("p (j e) -> p j e", e=C)).then_inc(S("a_powers"), 1)
                if 0 < i < PIECES:
                    measure_piece(i - 1)
            dve.wait_ge(S("a_powers"), 1 + len(DOUBLINGS) + 1)
            dve.wait_ge(S("a_coef"), 1)
            pairs = BABY // 2
            for odd, half in enumerate((slice(0, C), slice(C, 128))):
                of_half = lambda t: t.rearrange("p (g pair) e -> p g pair e", pair=pairs)
                dve.tensor_tensor(m.theta[half, :, :].rearrange("p pair (g e) -> p g pair e", e=C),
                                  of_half(pw[half, odd:DEG:2, :]),
                                  of_half(coef[half, odd:DEG:2].unsqueeze(2).broadcast_to([C, DEG // 2, C])), ALU.mult)
            dve.tensor_scalar(m.theta_top[:, :], pw[0:C, DEG, :], coef[0:C, DEG:DEG + 1], None, ALU.mult)
            measure_piece(PIECES - 1)

        @block.tensor
        def _(pe):
            def turn_piece(p):
                pe.wait_ge(piece_in[p], 16)
                for q in range(p * per // ROWS, (p + 1) * per // ROWS):
                    m.need(pe, copied, q - 3)
                    for r in range(ROWS):
                        last = pe.transpose(m.bank[q % 4][0:C, r * L:(r + 1) * L], m.nat3[:, ROWS * q + r, :], ident)
                    last.then_inc(chunk_turned, 1)

            pe.wait_ge(consts_in, 16)
            pe.wait_ge(S("a_fold0"), 1)
            pe.matmul(m.bank[4][0:C + 1, :], fold0, w_raw, start=True, stop=True).then_inc(S("a_w0_made"), 1)
            pe.matmul(m.bank[5][0:C + 1, 0:HEADS], fold0, wb_raw, start=True, stop=True).then_inc(S("a_w0b_made"), 1)
            pe.wait_ge(S("a_power_col"), 1)
            n = DEG + 1
            pe.matmul(m.bank[6][:, 0:n], power_col[0:n, :].to_broadcast([n, 128]), m.k("rk", n),
                      start=True, stop=True).then_inc(S("a_coef_made"), 1)
            pe.wait_ge(S("a_turn"), 1)
            pe.matmul(m.bank[7][:, 0:C], turn, ident64, start=True, stop=True).then_inc(S("a_first_power"), 1)
            pe.wait_ge(S("a_coef"), 1)
            for i, d in enumerate(DOUBLINGS):
                pe.wait_ge(S("a_powers"), i + 1)
                if d > 1:
                    pe.wait_ge(S("a_power_turn"), 2 * i)
                for at in range(0, d, 8):
                    n = min(8, d - at)
                    pe.matmul(m.bank[5 + (at > 0)][:, 0:n * C], turn, pw[0:C, 1 + at:1 + at + n, :],
                              start=True, stop=True).then_inc(S("a_doubled"), 1)
                if i + 1 < len(DOUBLINGS):
                    pe.wait_ge(S("a_powers"), i + 2)
                    pe.transpose(m.bank[7][0:C, 0:C], pw[0:C, 2 * d, :], ident64).then_inc(S("a_power_turned"), 1)
                if i > 0:
                    turn_piece(i - 1)

def group_norm(nc, m, layer, loads=(), loaded=None):
    mv, d, mg, e, std = (m.take(n, C) for n in (2, 1, 1, 1, 1))
    S = lambda name: m.sem("gn_" + name)
    acc = m.bank[0]
    with nc.Block() as block:

        @block.sync
        def _(sp):
            for dst, src in loads:
                sp.dma_start(dst, src).then_inc(loaded, 16)

        @block.vector
        def _(dve):
            step = m.chain(dve, "dve")
            dve.bn_aggr(mv, m.stats[:, :]).then_inc(S("mean"), 1)
            dve.wait_ge(S("group_mean"), layer + 1)
            step(dve.tensor_copy(mg, acc[0:C, 0:1]))
            step(dve.tensor_tensor(d, mv[:, 0:1], mg, ALU.subtract))
            dve.scalar_tensor_tensor(out=e, in0=d, scalar=d, in1=mv[:, 1:2], op0=ALU.mult, op1=ALU.add).then_inc(S("var"), 1)
            dve.wait_ge(S("std"), layer + 1)
            step(dve.reciprocal(m.scale[0:C, :], std))
            dve.scalar_tensor_tensor(out=m.shift[:, :], in0=mg, scalar=-1.0, in1=m.scale[0:C, :], op0=ALU.mult, op1=ALU.mult)

        @block.tensor
        def _(pe):
            pe.wait_ge(S("mean"), layer + 1)
            pe.matmul(acc[0:C, 0:1], m.k("pair", C), mv[:, 0:1], start=True, stop=True).then_inc(S("group_mean"), 1)
            pe.wait_ge(S("var"), layer + 1)
            pe.matmul(acc[0:C, 1:2], m.k("pair", C), e, start=True, stop=True).then_inc(S("group_var"), 1)

        @block.scalar
        def _(act):
            act.wait_ge(S("group_var"), layer + 1)
            act.activation(std, acc[0:C, 1:2], ACT.Sqrt, bias=m.eps[0:C, :]).then_inc(S("std"), 1)


def layer0_norm(nc, m):
    ident = m.k("ident", 128)
    m.open_arena()
    m.bias = m.take(HEADS * L)
    wide_scale, wide_shift = m.take(C), m.take(C)
    y = [m.take(ROWS * C).rearrange("p (r c) -> p r c", c=C) for _ in range(4)]
    mv = [m.take(2 * ROWS).rearrange("p (r s) -> p r s", s=2) for _ in range(2)]
    st = [m.take(6 * ROWS) for _ in range(2)]
    rstd = m.take(ROWS)
    std = [m.take(ROWS) for _ in range(2)]
    z = [m.take(ROWS * C).rearrange("p (r c) -> p r c", c=C) for _ in range(2)]
    S = lambda name: m.sem(f"z_{name}")
    y_scaled, y_ready, stats_ready, measured, std_ready = S("y_scaled"), S("y_ready"), S("stats_ready"), S("measured"), S("std_ready")
    rstd_ready, z_ready, z_turned, z_stored = S("rstd_ready"), S("z_ready"), S("z_turned"), S("z_stored")
    bias_made, bias_kept = S("bias_made"), S("bias_kept")
    LAG = 5
    UNROLL = 4
    SPAN = 32

    def over_chunks(eng, emit):
        for q in range(2 * UNROLL):
            emit(q, q % UNROLL)
        with eng.Fori(0, GROUPS // UNROLL - 2, 1) as it:
            for n in range(UNROLL):
                emit(it * UNROLL + (2 * UNROLL + n), n)
        for q in range(GROUPS, GROUPS + LAG):
            emit(q, q % UNROLL)

    def live(q, lo):
        return not isinstance(q, int) or lo <= q < GROUPS + lo

    def chunk(t, q, parity):
        return t.rearrange("p (i two x) -> p i two x", two=2, i=L // 2)[:, ds(2 * q - 2 * parity, ROWS), parity, :]

    with nc.Block() as block:

        @block.gpsimd
        def _(pool):
            def emit(q, n):
                if live(q, 0):
                    if isinstance(q, int) and q == 0:
                        pool.wait_ge(S("wide_ready"), 1)
                    m.need(pool, z_ready, q - 3)
                    pool.tensor_tensor(y[n], chunk(m.nat[:, :], q, n % 2), wide_scale.unsqueeze(1).broadcast_to([128, ROWS, C]),
                                       ALU.mult).then_inc(y_scaled, 1)
                    m.need(pool, y_scaled, q + 1)
                    pool.tensor_tensor(y[n], y[n], wide_shift.unsqueeze(1).broadcast_to([128, ROWS, C]), ALU.add).then_inc(y_ready, 1)
            over_chunks(pool, emit)

        @block.scalar
        def _(act):
            def emit(q, n):
                b = n % 2
                if live(q, 1):
                    m.need(act, measured, q)
                    act.activation(std[1 - b], mv[1 - b][:, :, 1], ACT.Sqrt, bias=m.eps[:, :]).then_inc(std_ready, 1)
                if live(q, 5) and b == 0:
                    m.need(act, bias_made, q - 4)
                    act.activation(m.nat[0:2 * SPAN, ds((q - 6) * ROWS * C, CH)], m.bank[2 + ((n + 2) % UNROLL) // 2][0:2 * SPAN, :],
                                   ACT.Copy).then_inc(bias_kept, 1)
                if live(q, 3):
                    m.need(act, z_turned, q - 2)
                    for odd in range(2):
                        last = act.activation(chunk(m.flat[0:C, :], q - 3, 1 - b)[:, odd:ROWS:2, :],
                                              m.bank[1 - b][odd * C:(odd + 1) * C, 0:2 * L].rearrange("p (r c) -> p r c", c=L), ACT.Copy)
                    last.then_inc(z_stored, 1)
            over_chunks(act, emit)

        @block.tensor
        def _(pe):
            pe.matmul(m.bank[6][:, 0:C], m.scale[0:C, :].to_broadcast([C, 128]), ident[0:C, 0:C], start=True, stop=True)
            pe.matmul(m.bank[6][:, C:2 * C], m.shift[:, :].to_broadcast([C, 128]), ident[0:C, 0:C],
                      start=True, stop=True).then_inc(S("wide_made"), 1)

            def emit(q, n):
                b = n % 2
                if live(q, 2):
                    m.need(pe, z_ready, q - 1)
                    m.need(pe, z_stored, q - 3)
                    for two in range(ROWS // 2):
                        last = pe.transpose(m.bank[b][:, two * L:(two + 1) * L], z[b][:, 2 * two:2 * two + 2, :], ident)
                    last.then_inc(z_turned, 1)
                if live(q, 4):
                    pair = m.bank[2 + n // 2]
                    m.need(pe, z_stored, q - 3)
                    at = (1 - b) * SPAN
                    pe.matmul(pair[0:2 * SPAN, :], m.w0b[:, at:at + 2 * SPAN], chunk(m.flat[:, :], q - 4, b),
                              start=(b == 0), stop=(b == 1)).then_inc(bias_made, 1)
            over_chunks(pe, emit)

        @block.vector
        def _(dve):
            dve.wait_ge(S("wide_made"), 1)
            dve.tensor_copy(wide_scale, m.bank[6][:, 0:C])
            dve.tensor_copy(wide_shift, m.bank[6][:, C:2 * C]).then_inc(S("wide_ready"), 1)

            def emit(q, n):
                b = n % 2
                if live(q, 0):
                    m.need(dve, y_ready, q + 1)
                    m.need(dve, measured, q - 1)
                    for r in range(ROWS):
                        last = dve.bn_stats(st[b][:, 6 * r:6 * r + 6], y[n][:, r, :])
                    last.then_inc(stats_ready, 1)
                if live(q, 1):
                    o = 1 - b
                    m.need(dve, std_ready, q)
                    m.need(dve, z_ready, q - 1)
                    dve.reciprocal(rstd, std[o]).then_inc(rstd_ready, 1)
                if live(q, 0):
                    m.need(dve, stats_ready, q + 1)
                    for r in range(ROWS):
                        last = dve.bn_aggr(mv[b][:, r, :], st[b][:, 6 * r:6 * r + 6])
                    last.then_inc(measured, 1)
                if live(q, 1):
                    m.need(dve, rstd_ready, q)
                    m.need(dve, z_turned, q - 2)
                    for r in range(ROWS):
                        last = dve.tensor_scalar(z[o][:, r, :], y[(n - 1) % UNROLL][:, r, :], mv[o][:, r, 0:1],
                                                 rstd[:, r:r + 1], ALU.subtract, ALU.mult)
                    last.then_inc(z_ready, 1)
            over_chunks(dve, emit)

        @block.sync
        def _(sp):
            sp.wait_ge(bias_kept, GROUPS // 2)
            for parity in range(2):
                for h in range(HEADS):
                    row = SPAN * parity + h
                    sp.dma_start(m.bias[parity:L:2, h * L:(h + 1) * L], m.nat[row:row + 1, :]).then_inc(S("bias_laid"), 16)
            sp.wait_ge(S("bias_laid"), 16 * 2 * HEADS)


def layer0_attention(nc, m, args):
    ident = m.k("ident", 128)
    m.arena_at = HEADS * L
    spare = [m.nat[:, i * 2048:(i + 1) * 2048] for i in range(4)]
    prob = [spare[0], spare[1]]
    qT = [spare[2][:, i * CH:(i + 1) * CH] for i in (0, 1)]
    th = spare[2][:, 3 * CH:4 * CH]
    v = [spare[3][:, i * CH:(i + 1) * CH] for i in (0, 1)]
    factor = spare[3][:, 2 * CH:3 * CH]
    gated = spare[3][:, 3 * CH:4 * CH]
    kb = [m.take(ROWS * HEADS * L).rearrange("p (r h k) -> p r h k", r=ROWS, h=HEADS) for _ in range(2)]
    zs = [m.take(CH, C + 1) for _ in range(2)]
    pT = [m.take(HEADS * L) for _ in range(2)]
    wo = m.take(C)
    least = [m.take(ROWS * HEADS) for _ in range(2)]
    total = [m.take(ROWS * HEADS) for _ in range(2)]
    rtotal = m.take(ROWS * HEADS)
    rwide = m.take(CH)
    S = lambda name: m.sem(f"l0_{name}")
    z_staged, wo_ready = S("z_staged"), S("wo_ready")
    q_made, k_made, v_made, g_made = S("q_made"), S("k_made"), S("v_made"), S("g_made")
    q_ready, v_ready, th_ready, k_low, k_high = S("q_ready"), S("v_ready"), S("th_ready"), S("k_low"), S("k_high")
    scores_made, shifted, probs_ready = S("scores_made"), S("shifted"), S("probs_ready")
    probs_turned, turned_even, turned_odd = S("probs_turned"), S("turned_even"), S("turned_odd")
    av_made, rtotal_ready, rwide_ready, r_turned = S("av_made"), S("rtotal_ready"), S("rwide_ready"), S("r_turned")
    factor_ready, gated_ready, out_made, x1_ready = S("factor_ready"), S("gated_ready"), S("out_made"), S("x1_ready")
    STEPS0 = GROUPS + 2
    PEEL = 3

    def over_steps(eng, emit):
        for g in range(PEEL + 1):
            emit(g, g % 2)
        with eng.Fori(0, (GROUPS - PEEL - 3) // 2, 1) as it:
            for b in range(2):
                emit(it * 2 + (PEEL + 1 + b), b)
        for g in range(GROUPS - 2, STEPS0):
            emit(g, g % 2)

    def live(g, lo, hi):
        return not isinstance(g, int) or lo <= g < hi

    def rows(t):
        return t.rearrange("p (r x) -> p r x", r=ROWS)

    def k_blocks(b, heads):
        for h in heads:
            part = slice(h * HD, (h + 1) * HD)
            yield kb[b][part, :, h, :], rows(m.bank[2][part, :])

    with nc.Block() as block:

        @block.sync
        def _(sp):
            sp.dma_start(wo, args["L0_conv_Wo"]).then_inc(wo_ready, 16)

        @block.gpsimd
        def _(pool):
            step = m.chain(pool, "pool")
            for b in range(2):
                step(pool.memset(kb[b], 0.0))
            pool.sem_inc(S("kb_zeroed"), 1)

            def stage_z(g, b):
                m.need(pool, v_made, g - 1)
                pool.tensor_copy(zs[b], m.flat[:, ds(g * CH, CH)]).then_inc(z_staged, 1)

            def emit(g, b):
                if live(g, 0, GROUPS - 1):
                    stage_z(g + 1, 1 - b)
                if live(g, 1, GROUPS + 1):
                    m.need(pool, rtotal_ready, g)
                    m.need(pool, r_turned, g - 1)
                    m.need(pool, z_staged, g + 2 if live(g, 0, GROUPS - 1) else GROUPS)
                    pool.tensor_copy(rwide.rearrange("p (x d) -> p x d", d=HD),
                                     rtotal.unsqueeze(2).broadcast_to([128, ROWS * HEADS, HD])).then_inc(rwide_ready, 1)
            stage_z(0, 0)
            over_steps(pool, emit)

        @block.scalar
        def _(act):
            def copy_q(g, b):
                m.need(act, q_made, g + 1)
                act.activation(qT[b], m.bank[2][:, :], ACT.Copy).then_inc(q_ready, 1)

            def copy_k(g, b):
                m.need(act, k_made, g + 1)
                for to, of in k_blocks(b, (0, 1)):
                    last = act.activation(to, of, ACT.Copy)
                last.then_inc(k_low, 1)

            def turn_even(g, r):
                m.need(act, probs_turned, (g - 1) * ROWS + (r + 1))
                m.need(act, av_made, (g - 1) * ROWS + (r - 1))
                act.activation(pT[0], m.bank[0][:, :], ACT.Copy).then_inc(turned_even, 1)

            def exponentials(g, b, r):
                m.need(act, shifted, g * ROWS + (r + 1))
                for h in range(HEADS):
                    t = prob[b][:, (r * HEADS + h) * L:(r * HEADS + h + 1) * L]
                    last = act.activation(t, t, ACT.Exp, scale=-1.0, bias=least[b][:, r * HEADS + h:r * HEADS + h + 1],
                                          accum_out=total[b][:, r * HEADS + h:r * HEADS + h + 1])
                last.then_inc(probs_ready, 1)

            def emit(g, b):
                own, before = live(g, 0, GROUPS), live(g, 1, GROUPS + 1)
                if own:
                    exponentials(g, b, 0)
                if before:
                    turn_even(g, 0)
                if live(g, 0, GROUPS - 1):
                    copy_k(g + 1, 1 - b)
                if own:
                    exponentials(g, b, 1)
                if live(g, 0, GROUPS - 1):
                    copy_q(g + 1, 1 - b)
                if before:
                    turn_even(g, 2)
                if own:
                    exponentials(g, b, 2)
                    exponentials(g, b, 3)
                    m.need(act, g_made, g + 1)
                    m.need(act, factor_ready, g)
                    act.activation(th, m.bank[0][:, :], ACT.Tanh, scale=0.5).then_inc(th_ready, 1)
            act.wait_ge(S("kb_zeroed"), 1)
            copy_k(0, 0)
            copy_q(0, 0)
            over_steps(act, emit)

        @block.vector
        def _(dve):
            dve.wait_ge(wo_ready, 16)
            dve.tensor_scalar(wo, wo, 0.5, None, ALU.mult).then_inc(S("wo_halved"), 1)

            def copy_k(g, b):
                m.need(dve, k_made, g + 1)
                for to, of in k_blocks(b, (2, 3)):
                    last = dve.tensor_copy(to, of)
                last.then_inc(k_high, 1)

            def shift_row(g, b, r):
                for h in range(HEADS):
                    at = (r * HEADS + h) * L
                    last = dve.tensor_tensor_reduce(prob[b][:, at:at + L], m.quad[:, r, h * L:(h + 1) * L],
                                                    m.bias[:, h * L:(h + 1) * L], -1.0, BIG, ALU.add, ALU.min,
                                                    least[b][:, r * HEADS + h:r * HEADS + h + 1])
                last.then_inc(shifted, 1)

            def turn_odd(g, r):
                m.need(dve, probs_turned, (g - 1) * ROWS + (r + 1))
                m.need(dve, av_made, (g - 1) * ROWS + (r - 1))
                dve.tensor_copy(pT[1], m.bank[1][:, :]).then_inc(turned_odd, 1)

            def emit(g, b):
                own, before, older = live(g, 0, GROUPS), live(g, 1, GROUPS + 1), live(g, 2, GROUPS + 2)
                if own:
                    m.need(dve, scores_made, g * ROWS + 1)
                    m.need(dve, probs_turned, (g - 1) * ROWS)
                    shift_row(g, b, 0)
                    m.need(dve, scores_made, g * ROWS + 2)
                    shift_row(g, b, 1)
                if before:
                    m.need(dve, probs_ready, g * ROWS)
                    m.need(dve, rwide_ready, g - 1)
                    dve.reciprocal(rtotal, total[1 - b]).then_inc(rtotal_ready, 1)
                if older:
                    m.need(dve, out_made, g - 1)
                    inner = m.inner((g - 2) * ROWS)
                    dve.scalar_tensor_tensor(out=inner, in0=rows(m.bank[3][0:C, :]), scalar=m.bo[:, :], in1=inner,
                                             op0=ALU.add, op1=ALU.add).then_inc(x1_ready, 1)
                if live(g, 0, GROUPS - 1):
                    copy_k(g + 1, 1 - b)
                if own:
                    m.need(dve, scores_made, g * ROWS + 3)
                    shift_row(g, b, 2)
                if before:
                    turn_odd(g, 1)
                if own:
                    m.need(dve, scores_made, g * ROWS + 4)
                    shift_row(g, b, 3)
                if before:
                    m.need(dve, r_turned, g)
                    m.need(dve, th_ready, g)
                    dve.scalar_tensor_tensor(out=factor, in0=th, scalar=1.0, in1=m.bank[2][:, :],
                                             op0=ALU.add, op1=ALU.mult).then_inc(factor_ready, 1)
                    turn_odd(g, 3)
                if own:
                    m.need(dve, v_made, g + 1)
                    m.need(dve, av_made, (g - 1) * ROWS)
                    dve.tensor_copy(v[b], m.bank[2][:, :]).then_inc(v_ready, 1)
                if before:
                    m.need(dve, av_made, g * ROWS)
                    m.need(dve, factor_ready, g)
                    m.need(dve, out_made, g - 1)
                    dve.tensor_tensor(gated, m.bank[3][:, :], factor, ALU.mult).then_inc(gated_ready, 1)
                if older:
                    m.need(dve, x1_ready, g - 1)
                    dve.bn_stats(m.stats[:, ds((g - 2) * 6, 6)], m.inner((g - 2) * ROWS))
                    dve.tensor_reduce(m.cells[:, ds((g - 2) * KVW, KVW)],
                                      m.inner((g - 2) * ROWS).rearrange("p r (k w) -> p k r w", k=KVW), AX.XY, ALU.add)
            dve.wait_ge(S("kb_zeroed"), 1)
            copy_k(0, 0)
            over_steps(dve, emit)

        @block.tensor
        def _(pe):
            def project(g, w, made):
                pe.matmul(m.bank[0 if w == 3 else 2][:, :], m.w0[:, w * 128:(w + 1) * 128], m.flat[:, ds(g * CH, CH)],
                          start=True, stop=True).then_inc(made, 1)

            def project_v(g, b):
                m.need(pe, z_staged, g + 1)
                for r in range(ROWS):
                    last = pe.matmul(m.bank[2][:, r * L:(r + 1) * L], zs[b][:, r * L:(r + 1) * L],
                                     m.w0[:, 256:384], start=True, stop=True)
                last.then_inc(v_made, 1)

            def scores(b, r):
                pe.matmul(m.quad[:, r, :], qT[b][:, r * L:(r + 1) * L], kb[b][:, r, :, :],
                          start=True, stop=True).then_inc(scores_made, 1)

            def turn(g, b, r):
                m.need(pe, probs_ready, (g - 1) * ROWS + (r + 1))
                m.need(pe, turned_odd if r % 2 else turned_even, (g - 1) * 2 + r // 2)
                if r == 0:
                    m.need(pe, th_ready, g)
                for h in range(HEADS):
                    at = (r * HEADS + h) * L
                    last = pe.transpose(m.bank[r % 2][:, h * L:(h + 1) * L], prob[1 - b][:, at:at + L], ident)
                last.then_inc(probs_turned, 1)

            def weigh(g, b, r):
                m.need(pe, turned_odd if r % 2 else turned_even, (g - 1) * 2 + (r // 2 + 1))
                if r == 0:
                    m.need(pe, v_ready, g)
                    m.need(pe, x1_ready, g - 1)
                for h in range(HEADS):
                    at = (r * HEADS + h) * HD
                    last = pe.matmul(m.bank[3][h * HD:(h + 1) * HD, r * L:(r + 1) * L], v[1 - b][:, at:at + HD],
                                     pT[r % 2][:, h * L:(h + 1) * L], start=True, stop=True, skip_group_check=True)
                last.then_inc(av_made, 1)

            def emit(g, b):
                own, before, older = live(g, 0, GROUPS), live(g, 1, GROUPS + 1), live(g, 2, GROUPS + 2)
                ahead = live(g, 0, GROUPS - 1)
                if own:
                    m.need(pe, q_ready, g + 1)
                    m.need(pe, k_low, g + 1)
                    m.need(pe, k_high, g + 1)
                    m.need(pe, shifted, g * ROWS)
                    scores(b, 0)
                    scores(b, 1)
                if before:
                    turn(g, b, 0)
                if older:
                    m.need(pe, gated_ready, g - 1)
                    pe.matmul(m.bank[3][0:C, :], wo, gated, start=True, stop=True).then_inc(out_made, 1)
                if ahead:
                    m.need(pe, v_ready, g)
                    project(g + 1, 1, k_made)
                if own:
                    scores(b, 2)
                    scores(b, 3)
                if before:
                    turn(g, b, 1)
                if ahead:
                    m.need(pe, k_low, g + 2)
                    m.need(pe, k_high, g + 2)
                    project(g + 1, 0, q_made)
                if before:
                    weigh(g, b, 0)
                    turn(g, b, 2)
                    weigh(g, b, 1)
                    m.need(pe, rwide_ready, g)
                    m.need(pe, q_ready if ahead else v_ready, g + 2 if ahead else g)
                    for r in range(ROWS):
                        last = pe.transpose(m.bank[2][:, r * L:(r + 1) * L], rwide[:, r * L:(r + 1) * L], ident)
                    last.then_inc(r_turned, 1)
                    turn(g, b, 3)
                    weigh(g, b, 2)
                if own:
                    m.need(pe, turned_even, g * 2)
                    project(g, 3, g_made)
                    m.need(pe, factor_ready if before else q_ready, g if before else g + 2)
                    project_v(g, b)
                if before:
                    weigh(g, b, 3)
            project(0, 1, k_made)
            pe.wait_ge(k_low, 1)
            pe.wait_ge(k_high, 1)
            project(0, 0, q_made)
            pe.wait_ge(S("wo_halved"), 1)
            over_steps(pe, emit)


def layer1(nc, m, args):
    ident = m.k("ident", 128)
    ident64 = ident[0:C, 0:C]
    TAPS = 9
    TOKENS = NWIN * KVW * KVW
    m.open_arena()
    kv_raw = m.take(C + 1)
    q_raw = m.take(C + 1, C)
    v_raw = m.take(C + 1, C)
    wo_raw = m.take(C, C)
    dw_raw = m.take(C, TAPS)
    dw_b, wo_b = m.take(1, C), m.take(1, C)
    turned = m.take(192 + C + TAPS, C + 1)
    kvT, qT = turned[:, 0:128], turned[:, 128:192]
    woT, dwT = turned[0:C, 192:256], turned[0:C, 256:256 + TAPS]
    spread = m.take(TAPS * C, C)
    taps = m.take(TAPS * C, C + 1)
    folded = m.take(TAPS * C, C + 1)
    centre = m.take(NWIN * C, C + 1)
    centre_folded = m.take(NWIN * C, C + 1)
    fold = m.take(C + 1, C + 1)
    pooled = m.take(TOKENS, C + 1)
    pooled_win = m.take(NWIN, C + 1)
    kv = m.take(128)
    q_win = m.take(NWIN, C)
    logits = m.take(NWIN, NWIN)
    above = m.take(64, NWIN).rearrange("p (j k) -> p j k", k=NWIN)
    same = m.take(64, NWIN).rearrange("p (j k) -> p j k", k=NWIN)
    rank, chosen, chosen_t = m.take(NWIN, NWIN), m.take(NWIN, NWIN), m.take(NWIN, NWIN)
    token_mask = m.take(NWIN)
    k_masked = m.take(NWIN * C)
    mT = m.take(NWIN * C, C)
    m_wo = m.take(NWIN * C, C)
    const_out = m.take(1, C)
    packed = m.nat[:, 0:2 * (2 + NWIN) * 128].rearrange("p (i k e o) -> p i k e o", i=2, k=2 + NWIN, e=2)
    outer = [packed[:, i, 0:2, :, :] for i in range(2)]
    middle = [packed[:, i, 2:2 + NWIN, :, :] for i in range(2)]
    bias_sum = m.take(C, C + 1)[C:C + 1, :]
    bias_rows = m.take(NWIN * 128, C + 1)[C:C + 1, :].rearrange("p (w e o) -> p w e o", w=NWIN, e=2)
    col_rows = m.take(3 * 128, C + 1)[C:C + 1, :].rearrange("p (x e o) -> p x e o", x=3, e=2)
    edge_rows = m.take(2 * 3 * 128, C + 1)[C:C + 1, :].rearrange("p (t x e o) -> p t x e o", t=2, x=3, e=2)
    bias = m.take(NWIN)
    BANKS = L // 8
    S = lambda name: m.sem(f"l1_{name}")
    loads = [
        (kv_raw[:, 0:C], args["L1_conv_qkv_w"][C:3 * C, :]),
        (kv_raw[:, C:C + 1], args["L1_conv_qkv_b"].rearrange("(o a) -> o a", a=1)[C:3 * C, :]),
        (q_raw[:, 0:C], args["L1_conv_qkv_w"][0:C, :]),
        (q_raw[:, C:C + 1], args["L1_conv_qkv_b"].rearrange("(o a) -> o a", a=1)[0:C, :]),
        (v_raw[:, 0:C], args["L1_conv_qkv_w"][2 * C:3 * C, :]),
        (v_raw[:, C:C + 1], args["L1_conv_qkv_b"].rearrange("(o a) -> o a", a=1)[2 * C:3 * C, :]),
        (wo_raw, args["L1_conv_wo_w"]),
        (dw_raw, args["L1_conv_dw_w"].rearrange("kh kw a m -> (kh kw a) m")),
        (dw_b, args["L1_conv_dw_b"].rearrange("(c a) -> c a", a=1)),
        (wo_b, args["L1_conv_wo_b"].rearrange("(c a) -> c a", a=1)),
    ]
    B = m.bank
    by_window = lambda t: t.rearrange("p (w c) -> p w c", w=NWIN)
    in_pairs = lambda t: t.rearrange("p (m c) -> p m c", c=L)

    def out_rows(g, parity):
        return m.flat[0:C, 8 * g * L:8 * (g + 1) * L].rearrange("p (m e c) -> p m e c", e=2, c=L)[:, :, parity, :]

    def tap(dy, dx, lo=0, hi=C):
        return folded[lo:hi, (3 * dy + dx) * C:(3 * dy + dx + 1) * C]

    group_norm(nc, m, 1, loads, S("loaded"))
    with nc.Block() as block:

        @block.vector
        def _(dve):
            step = m.chain(dve, "dve")
            step(dve.tensor_scalar(fold, ident[0:C + 1, 0:C + 1], m.scale[:, :], None, ALU.mult))
            dve.tensor_copy(fold[0:C, C:C + 1], m.shift[:, :]).then_inc(S("prep_ready"), 1)
            step(dve.tensor_scalar(pooled[0:C, :], m.cells[:, :], 1.0 / CELL, None, ALU.mult))
            step(dve.tensor_scalar(pooled[0:C, :], pooled[0:C, :], m.scale[0:C, :], m.shift[:, :], ALU.mult, ALU.add))
            step(dve.memset(pooled[C:C + 1, :], 1.0))
            step(dve.tensor_reduce(pooled_win, pooled.rearrange("p (w t) -> p w t", w=NWIN), AX.X, ALU.add))
            dve.tensor_scalar(pooled_win, pooled_win, 1.0 / (KVW * KVW), None, ALU.mult).then_inc(S("prep_ready"), 1)
            dve.wait_ge(S("prep_made"), 1)
            dve.tensor_copy(turned[:, 0:192], B[0][0:C + 1, 0:192])
            step(dve.tensor_copy(turned[0:C, 192:256 + TAPS], B[0][0:C, 192:256 + TAPS]))
            dve.tensor_tensor(spread.rearrange("p (t o) -> p t o", t=TAPS), woT.unsqueeze(1).broadcast_to([C, TAPS, C]),
                              dwT.unsqueeze(2).broadcast_to([C, TAPS, C]), ALU.mult).then_inc(S("prep_ready"), 1)
            dve.wait_ge(S("prep_made"), 2)
            dve.tensor_copy(kv, B[1][:, 0:128])
            dve.tensor_copy(q_win, B[2][0:C, 0:NWIN]).then_inc(S("prep_ready"), 1)
            dve.wait_ge(S("prep_made"), 3)
            dve.tensor_copy(taps[:, 0:512], B[3][0:C + 1, :])
            step(dve.tensor_copy(taps[:, 512:TAPS * C], B[4][0:C + 1, 0:C]))
            dve.sem_inc(S("prep_ready"), 1)
            dve.wait_ge(S("window_made"), 1)
            step(dve.tensor_scalar(logits, B[5][0:NWIN, 0:NWIN], float(C) ** -0.5, None, ALU.mult))
            of_j = logits.unsqueeze(2).broadcast_to([NWIN, NWIN, NWIN])
            of_k = logits.unsqueeze(1).broadcast_to([NWIN, NWIN, NWIN])
            step(dve.tensor_tensor(above, of_k, of_j, ALU.is_gt))
            step(dve.tensor_tensor(same, of_k, of_j, ALU.is_equal))
            step(dve.tensor_tensor(same, same, m.k("earlier", NWIN).rearrange("p (j k) -> p j k", k=NWIN), ALU.mult))
            step(dve.tensor_tensor(above, above, same, ALU.add))
            step(dve.tensor_reduce(rank, above, AX.X, ALU.add))
            dve.tensor_scalar(chosen, rank, TOPW - 0.5, None, ALU.is_lt).then_inc(S("window_ready"), 1)
            dve.wait_ge(S("window_made"), 2)
            dve.tensor_copy(chosen_t, B[5][0:NWIN, 16:16 + NWIN]).then_inc(S("window_ready"), 1)
            dve.wait_ge(S("window_made"), 3)
            step(dve.tensor_copy(token_mask, B[6][:, 0:NWIN]))
            dve.tensor_tensor(by_window(k_masked), kv[:, 0:C].unsqueeze(1).broadcast_to([128, NWIN, C]),
                              token_mask.unsqueeze(2).broadcast_to([128, NWIN, C]), ALU.mult).then_inc(S("window_ready"), 1)
            dve.wait_ge(S("window_made"), 4)
            dve.scalar_tensor_tensor(out=by_window(mT), in0=by_window(B[7][0:C, :]), scalar=float(C) ** -0.5,
                                     in1=m.k("headmask", C).unsqueeze(1).broadcast_to([C, NWIN, C]),
                                     op0=ALU.mult, op1=ALU.mult).then_inc(S("window_ready"), 1)
            dve.wait_ge(S("window_made"), 5)
            dve.tensor_copy(m_wo, B[0][0:C, :]).then_inc(S("window_ready"), 1)
            dve.wait_ge(S("window_made"), 6)
            dve.tensor_tensor(by_window(centre), by_window(B[1][0:C + 1, :]),
                              taps[:, 4 * C:5 * C].unsqueeze(1).broadcast_to([C + 1, NWIN, C]), ALU.add).then_inc(S("window_ready"), 1)
            dve.wait_ge(S("folded_made"), 1)
            dve.tensor_tensor(by_window(centre_folded[0:C, :]), by_window(B[2][0:C, :]),
                              ident64.unsqueeze(1).broadcast_to([C, NWIN, C]), ALU.add)
            dve.tensor_copy(centre_folded[C:C + 1, :], B[2][C:C + 1, :])
            dve.tensor_copy(folded[:, 0:512], B[3][0:C + 1, :])
            dve.tensor_copy(folded[:, 512:TAPS * C], B[4][0:C + 1, 0:C])
            step(dve.tensor_scalar(const_out, B[5][0:C, 32:33], wo_b, None, ALU.add))
            dve.sem_inc(S("weights_ready"), 1)
            row = folded[C:C + 1, :]
            for e in range(2):
                last = dve.tensor_reduce(col_rows[:, :, e, :], row.rearrange("p (y x o) -> p x o y", y=3, x=3), AX.X, ALU.add)
                dve.tensor_copy(edge_rows[:, e, :, e, :], row.rearrange("p (y x o) -> p y x o", y=3, x=3)[:, 2 * e, :, :])
            step(last)
            dve.sem_inc(S("edges_ready"), 1)
            step(dve.tensor_reduce(bias_sum, col_rows[:, :, 0, :].rearrange("p x o -> p o x"), AX.X, ALU.add))
            step(dve.tensor_tensor(bias_sum, bias_sum, tap(1, 1, C, C + 1), ALU.subtract))
            for e in range(2):
                last = dve.tensor_tensor(bias_rows[:, :, e, :], by_window(centre_folded[C:C + 1, :]),
                                         bias_sum.unsqueeze(1).broadcast_to([1, NWIN, C]), ALU.add)
            last.then_inc(S("bias_rows_ready"), 1)
            dve.wait_ge(S("bias_turned"), 1)
            dve.tensor_scalar(bias[0:C, :], B[6][0:C, 0:NWIN], const_out, None, ALU.add)
            step(dve.tensor_scalar(bias[C:128, :], B[6][C:128, 0:NWIN], const_out, None, ALU.add))
            dve.sem_inc(S("bias_ready"), 1)
            for g in range(BANKS):
                dve.wait_ge(S("conv_made"), g + 1)
                dve.tensor_scalar(out_rows(g, 1), in_pairs(B[g % 8][C:128, :]), bias[C:128, g // 2:g // 2 + 1], None,
                                  ALU.add).then_inc(S("odd_ready"), 1)
                dve.wait_ge(S("odd_ready"), g + 1)
                dve.wait_ge(S("even_ready"), g + 1)
                for half in range(2):
                    at = 2 * g + half
                    dve.bn_stats(m.stats[:, 6 * at:6 * at + 6], m.flat[0:C, at * CH:(at + 1) * CH])

        @block.gpsimd
        def _(pool):
            step = m.chain(pool, "pool")
            for part in (outer, middle):
                step(pool.memset(part[0][0:C, :, 1, :], 0.0))
                step(pool.memset(part[1][C:128, :, 0, :], 0.0))
            step(pool.memset(edge_rows[:, 0, :, 1, :], 0.0))
            step(pool.memset(edge_rows[:, 1, :, 0, :], 0.0))
            pool.sem_inc(S("blocks_zeroed"), 1)
            pool.wait_ge(S("weights_ready"), 1)
            for dx in (0, 2):
                for pair, dy in ((0, 0), (1, 2)):
                    step(pool.tensor_copy(outer[pair][0:C, dx // 2, 0, :], tap(dy, dx)))
                    step(pool.tensor_copy(outer[pair][C:128, dx // 2, 1, :], tap(dy, dx)))
                step(pool.tensor_copy(outer[0][C:128, dx // 2, 0, :], tap(1, dx)))
                step(pool.tensor_copy(outer[1][0:C, dx // 2, 1, :], tap(1, dx)))
            pool.sem_inc(S("outer_ready"), 1)

        @block.scalar
        def _(act):
            quarter = L // 4
            for n in range(4):
                last = act.activation(m.img3[C:128, n * quarter:(n + 1) * quarter:2, :],
                                      m.img3[0:C, n * quarter + 1:(n + 1) * quarter + 1:2, :], ACT.Copy)
            last.then_inc(S("rows_paired"), 1)
            act.wait_ge(S("blocks_zeroed"), 1)
            act.wait_ge(S("weights_ready"), 1)
            for pair, dy in ((0, 0), (1, 2)):
                act.activation(middle[pair][0:C, :, 0, :], tap(dy, 1).unsqueeze(1).broadcast_to([C, NWIN, C]), ACT.Copy)
                act.activation(middle[pair][C:128, :, 1, :], tap(dy, 1).unsqueeze(1).broadcast_to([C, NWIN, C]), ACT.Copy)
            act.activation(middle[0][C:128, :, 0, :], by_window(centre_folded[0:C, :]), ACT.Copy)
            act.activation(middle[1][0:C, :, 1, :], by_window(centre_folded[0:C, :]), ACT.Copy).then_inc(S("middle_ready"), 1)
            act.wait_ge(S("bias_ready"), 1)
            for g in range(BANKS):
                act.wait_ge(S("conv_made"), g + 1)
                act.activation(out_rows(g, 0), in_pairs(B[g % 8][0:C, :]), ACT.Identity,
                               bias=bias[0:C, g // 2:g // 2 + 1]).then_inc(S("even_ready"), 1)

        @block.tensor
        def _(pe):
            pe.wait_ge(S("loaded"), 16 * len(loads))
            pe.transpose(B[0][0:C + 1, 0:128], kv_raw, ident)
            pe.transpose(B[0][0:C + 1, 128:192], q_raw, ident64)
            pe.transpose(B[0][0:C, 192:256], wo_raw, ident64)
            pe.transpose(B[0][0:C, 256:256 + TAPS], dw_raw, ident[0:TAPS, 0:TAPS]).then_inc(S("prep_made"), 1)
            pe.wait_ge(S("prep_ready"), 3)
            pe.wait_ge(S("prep_ready"), 2)
            pe.matmul(B[1][:, 0:128], pooled, kvT, start=True, stop=True)
            pe.matmul(B[2][0:C, 0:NWIN], qT, pooled_win, start=True, stop=True).then_inc(S("prep_made"), 1)
            pe.matmul(B[3][0:C + 1, :], v_raw, spread[:, 0:512], start=True, stop=True)
            pe.matmul(B[4][0:C + 1, 0:C], v_raw, spread[:, 512:TAPS * C], start=True, stop=True).then_inc(S("prep_made"), 1)
            pe.wait_ge(S("prep_ready"), 4)
            pe.matmul(B[5][0:NWIN, 0:NWIN], q_win, q_win, start=True, stop=True).then_inc(S("window_made"), 1)
            pe.wait_ge(S("window_ready"), 1)
            pe.transpose(B[5][0:NWIN, 16:16 + NWIN], chosen, ident[0:NWIN, 0:NWIN]).then_inc(S("window_made"), 1)
            pe.wait_ge(S("window_ready"), 2)
            pe.matmul(B[6][:, 0:NWIN], m.k("expand", NWIN), chosen_t, start=True, stop=True).then_inc(S("window_made"), 1)
            pe.wait_ge(S("window_ready"), 3)
            pe.matmul(B[7][0:C, :], kv[:, C:128], k_masked, start=True, stop=True).then_inc(S("window_made"), 1)
            pe.wait_ge(S("window_ready"), 4)
            for w in range(NWIN):
                last = pe.matmul(B[0][0:C, w * C:(w + 1) * C], mT[:, w * C:(w + 1) * C], woT, start=True, stop=True)
            last.then_inc(S("window_made"), 1)
            pe.wait_ge(S("window_ready"), 5)
            pe.matmul(B[1][0:C + 1, :], q_raw, m_wo, start=True, stop=True).then_inc(S("window_made"), 1)
            pe.wait_ge(S("window_ready"), 6)
            pe.wait_ge(S("prep_ready"), 5)
            pe.wait_ge(S("prep_ready"), 1)
            pe.matmul(B[2][0:C + 1, :], fold, centre, start=True, stop=True)
            pe.matmul(B[3][0:C + 1, :], fold, taps[:, 0:512], start=True, stop=True)
            pe.matmul(B[4][0:C + 1, 0:C], fold, taps[:, 512:TAPS * C], start=True, stop=True)
            pe.matmul(B[5][0:C, 32:33], woT, dw_b, start=True, stop=True).then_inc(S("folded_made"), 1)
            pe.wait_ge(S("weights_ready"), 1)
            pe.wait_ge(S("rows_paired"), 1)
            pe.wait_ge(S("outer_ready"), 1)
            pe.wait_ge(S("middle_ready"), 1)
            minus = m.const[C:C + 1, CONSTS["minus"]]
            for g in range(BANKS):
                if g == 2:
                    pe.wait_ge(S("bias_rows_ready"), 1)
                    for w in range(NWIN):
                        last = pe.matmul(B[6][:, w:w + 1], bias_rows[:, w, :, :], m.scale[C:C + 1, :], start=True, stop=True)
                    last.then_inc(S("bias_turned"), 1)
                if g == 6:
                    pe.wait_ge(S("bias_ready"), 1)
                if g >= 8:
                    pe.wait_ge(S("even_ready"), g - 7)
                    pe.wait_ge(S("odd_ready"), g - 7)
                for n, (pair, dx) in enumerate((p, dx) for p in range(2) for dx in range(3)):
                    weights = middle[pair][:, g // 2, :, :] if dx == 1 else outer[pair][:, dx // 2, :, :]
                    first = 8 * g + 2 * pair
                    pe.matmul(B[g % 8][:, :], weights, m.img3[:, first:first + 7:2, dx:dx + L],
                              start=(n == 0), stop=False, skip_group_check=True)
                if g == 0:
                    pe.wait_ge(S("edges_ready"), 1)
                for dx, column in ((0, 0), (2, L - 1)):
                    last = pe.matmul(B[g % 8][:, column:column + 3 * L + 1:L], col_rows[:, dx, :, :], minus[:, 1:5],
                                     start=False, stop=True, skip_group_check=True)
                if g in (0, BANKS - 1):
                    e = g // (BANKS - 1)
                    for dx in range(3):
                        last = pe.matmul(B[g % 8][:, e * 3 * L:(e * 3 + 1) * L], edge_rows[:, e, dx, :, :],
                                         minus[:, dx:dx + L], start=False, stop=True, skip_group_check=True)
                last.then_inc(S("conv_made"), 1)


def layer2(nc, m):
    ident = m.k("ident", 128)
    HALF = ROWS // 2
    RULE = GIANTS // 2 + 1
    m.open_arena()
    nat_tiles = iter(m.nat[:, n:n + CH] for n in range(0, L * C, CH))
    m.colsum = m.take(CH, C)
    vt = [m.take(ROWS * 256).rearrange("p (n x) -> p n x", n=ROWS) for _ in range(2)]
    yv = [m.take(2 * ROWS * C).rearrange("p (n k d) -> p n k d", n=ROWS, k=2) for _ in range(2)]
    xs = m.take(ROWS * C)
    xsT = m.take(CH, C)
    cor = m.take(CH)
    rem = m.take(CH)
    a1 = m.take(CH)
    a2 = m.take(CH)
    a4, a8 = ([next(nat_tiles) for _ in range(2)] for _ in range(2))
    z_top = m.take(ROWS * C)
    zs = [[next(nat_tiles)[:, 0:HALF * 2 * C].rearrange("p (n x) -> p n x", n=HALF) for _ in range(2)]
          for _ in range(2)]
    st = m.take(6 * ROWS)
    mv = m.take(2 * ROWS).rearrange("p (r s) -> p r s", s=2)
    std, rstd, deg, dsq, dinv = (m.take(ROWS) for _ in range(5))
    top = m.take(8 * ROWS)
    S = lambda name: m.sem(f"l2_{name}")
    y_ready, y_turned, yn_ready, stats_ready, measured, std_ready, std_eased, rstd_ready, xs_ready, xs_turned, xsT_ready = map(
        S, "y_ready y_turned yn_ready stats_ready measured std_ready std_eased rstd_ready xs_ready xs_turned xsT_ready".split())
    cor_made, cor_ready, topk_step, rem_ready, diag_added, m_turned, deg_summed, deg_ready, dsq_ready, dinv_ready, b_ready = map(
        S, "cor_made cor_ready topk_step rem_ready diag_added m_turned deg_summed deg_ready dsq_ready dinv_ready b_ready".split())
    b_turned, a2_made, a2_ready, ay_made, ay_ready, v1_turned, v1_ready, a4_made, a4_ready, a8_made, a8_ready, v23_made, v23_ready = map(
        S, "b_turned a2_made a2_ready ay_made ay_ready v1_turned v1_ready a4_made a4_ready a8_made a8_ready v23_made v23_ready".split())
    low_used, col_added = S("low_used"), S("col_added")
    horner_made, z_ready, z_turned, x3_ready, a_ready = ([S(f"{name}_{half}") for half in ("first", "last")]
                                                for name in ("horner_made", "z_ready", "z_turned", "x3_ready", "a_ready"))
    B = m.bank

    def over_steps(eng, emit):
        for s in range(4):
            emit(s, s % 2)
        with eng.Fori(0, (GROUPS - 6) // 2, 1) as it:
            for b in range(2):
                emit(it * 2 + (4 + b), b)
        for s in range(GROUPS - 2, GROUPS + 2):
            emit(s, s % 2)

    def live(s, lo, hi):
        return not isinstance(s, int) or lo <= s < hi

    def parts(s):
        return live(s, 0, GROUPS), live(s, 1, GROUPS + 1), live(s, 2, GROUPS + 2)

    def quarters(t):
        return t.rearrange("p (n x) -> p n x", n=ROWS)

    def halves(t):
        return t.rearrange("p (n x) -> p n x", n=HALF)

    def done(s, half, k):
        return (s - 1 - half) * RULE + k

    def place(k):
        return (GIANTS - 2 - 2 * k, 2) if k < RULE - 1 else (0, 1)

    with nc.Block() as block:

        @block.gpsimd
        def _(pool):
            step = m.chain(pool, "pool")
            step(pool.memset(m.colsum, 0.0))

            def emit(s, b):
                p, _, r = parts(s)
                if p:
                    m.need(pool, rem_ready, s + 1)
                    pool.tensor_tensor(quarters(rem), quarters(rem), ident.unsqueeze(1).broadcast_to([128, ROWS, 128]),
                                       ALU.add).then_inc(diag_added, 1)
                if r:
                    m.need(pool, x3_ready[1], s - 1)
                    m.need(pool, col_added, s - 2)
                    pool.tensor_tensor(quarters(m.colsum), quarters(m.colsum), m.inner((s - 2) * ROWS), ALU.add).then_inc(col_added, 1)
            over_steps(pool, emit)

        @block.scalar
        def _(act):
            def take_y(s, b):
                act.activation(vt[b][0:C, :, 0:L], quarters(m.flat[0:C, ds(s * CH, CH)]), ACT.Identity,
                               scale=m.scale[0:C, :], bias=m.shift[:, :]).then_inc(y_ready, 1)

            def keep_z(s, half, k):
                g, n = place(k)
                m.need(act, horner_made[half], done(s, half, k + 1))
                act.activation(zs[half][k % 2][:, :, 0:n * C], m.quad[:, HALF * half:HALF * (half + 1), g * C:(g + n) * C],
                               ACT.Copy if k < RULE - 1 else ACT.Relu).then_inc(z_ready[half], 1)

            def turned_y(s, b):
                m.need(act, y_turned, s + 1)
                act.activation(yv[b][:, :, 0, :], quarters(B[0][:, 0:ROWS * C]), ACT.Copy).then_inc(yn_ready, 1)

            def deviation(s):
                m.need(act, measured, s + 1)
                act.activation(std, mv[:, :, 1], ACT.Sqrt, scale=C / (C - 1)).then_inc(std_ready, 1)

            def emit(s, b):
                p, q, r = parts(s)
                ahead = live(s, 0, GROUPS - 1)
                o = 1 - b
                if r:
                    keep_z(s, 1, 0)
                if q:
                    m.need(act, a2_made, s)
                    act.activation(a2, B[0][:, :], ACT.Copy).then_inc(a2_ready, 1)
                if r:
                    keep_z(s, 1, 1)
                if p:
                    m.need(act, xs_turned, s + 1)
                    act.activation(xsT, B[2][0:C, :], ACT.Copy).then_inc(xsT_ready, 1)
                if r:
                    keep_z(s, 1, 2)
                if p:
                    m.need(act, cor_made, s + 1)
                    m.need(act, b_turned, s)
                    act.activation(cor, B[2][:, :], ACT.Copy, scale=1.0 / (C - 1 + 1e-6)).then_inc(cor_ready, 1)
                if q:
                    m.need(act, a4_made, s)
                    act.activation(a4[o], B[0][:, :], ACT.Copy).then_inc(a4_ready, 1)
                if r:
                    keep_z(s, 1, 3)
                    keep_z(s, 1, 4)
                if q:
                    m.need(act, a8_made, s)
                    act.activation(a8[o], B[0][:, :], ACT.Copy).then_inc(a8_ready, 1)
                    m.need(act, v23_made, s)
                    act.activation(vt[o][:, :, L:2 * L], quarters(B[1][:, :]), ACT.Copy).then_inc(v23_ready, 1)
                if ahead:
                    m.need(act, low_used, s)
                    take_y(s + 1, o)
                if p:
                    m.need(act, deg_ready, s + 1)
                    act.activation(dsq, deg, ACT.Sqrt).then_inc(dsq_ready, 1)
                if q:
                    keep_z(s, 0, 0)
                if ahead:
                    turned_y(s + 1, o)
                if q:
                    keep_z(s, 0, 1)
                for half in range(2):
                    if q:
                        keep_z(s, 0, 2 + half)
                    if p:
                        m.need(act, b_turned, s + 1)
                        for n in range(HALF * half, HALF * (half + 1)):
                            last = act.activation(a1[:, n * L:(n + 1) * L], B[2][:, n * L:(n + 1) * L], ACT.Copy,
                                                  scale=dinv[:, n:n + 1])
                        last.then_inc(a_ready[half], 1)
                if ahead:
                    deviation(s + 1)
                if q:
                    keep_z(s, 0, 4)
            take_y(0, 0)
            turned_y(0, 0)
            deviation(0)
            over_steps(act, emit)

        @block.vector
        def _(dve):
            def finish(s, half):
                row = (s - 2) * ROWS + HALF * half
                m.need(dve, z_turned[half], s - 1)
                dve.tensor_tensor(m.inner(row, HALF), halves(B[3][0:C, 0:HALF * L]), halves(m.flat[0:C, ds(row * L, HALF * L)]),
                                  ALU.add).then_inc(x3_ready[half], 1)

            def measure(s, b):
                m.need(dve, yn_ready, s + 1)
                for n in range(ROWS):
                    last = dve.bn_stats(st[:, 6 * n:6 * n + 6], yv[b][:, n, 0, :])
                last.then_inc(stats_ready, 1)
                m.need(dve, stats_ready, s + 1)
                m.need(dve, xs_ready, s)
                for n in range(ROWS):
                    last = dve.bn_aggr(mv[:, n, :], st[:, 6 * n:6 * n + 6])
                last.then_inc(measured, 1)

            def standardise(s, b):
                m.need(dve, std_ready, s + 1)
                dve.tensor_scalar(std, std, 1e-6, None, ALU.add).then_inc(std_eased, 1)
                m.need(dve, std_eased, s + 1)
                dve.reciprocal(rstd, std).then_inc(rstd_ready, 1)
                m.need(dve, rstd_ready, s + 1)
                m.need(dve, xs_turned, s)
                for n in range(ROWS):
                    last = dve.tensor_scalar(xs[:, n * C:(n + 1) * C], yv[b][:, n, 0, :], mv[:, n, 0:1], rstd[:, n:n + 1],
                                             ALU.subtract, ALU.mult)
                last.then_inc(xs_ready, 1)

            def emit(s, b):
                p, q, r = parts(s)
                o = 1 - b
                before = s * (4 * ROWS + 1)
                if r:
                    finish(s, 0)
                if q:
                    m.need(dve, ay_made, s)
                    dve.tensor_copy(yv[o][:, :, 1, :], quarters(B[3][:, 0:ROWS * C]))
                    dve.tensor_copy(z_top, B[3][:, ROWS * C:2 * ROWS * C]).then_inc(ay_ready, 1)
                if p:
                    m.need(dve, cor_ready, s + 1)
                    for n in range(ROWS):
                        dve.max(top[:, 8 * n:8 * n + 8], cor[:, n * L:(n + 1) * L]).then_inc(topk_step, 1)
                if q:
                    m.need(dve, v1_turned, s)
                    dve.tensor_copy(vt[o][C:128, :, 0:L], quarters(B[1][C:128, :])).then_inc(v1_ready, 1)
                if p:
                    m.need(dve, m_turned, s)
                    for n in range(ROWS):
                        m.need(dve, topk_step, before + (n + 1))
                        dve.match_replace(rem[:, n * L:(n + 1) * L], top[:, 8 * n:8 * n + 8], cor[:, n * L:(n + 1) * L],
                                          -BIG).then_inc(topk_step, 1)
                if p:
                    for n in range(ROWS):
                        m.need(dve, topk_step, before + (ROWS + n + 1))
                        dve.max(top[:, 8 * n:8 * n + 8], rem[:, n * L:(n + 1) * L]).then_inc(topk_step, 1)
                    m.need(dve, topk_step, before + 3 * ROWS)
                    dve.memset(top.rearrange("p (n k) -> p n k", k=8)[:, :, 1:8], -BIG).then_inc(topk_step, 1)
                if p:
                    m.need(dve, topk_step, before + (3 * ROWS + 1))
                    for n in range(ROWS):
                        dve.match_replace(rem[:, n * L:(n + 1) * L], top[:, 8 * n:8 * n + 8], rem[:, n * L:(n + 1) * L],
                                          -BIG).then_inc(topk_step, 1)
                    m.need(dve, topk_step, before + (4 * ROWS + 1))
                    dve.scalar_tensor_tensor(out=rem, in0=rem, scalar=-BIG, in1=cor, op0=ALU.is_equal, op1=ALU.mult).then_inc(rem_ready, 1)
                    m.need(dve, m_turned, s + 1)
                    for n in range(ROWS):
                        last = dve.tensor_tensor_reduce(cor[:, n * L:(n + 1) * L], rem[:, n * L:(n + 1) * L],
                                                        B[1][:, n * L:(n + 1) * L], 1.0, 0.0, ALU.add, ALU.add, deg[:, n:n + 1])
                    last.then_inc(deg_summed, 1)
                    m.need(dve, deg_summed, s + 1)
                    dve.tensor_scalar(deg, deg, 0.5, 1e-6, ALU.mult, ALU.max).then_inc(deg_ready, 1)
                    m.need(dve, dsq_ready, s + 1)
                    m.need(dve, a_ready[1], s)
                    dve.reciprocal(dinv, dsq).then_inc(dinv_ready, 1)
                    m.need(dve, dinv_ready, s + 1)
                    for n in range(ROWS):
                        last = dve.tensor_scalar(cor[:, n * L:(n + 1) * L], cor[:, n * L:(n + 1) * L], dinv[:, n:n + 1], 0.5,
                                                 ALU.mult, ALU.mult)
                    last.then_inc(b_ready, 1)
                if r:
                    finish(s, 1)
                if live(s, 0, GROUPS - 1):
                    measure(s + 1, o)
                if r:
                    m.need(dve, x3_ready[1], s - 1)
                    dve.bn_stats(m.stats[:, ds((s - 2) * 6, 6)], m.inner((s - 2) * ROWS))
                    dve.tensor_reduce(m.cells[:, ds((s - 2) * ROWS, ROWS)], m.inner((s - 2) * ROWS), AX.X, ALU.add)
                if live(s, 0, GROUPS - 1):
                    standardise(s + 1, o)
            measure(0, 0)
            standardise(0, 0)
            over_steps(dve, emit)

        @block.tensor
        def _(pe):
            def col(n, w=L):
                return slice(n * w, (n + 1) * w)

            def horner(s, half, k, chunk):
                g, width = place(k)
                if k:
                    m.need(pe, z_ready[half], done(s, half, k))
                for n in range(HALF):
                    row = HALF * half + n
                    if k == 0:
                        value, width = z_top[:, col(row, C)], 1
                    elif k < RULE - 1:
                        value = zs[half][(k - 1) % 2][:, n, :]
                    else:
                        value = zs[half][(k - 1) % 2][:, n, C:2 * C]
                    power = a8[chunk] if k < RULE - 1 else a4[chunk]
                    last = pe.matmul(m.quad[:, row, g * C:(g + width) * C], power[:, col(row)], value,
                                     start=False, stop=(k == RULE - 1), skip_group_check=True)
                last.then_inc(horner_made[half], 1)

            def low(n, o):
                return pe.matmul(m.quad[:, n, :], vt[o][:, n, 0:L], m.theta[:, 0, :], start=True, stop=False, skip_group_check=True)

            def high(n, o):
                return pe.matmul(m.quad[:, n, :], vt[o][:, n, L:2 * L], m.theta[:, 1, :], start=False, stop=False, skip_group_check=True)

            def turn_z(s, half):
                m.need(pe, z_ready[half], done(s - 1 + half, half, RULE))
                for n in range(HALF):
                    last = pe.transpose(B[3][0:C, col(n)], zs[half][0][:, n, 0:C], ident)
                last.then_inc(z_turned[half], 1)

            def turn_y(s, b):
                m.need(pe, y_ready, s + 1)
                for n in range(ROWS):
                    last = pe.transpose(B[0][:, col(n, C)], vt[b][0:C, n, 0:L], ident[0:C, 0:C])
                last.then_inc(y_turned, 1)

            def emit(s, b):
                p, q, r = parts(s)
                o = 1 - b

                def square(source):
                    for n in range(ROWS):
                        last = pe.matmul(B[0][:, col(n)], source[:, col(n)], source[:, col(n)], start=True, stop=True)
                    return last

                def slot(half, k):
                    if half and r:
                        horner(s, 1, k, b)
                    if not half and q:
                        horner(s, 0, k, o)

                slot(1, 0)
                if q:
                    m.need(pe, a_ready[1], s)
                    m.need(pe, yn_ready, s + 1 if p else s)
                    square(a1).then_inc(a2_made, 1)
                if r:
                    m.need(pe, x3_ready[1], s - 2)
                    turn_z(s, 0)
                slot(1, 1)
                if p:
                    m.need(pe, xs_ready, s + 1)
                    m.need(pe, a_ready[1], s)
                    for n in range(ROWS):
                        last = pe.transpose(B[2][0:C, col(n)], xs[:, col(n, C)], ident)
                    last.then_inc(xs_turned, 1)
                if q:
                    m.need(pe, x3_ready[0], s - 1)
                    for n in range(ROWS):
                        pe.matmul(B[3][:, col(n, C)], a1[:, col(n)], yv[o][:, n, 0, :], start=True, stop=True)
                    for n in range(ROWS):
                        last = pe.matmul(B[3][:, col(ROWS + n, C)], vt[o][0:C, n, 0:L], m.theta_top[:, :], start=True, stop=True)
                    last.then_inc(ay_made, 1)
                slot(1, 2)
                if p:
                    m.need(pe, xsT_ready, s + 1)
                    for n in range(ROWS):
                        last = pe.matmul(B[2][:, col(n)], xsT[:, col(n)], xsT[:, col(n)], start=True, stop=True)
                    last.then_inc(cor_made, 1)
                if q:
                    m.need(pe, a2_ready, s)
                    square(a2).then_inc(a4_made, 1)
                slot(1, 3)
                if q:
                    m.need(pe, ay_ready, s)
                    m.need(pe, deg_summed, s)
                    for n in range(ROWS):
                        last = pe.transpose(B[1][:, col(n)], yv[o][:, n, :, :], ident)
                    last.then_inc(v1_turned, 1)
                slot(1, 4)
                if q:
                    m.need(pe, a4_ready, s)
                    square(a4[o]).then_inc(a8_made, 1)
                    m.need(pe, v1_ready, s)
                    for n in range(ROWS):
                        last = pe.matmul(B[1][:, col(n)], yv[o][:, n, :, :], a2[:, col(n)], start=True, stop=True)
                    last.then_inc(v23_made, 1)
                    m.need(pe, z_ready[0], done(s, 0, 0))
                    low(0, o)
                    low(1, o)
                    m.need(pe, z_ready[1], done(s, 1, RULE))
                    low(2, o)
                    low(3, o).then_inc(low_used, 1)
                    m.need(pe, v23_ready, s)
                if p:
                    m.need(pe, diag_added, s + 1)
                    for n in range(ROWS):
                        last = pe.transpose(B[1][:, col(n)], rem[:, col(n)], ident)
                    last.then_inc(m_turned, 1)
                if q:
                    high(0, o)
                    high(1, o)
                    m.need(pe, a8_ready, s)
                slot(0, 0)
                if r:
                    m.need(pe, ay_ready if q else x3_ready[0], s if q else s - 1)
                    turn_z(s, 1)
                if live(s, 0, GROUPS - 1):
                    turn_y(s + 1, o)
                slot(0, 1)
                if q:
                    high(2, o)
                slot(0, 2)
                if p:
                    m.need(pe, b_ready, s + 1)
                    m.need(pe, cor_ready, s + 1)
                    for n in range(ROWS):
                        last = pe.transpose(B[2][:, col(n)], cor[:, col(n)], ident)
                    last.then_inc(b_turned, 1)
                slot(0, 3)
                if q:
                    high(3, o)
                slot(0, 4)
            turn_y(0, 0)
            over_steps(pe, emit)


def layer3(nc, m, args, out):
    ident = m.k("ident", 128)
    ident64 = ident[0:C, 0:C]
    KINDS = 15
    COLS = 8
    STEPS3 = L // COLS
    m.arena_at = CH
    ws = m.take(KINDS * C, C)
    wm = m.take(C, C)
    bm = m.take(C, 1)
    wsT = m.take(KINDS * C, C)
    w = m.take(KINDS * C, C)
    spread_scale = m.take(C, C)
    both = m.take(C)
    rows_x, cols_x, diag_raw, diag_x = (m.take(L, C) for _ in range(4))
    mean_diag, mean_all, mean_diag2 = (m.take(1, C) for _ in range(3))
    of_row, of_col = m.take(C), m.take(C)
    diag_ret, diag_out = m.take(C), m.take(C)
    xx = [m.take(COLS * L) for _ in range(2)]
    before, ready = ([m.arena[:, CH + (2 * n + b) * COLS * C:CH + (2 * n + b + 1) * COLS * C] for b in range(2)] for n in range(2))
    split = m.take(3 * C)
    rest = m.take(C)
    s_flat = m.nat[0:3, :]
    S = lambda name: m.sem(f"l3_{name}")
    B = m.bank
    kind = lambda k: w[:, (k - 1) * C:k * C]
    by_col = lambda t: t.rearrange("p (j x) -> p j x", j=COLS)
    group_norm(nc, m, 3, [
        (ws.rearrange("d (k e) -> d k e", k=KINDS), args["L3_conv_Ws"].rearrange("k d e -> d k e")),
        (wm, args["L3_conv_Wm"]),
        (bm, args["L3_conv_bm"].rearrange("(a c) -> a c", a=1)),
    ], S("loaded"))
    with nc.Block() as block:

        @block.sync
        def _(sp):
            sp.wait_ge(S("of_col"), 1)
            for n in range(3):
                sp.dma_start(s_flat[n:n + 1, :].rearrange("a (j c) -> a j c", c=C), split[:, n * C:(n + 1) * C]).then_inc(S("flattened"), 16)
            sp.wait_ge(S("flattened"), 16 * 3)

        @block.scalar
        def _(act):
            act.wait_ge(S("ws_turned"), 2)
            act.activation(wsT[:, 512:KINDS * C], B[1][0:C, 0:KINDS * C - 512], ACT.Copy).then_inc(S("copied_upper"), 1)
            act.wait_ge(S("w_made"), 2)
            act.activation(w[:, 512:KINDS * C], B[3][0:C, 0:KINDS * C - 512], ACT.Copy).then_inc(S("copied_upper"), 1)

        @block.vector
        def _(dve):
            step = m.chain(dve, "dve")
            step(dve.tensor_reduce(cols_x, m.colsum.rearrange("p (r c) -> p c r", r=ROWS), AX.X, ALU.add))
            step(dve.tensor_scalar(cols_x, cols_x, 1.0 / L, None, ALU.mult))
            step(dve.tensor_scalar(rows_x, m.cells[:, :], 1.0 / L, None, ALU.mult))
            step(dve.tensor_scalar(rows_x, rows_x, m.scale[0:C, :], m.shift[:, :], ALU.mult, ALU.add))
            step(dve.tensor_copy(diag_raw, m.img[0:C, PW + 1:L * (PW + 1) + 1:PW + 1]))
            step(dve.tensor_scalar(diag_x, diag_raw, m.scale[0:C, :], m.shift[:, :], ALU.mult, ALU.add))
            step(dve.tensor_reduce(mean_diag, diag_x, AX.X, ALU.add))
            step(dve.tensor_reduce(mean_all, rows_x, AX.X, ALU.add))
            step(dve.tensor_scalar(mean_diag2, mean_diag, 2.0 / L, None, ALU.mult))
            step(dve.tensor_scalar(mean_diag, mean_diag, 1.0 / L, None, ALU.mult))
            step(dve.tensor_scalar(mean_all, mean_all, 1.0 / L, None, ALU.mult))
            step(dve.tensor_scalar(spread_scale, ident64, m.scale[0:C, :], None, ALU.mult))
            dve.tensor_scalar(cols_x, cols_x, m.scale[0:C, :], m.shift[:, :], ALU.mult, ALU.add).then_inc(S("means_ready"), 1)
            dve.wait_ge(S("ws_turned"), 1)
            dve.tensor_copy(wsT[:, 0:512], B[0][0:C, :]).then_inc(S("copied_lower"), 1)
            dve.wait_ge(S("w_made"), 1)
            dve.tensor_copy(w[:, 0:512], B[2][0:C, :]).then_inc(S("copied_lower"), 1)
            dve.wait_ge(S("of_col_made"), 1)
            step(dve.tensor_copy(of_col, B[5][:, 0:C]))
            step(dve.memset(m.part_sum[:, :], 1.0))
            left = of_col
            for n in range(3):
                part = split[:, n * C:(n + 1) * C]
                step(dve.tensor_copy(m.rounded[:, :], left))
                step(dve.tensor_copy(part, m.rounded[:, :]))
                if n < 2:
                    step(dve.tensor_tensor(rest, left, part, ALU.subtract))
                    left = rest
            dve.sem_inc(S("of_col"), 1)
            dve.wait_ge(S("terms_made"), 1)
            dve.tensor_copy(of_row, B[6][:, 0:C])
            dve.tensor_copy(both, B[7][:, 0:C])
            step(dve.tensor_copy(diag_ret, B[0][:, 0:C]))
            dve.scalar_tensor_tensor(out=diag_out, in0=diag_ret, scalar=0.0, in1=B[1][:, 0:C], op0=ALU.max, op1=ALU.add).then_inc(S("diag_ready"), 1)

        @block.tensor
        def _(pe):
            pe.wait_ge(S("loaded"), 16 * 3)
            for half, ks in enumerate((range(0, 8), range(8, KINDS))):
                for k in ks:
                    at = (k - 8 * half) * C
                    last = pe.transpose(B[half][0:C, at:at + C], ws[:, k * C:(k + 1) * C], ident64)
                last.then_inc(S("ws_turned"), 1)
            for half, ks in enumerate((range(0, 8), range(8, KINDS))):
                pe.wait_ge(S("copied_upper" if half else "copied_lower"), 1)
                for k in ks:
                    at = (k - 8 * half) * C
                    last = pe.matmul(B[2 + half][0:C, at:at + C], wsT[:, k * C:(k + 1) * C], wm, start=True, stop=True)
                last.then_inc(S("w_made"), 1)

            def total(bank, terms):
                for n, (vector, weights) in enumerate(terms):
                    last = pe.matmul(bank[:, 0:C], vector, weights, start=(n == 0), stop=(n == len(terms) - 1))
                return last

            everywhere = lambda t: t.to_broadcast([C, L])
            pe.wait_ge(S("means_ready"), 1)
            pe.wait_ge(S("copied_lower"), 2)
            pe.wait_ge(S("copied_upper"), 2)
            total(B[5], [(rows_x, kind(7)), (cols_x, kind(9)), (diag_x, kind(13))]).then_inc(S("of_col_made"), 1)
            total(B[6], [(rows_x, kind(6)), (cols_x, kind(8)), (diag_x, kind(12)), (everywhere(mean_diag2), kind(14)),
                         (everywhere(m.shift[:, :]), kind(10)), (everywhere(m.shift[:, :]), kind(11)), (m.one[:, :], bm)])
            pe.matmul(B[7][0:C, 0:C], spread_scale, kind(10), start=True, stop=True)
            pe.matmul(B[7][C:128, 0:C], spread_scale, kind(11), start=True, stop=True)
            total(B[0], [(diag_x, kind(k)) for k in (10, 11, 12, 13, 1)] + [(rows_x, kind(k)) for k in (6, 7, 3)]
                  + [(cols_x, kind(k)) for k in (8, 9, 4)]
                  + [(everywhere(mean_diag2), kind(14)), (everywhere(mean_diag), kind(2)), (everywhere(mean_all), kind(5)),
                     (m.one[:, :], bm)])
            pe.transpose(B[1][:, 0:C], diag_raw, ident64).then_inc(S("terms_made"), 1)

    xx_ready, parts_ready, ret_made, added, out_ready = (S(n) for n in ("xx_ready", "parts_ready", "ret_made", "added", "out_ready"))
    sent = [S("sent_even"), S("sent_odd")]

    def over_steps(eng, emit):
        for t in range(2):
            emit(t, t, 0)
        with eng.Fori(0, (STEPS3 - 2) // 2, 1) as it:
            for b in range(2):
                emit(it * 2 + (2 + b), b, it + 1)

    with nc.Block() as block:

        @block.gpsimd
        def _(pool):
            def emit(t, b, turn):
                m.need(pool, ret_made, t - 1)
                pool.tensor_copy(m.parts[b][:, :], s_flat[:, ds(t * COLS * C, COLS * C)]).then_inc(parts_ready, 1)
            over_steps(pool, emit)

        @block.scalar
        def _(act):
            def emit(t, b, turn):
                m.need(act, ret_made, t - 1)
                act.activation(by_col(xx[b][0:C, :]), m.img3[0:C, 1:L + 1, ds(t * COLS + 1, COLS)].rearrange("p i j -> p j i"),
                               ACT.Copy)
                act.activation(by_col(xx[b][C:128, :]), m.inner(t * COLS, COLS), ACT.Copy).then_inc(xx_ready, 1)
            over_steps(act, emit)

        @block.tensor
        def _(pe):
            def emit(t, b, turn):
                m.need(pe, xx_ready, t + 1)
                m.need(pe, out_ready, t - 1)
                m.need(pe, parts_ready, t + 1)
                pe.matmul(B[b][:, :], m.part_sum[:, :], m.parts[b][:, :], start=True, stop=False, skip_group_check=True)
                for j in range(COLS):
                    pe.matmul(B[b][:, j * C:(j + 1) * C], xx[b][:, j * L:(j + 1) * L], both, start=False, stop=True, skip_group_check=True)
                for j in range(COLS):
                    last = pe.transpose(B[2 + b][:, j * C:(j + 1) * C], xx[b][0:C, j * L:(j + 1) * L], ident64)
                last.then_inc(ret_made, 1)
            over_steps(pe, emit)

        @block.vector
        def _(dve):
            def emit(t, b, turn):
                m.need(dve, ret_made, t + 1)
                dve.tensor_tensor(by_col(before[b]), by_col(B[b][:, :]), of_row.unsqueeze(1).broadcast_to([128, COLS, C]),
                                  ALU.add).then_inc(added, 1)
                m.need(dve, added, t + 1)
                m.need(dve, sent[b], turn * 16)
                dve.scalar_tensor_tensor(out=ready[b], in0=before[b], scalar=0.0, in1=B[2 + b][:, :],
                                         op0=ALU.max, op1=ALU.add).then_inc(out_ready, 1)
            over_steps(dve, emit)

        @block.sync
        def _(sp):
            def emit(t, b, turn):
                m.need(sp, out_ready, t + 1)
                sp.dma_start(out.rearrange("b i j c -> (b i) j c")[:, ds(t * COLS, COLS), :], by_col(ready[b])).then_inc(sent[b], 16)
            over_steps(sp, emit)
            for b in range(2):
                sp.wait_ge(sent[b], 16 * STEPS3 // 2)
            sp.dma_start(out.rearrange("b i j c -> (b i j) c")[0:L * L:L + 1, :], diag_out).then_inc(S("diag_sent"), 16)
            sp.wait_ge(S("diag_sent"), 16)


def build(nc, args, out):
    with ExitStack() as ctx:
        m = Memory(nc, ctx)
        load_and_prepare(nc, m, args)
        group_norm(nc, m, 0)
        layer0_norm(nc, m)
        layer0_attention(nc, m, args)
        layer1(nc, m, args)
        m.open_arena()
        group_norm(nc, m, 2)
        layer2(nc, m)
        layer3(nc, m, args, out)


_INS = ['x', 'L0_conv_gamma', 'L0_conv_beta', 'L0_conv_Wq', 'L0_conv_Wk', 'L0_conv_Wv', 'L0_conv_Wb', 'L0_conv_Wg',
        'L0_conv_bg', 'L0_conv_Wo', 'L0_conv_bo', 'L1_conv_qkv_w', 'L1_conv_qkv_b', 'L1_conv_wo_w', 'L1_conv_wo_b',
        'L1_conv_dw_w', 'L1_conv_dw_b', 'L2_conv_theta_w', 'L2_conv_alpha_raw', 'L3_conv_Ws', 'L3_conv_Wm', 'L3_conv_bm']


def kernel(**inputs):
    import concourse.bacc as bacc
    from concourse.bass_utils import run_bass_kernel_spmd

    nc = bacc.Bacc("TRN2", target_bir_lowering=False, num_devices=1)
    arrays, args = {}, {}
    for name in _INS:
        a = np.ascontiguousarray(inputs[name])
        arrays[f"in_{name}"] = a
        args[name] = nc.dram_tensor(f"in_{name}", a.shape, mybir.dt.from_np(a.dtype), kind="ExternalInput").ap()
    arrays["in_constants"] = constants()
    args["constants"] = nc.dram_tensor("in_constants", (128, NCONST), F32, kind="ExternalInput").ap()
    out = nc.dram_tensor("out", (1, L, L, C), F32, kind="ExternalOutput").ap()
    build(nc, args, out)
    result = run_bass_kernel_spmd(nc, [arrays], core_ids=[0])
    return result.results[0]["out"]
```
